# Optimizing a Trainium2 kernel written in Bass

```python
import numpy as np
import jax
import jax.numpy as jnp

def _softmax(x, axis=-1):
    return jax.nn.softmax(x, axis=axis)

def _gelu(x):
    return jax.nn.gelu(x, approximate=True)

def _silu(x):
    return jax.nn.silu(x)

def _sigmoid(x):
    return jax.nn.sigmoid(x)

def _layernorm(x, axis=-1, eps=1e-05):
    m = jnp.mean(x, axis=axis, keepdims=True)
    v = jnp.var(x, axis=axis, keepdims=True)
    return (x - m) / jnp.sqrt(v + eps)

def _scatter_add(tgt, idx, src, axis=0):
    return tgt.at[idx].add(src)

def _segment_sum(src, seg, n):
    return jax.ops.segment_sum(src, seg, n)
kernel_name = 'mk_early_fusion_embed_d1_tok_img768_r4_3b362c'

def setup_inputs(seed: int=0):
    np.random.seed(seed)
    _w = jnp.asarray

    def _rec_inputs():
        import jax
        import jax.numpy as jnp
        _rk = jax.random.key(seed)
        x = -0.00040386 + 0.999972 * jax.random.normal(jax.random.fold_in(_rk, 1), (8, 3, 128, 128), jnp.float32)
        x_txt = jax.random.randint(jax.random.fold_in(_rk, 51), (8, 128), 0, 30522, jnp.int32)
        itok_BS_0_4999 = jax.random.randint(jax.random.fold_in(_rk, 71), (8, 128), 0, 1250, jnp.int32)
        mask_BS_i0_1 = jnp.where(jnp.ones((8, 128), dtype=bool), 0, 1).astype(jnp.int32)
        pos_BS = jnp.broadcast_to(jnp.arange(128, dtype=jnp.int32), (8, 128))
        return (x, x_txt, itok_BS_0_4999, mask_BS_i0_1, pos_BS)
    x, x_txt, itok_BS_0_4999, mask_BS_i0_1, pos_BS = _rec_inputs()

    def _L0_tok_setup():
        import jax, jax.numpy as jnp
        import numpy as np
        P = 16
        WIN = 64
        NH = 12

        def _layernorm(x, g, b, eps=1e-05):
            m = x.mean(-1, keepdims=True)
            v = ((x - m) ** 2).mean(-1, keepdims=True)
            return (x - m) * jax.lax.rsqrt(v + eps) * g + b

        def _sinusoidal_pe(n, d):
            pos = jnp.arange(n, dtype=jnp.float32)[:, None]
            i = jnp.arange(d // 2, dtype=jnp.float32)[None, :]
            ang = pos / jnp.power(10000.0, 2.0 * i / d)
            pe = jnp.zeros((n, d), jnp.float32)
            pe = pe.at[:, 0::2].set(jnp.sin(ang)).at[:, 1::2].set(jnp.cos(ang))
            return pe
        key = jax.random.key(seed)
        ks = jax.random.split(key, 8)
        B, C, H, W, D, F = (16, 3, 128, 128, 192, 768)
        s = lambda k, shape: jax.random.normal(k, shape, jnp.float32) * 0.02
        return {'input': jax.random.normal(ks[0], (B, C, H, W), jnp.float32), 'patch_w': s(ks[1], (D, C, P, P)), 'patch_b': jnp.zeros((D,), jnp.float32), 'ln_g': jnp.ones((D,), jnp.float32), 'ln_b': jnp.zeros((D,), jnp.float32), 'qkv_w': s(ks[2], (D, 3 * D)), 'qkv_b': jnp.zeros((3 * D,), jnp.float32), 'proj_w': s(ks[3], (D, D)), 'proj_b': jnp.zeros((D,), jnp.float32), 'ff1_w': s(ks[4], (D, F)), 'ff1_b': jnp.zeros((F,), jnp.float32), 'ff2_w': s(ks[5], (F, D)), 'ff2_b': jnp.zeros((D,), jnp.float32)}
    _L0_tok_all = _L0_tok_setup()
    _L0_tok_in = {k: v for k, v in _L0_tok_all.items() if k in ('patch_w', 'patch_b', 'ln_g', 'ln_b', 'qkv_w', 'qkv_b', 'proj_w', 'proj_b', 'ff1_w', 'ff1_b', 'ff2_w', 'ff2_b')}
    del _L0_tok_all

    def _L0_txt_setup():
        import jax, jax.numpy as jnp
        import numpy as np
        VOCAB = 30522
        HIDDEN = 192
        MAX_POS = 128
        TYPE_VOCAB = 2
        DOMAIN_VOCAB = 1250
        DOMAIN_DIM = 128
        EPS = 1e-12
        B, S = (64, 128)
        key = jax.random.key(seed)
        ks = jax.random.split(key, 10)
        input_ids = jax.random.randint(ks[0], (B, S), 0, VOCAB)
        domain_ids = jax.random.randint(ks[1], (B, S), 0, DOMAIN_VOCAB)
        token_type_ids = jax.random.randint(ks[2], (B, S), 0, TYPE_VOCAB)
        position_ids = jnp.broadcast_to(jnp.arange(S, dtype=jnp.int64 if jax.config.jax_enable_x64 else jnp.int32), (B, S))
        word_table = jax.random.normal(ks[3], (VOCAB, HIDDEN), dtype=jnp.float32) * 0.02
        word_table = word_table.at[0].set(0.0)
        domain_table = jax.random.normal(ks[4], (DOMAIN_VOCAB, DOMAIN_DIM), dtype=jnp.float32) * 0.02
        pos_table = jax.random.normal(ks[5], (MAX_POS, HIDDEN), dtype=jnp.float32) * 0.02
        type_table = jax.random.normal(ks[6], (TYPE_VOCAB, HIDDEN), dtype=jnp.float32) * 0.02
        proj_w = jax.random.normal(ks[7], (HIDDEN, DOMAIN_DIM), dtype=jnp.float32) * (1.0 / np.sqrt(DOMAIN_DIM))
        proj_b = jnp.zeros((HIDDEN,), dtype=jnp.float32)
        ln_gamma = jnp.ones((HIDDEN,), dtype=jnp.float32)
        ln_beta = jnp.zeros((HIDDEN,), dtype=jnp.float32)
        return {'input_ids': input_ids, 'domain_ids': domain_ids, 'token_type_ids': token_type_ids, 'position_ids': position_ids, 'word_table': word_table, 'domain_table': domain_table, 'pos_table': pos_table, 'type_table': type_table, 'proj_w': proj_w, 'proj_b': proj_b, 'ln_gamma': ln_gamma, 'ln_beta': ln_beta}
    _L0_txt_all = _L0_txt_setup()
    _L0_txt_in = {k: v for k, v in _L0_txt_all.items() if k in ('word_table', 'domain_table', 'pos_table', 'type_table', 'proj_w', 'proj_b', 'ln_gamma', 'ln_beta')}
    del _L0_txt_all

    def _L0_attn_setup():
        import jax, jax.numpy as jnp
        import numpy as np
        NUM_HEADS = 12
        WINDOW = 64
        LN_EPS = 1e-05

        def _ln(x, g, b):
            m = x.mean(-1, keepdims=True)
            v = x.var(-1, keepdims=True)
            return (x - m) / jnp.sqrt(v + LN_EPS) * g + b
        key = jax.random.key(seed)
        ks = jax.random.split(key, 10)
        B, L, D = (1, 512, 192)
        s = 0.02

        def w(k, shape):
            return jax.random.normal(k, shape, jnp.float32) * s
        return {'x': jax.random.normal(ks[0], (B, L, D), jnp.float32), 'ln1_g': jnp.ones((D,), jnp.float32), 'ln1_b': jnp.zeros((D,), jnp.float32), 'attn_qkv_w': w(ks[1], (D, 3 * D)), 'attn_qkv_b': jnp.zeros((3 * D,), jnp.float32), 'attn_proj_w': w(ks[2], (D, D)), 'attn_proj_b': jnp.zeros((D,), jnp.float32), 'ssm_qkv_w': w(ks[3], (D, 3 * D)), 'ssm_qkv_b': jnp.zeros((3 * D,), jnp.float32), 'ssm_out_w': w(ks[4], (D, D)), 'ssm_out_b': jnp.zeros((D,), jnp.float32), 'ssm_ln_g': jnp.ones((D,), jnp.float32), 'ssm_ln_b': jnp.zeros((D,), jnp.float32), 'out_w': w(ks[5], (D, D)), 'out_b': jnp.zeros((D,), jnp.float32), 'mlp_w1': w(ks[6], (D, 4 * D)), 'mlp_b1': jnp.zeros((4 * D,), jnp.float32), 'mlp_w2': w(ks[7], (4 * D, D)), 'mlp_b2': jnp.zeros((D,), jnp.float32), 'lnm_g': jnp.ones((D,), jnp.float32), 'lnm_b': jnp.zeros((D,), jnp.float32)}
    _L0_attn_all = _L0_attn_setup()
    _L0_attn_in = {k: v for k, v in _L0_attn_all.items() if k in ('ln1_g', 'ln1_b', 'attn_qkv_w', 'attn_qkv_b', 'attn_proj_w', 'attn_proj_b', 'ssm_qkv_w', 'ssm_qkv_b', 'ssm_out_w', 'ssm_out_b', 'ssm_ln_g', 'ssm_ln_b', 'out_w', 'out_b', 'mlp_w1', 'mlp_b1', 'mlp_w2', 'mlp_b2', 'lnm_g', 'lnm_b')}
    del _L0_attn_all

    def _L0_ffn_setup():
        import jax, jax.numpy as jnp
        import numpy as np
        H, I, E, S, K = (192, 768, 16, 2, 2)
        SCALE = 1.0
        key = jax.random.key(seed)
        ks = jax.random.split(key, 8)
        sd = 0.02
        return {'hidden_states': jax.random.normal(ks[0], (2, 256, H), jnp.float32), 'gate_w': jax.random.normal(ks[1], (E, H), jnp.float32) * sd, 'shared_wg': jax.random.normal(ks[2], (S, H, I), jnp.float32) * sd, 'shared_wu': jax.random.normal(ks[3], (S, H, I), jnp.float32) * sd, 'shared_wd': jax.random.normal(ks[4], (S, I, H), jnp.float32) * sd, 'wg': jax.random.normal(ks[5], (E, H, I), jnp.float32) * sd, 'wu': jax.random.normal(ks[6], (E, H, I), jnp.float32) * sd, 'wd': jax.random.normal(ks[7], (E, I, H), jnp.float32) * sd}
    _L0_ffn_all = _L0_ffn_setup()
    _L0_ffn_in = {k: v for k, v in _L0_ffn_all.items() if k in ('gate_w', 'shared_wg', 'shared_wu', 'shared_wd', 'wg', 'wu', 'wd')}
    del _L0_ffn_all
    return {'x': x, 'x_txt': x_txt, 'itok_BS_0_4999': itok_BS_0_4999, 'mask_BS_i0_1': mask_BS_i0_1, 'pos_BS': pos_BS, 'L0_tok_patch_w': _L0_tok_in['patch_w'], 'L0_tok_patch_b': _L0_tok_in['patch_b'], 'L0_tok_ln_g': _L0_tok_in['ln_g'], 'L0_tok_ln_b': _L0_tok_in['ln_b'], 'L0_tok_qkv_w': _L0_tok_in['qkv_w'], 'L0_tok_qkv_b': _L0_tok_in['qkv_b'], 'L0_tok_proj_w': _L0_tok_in['proj_w'], 'L0_tok_proj_b': _L0_tok_in['proj_b'], 'L0_tok_ff1_w': _L0_tok_in['ff1_w'], 'L0_tok_ff1_b': _L0_tok_in['ff1_b'], 'L0_tok_ff2_w': _L0_tok_in['ff2_w'], 'L0_tok_ff2_b': _L0_tok_in['ff2_b'], 'L0_txt_word_table': _L0_txt_in['word_table'], 'L0_txt_domain_table': _L0_txt_in['domain_table'], 'L0_txt_pos_table': _L0_txt_in['pos_table'], 'L0_txt_type_table': _L0_txt_in['type_table'], 'L0_txt_proj_w': _L0_txt_in['proj_w'], 'L0_txt_proj_b': _L0_txt_in['proj_b'], 'L0_txt_ln_gamma': _L0_txt_in['ln_gamma'], 'L0_txt_ln_beta': _L0_txt_in['ln_beta'], 'L0_attn_ln1_g': _L0_attn_in['ln1_g'], 'L0_attn_ln1_b': _L0_attn_in['ln1_b'], 'L0_attn_attn_qkv_w': _L0_attn_in['attn_qkv_w'], 'L0_attn_attn_qkv_b': _L0_attn_in['attn_qkv_b'], 'L0_attn_attn_proj_w': _L0_attn_in['attn_proj_w'], 'L0_attn_attn_proj_b': _L0_attn_in['attn_proj_b'], 'L0_attn_ssm_qkv_w': _L0_attn_in['ssm_qkv_w'], 'L0_attn_ssm_qkv_b': _L0_attn_in['ssm_qkv_b'], 'L0_attn_ssm_out_w': _L0_attn_in['ssm_out_w'], 'L0_attn_ssm_out_b': _L0_attn_in['ssm_out_b'], 'L0_attn_ssm_ln_g': _L0_attn_in['ssm_ln_g'], 'L0_attn_ssm_ln_b': _L0_attn_in['ssm_ln_b'], 'L0_attn_out_w': _L0_attn_in['out_w'], 'L0_attn_out_b': _L0_attn_in['out_b'], 'L0_attn_mlp_w1': _L0_attn_in['mlp_w1'], 'L0_attn_mlp_b1': _L0_attn_in['mlp_b1'], 'L0_attn_mlp_w2': _L0_attn_in['mlp_w2'], 'L0_attn_mlp_b2': _L0_attn_in['mlp_b2'], 'L0_attn_lnm_g': _L0_attn_in['lnm_g'], 'L0_attn_lnm_b': _L0_attn_in['lnm_b'], 'L0_ffn_gate_w': _L0_ffn_in['gate_w'], 'L0_ffn_shared_wg': _L0_ffn_in['shared_wg'], 'L0_ffn_shared_wu': _L0_ffn_in['shared_wu'], 'L0_ffn_shared_wd': _L0_ffn_in['shared_wd'], 'L0_ffn_wg': _L0_ffn_in['wg'], 'L0_ffn_wu': _L0_ffn_in['wu'], 'L0_ffn_wd': _L0_ffn_in['wd']}

def reference(x, x_txt, itok_BS_0_4999, mask_BS_i0_1, pos_BS, L0_tok_patch_w, L0_tok_patch_b, L0_tok_ln_g, L0_tok_ln_b, L0_tok_qkv_w, L0_tok_qkv_b, L0_tok_proj_w, L0_tok_proj_b, L0_tok_ff1_w, L0_tok_ff1_b, L0_tok_ff2_w, L0_tok_ff2_b, L0_txt_word_table, L0_txt_domain_table, L0_txt_pos_table, L0_txt_type_table, L0_txt_proj_w, L0_txt_proj_b, L0_txt_ln_gamma, L0_txt_ln_beta, L0_attn_ln1_g, L0_attn_ln1_b, L0_attn_attn_qkv_w, L0_attn_attn_qkv_b, L0_attn_attn_proj_w, L0_attn_attn_proj_b, L0_attn_ssm_qkv_w, L0_attn_ssm_qkv_b, L0_attn_ssm_out_w, L0_attn_ssm_out_b, L0_attn_ssm_ln_g, L0_attn_ssm_ln_b, L0_attn_out_w, L0_attn_out_b, L0_attn_mlp_w1, L0_attn_mlp_b1, L0_attn_mlp_w2, L0_attn_mlp_b2, L0_attn_lnm_g, L0_attn_lnm_b, L0_ffn_gate_w, L0_ffn_shared_wg, L0_ffn_shared_wu, L0_ffn_shared_wd, L0_ffn_wg, L0_ffn_wu, L0_ffn_wd):
    import jax
    import jax.numpy as jnp

    def _L0_tok_ref(input, patch_w, patch_b, ln_g, ln_b, qkv_w, qkv_b, proj_w, proj_b, ff1_w, ff1_b, ff2_w, ff2_b):
        import jax, jax.numpy as jnp
        import numpy as np
        P = 16
        WIN = 64
        NH = 12

        def _layernorm(x, g, b, eps=1e-05):
            m = x.mean(-1, keepdims=True)
            v = ((x - m) ** 2).mean(-1, keepdims=True)
            return (x - m) * jax.lax.rsqrt(v + eps) * g + b

        def _sinusoidal_pe(n, d):
            pos = jnp.arange(n, dtype=jnp.float32)[:, None]
            i = jnp.arange(d // 2, dtype=jnp.float32)[None, :]
            ang = pos / jnp.power(10000.0, 2.0 * i / d)
            pe = jnp.zeros((n, d), jnp.float32)
            pe = pe.at[:, 0::2].set(jnp.sin(ang)).at[:, 1::2].set(jnp.cos(ang))
            return pe
        B, C, H, W = input.shape
        D = patch_w.shape[0]
        dh = D // NH
        xp = input.reshape(B, C, H // P, P, W // P, P)
        x = jnp.einsum('bchpwq,dcpq->bhwd', xp, patch_w) + patch_b
        x = x.reshape(B, -1, D)
        x = _layernorm(x, ln_g, ln_b)
        N = x.shape[1]
        x = x + _sinusoidal_pe(N, D)

        def ff(y):
            return jax.nn.gelu(y @ ff1_w + ff1_b) @ ff2_w + ff2_b

        def sparse_attn(y):
            nW = N // WIN
            qkv = (y @ qkv_w + qkv_b).reshape(B, nW, WIN, 3, NH, dh)
            q, k, v = (qkv[:, :, :, 0], qkv[:, :, :, 1], qkv[:, :, :, 2])
            scores = jnp.einsum('bwqhd,bwkhd->bwhqk', q, k) * dh ** (-0.5)
            a = jax.nn.softmax(scores, axis=-1)
            o = jnp.einsum('bwhqk,bwkhd->bwqhd', a, v).reshape(B, N, D)
            return o @ proj_w + proj_b
        identity = x
        x = ff(x)
        x = sparse_attn(x)
        x = x + identity
        identity = x
        x = ff(x)
        x = x + identity
        return x

    def _L0_txt_ref(input_ids, domain_ids, token_type_ids, position_ids, word_table, domain_table, pos_table, type_table, proj_w, proj_b, ln_gamma, ln_beta):
        import jax, jax.numpy as jnp
        import numpy as np
        VOCAB = 30522
        HIDDEN = 192
        MAX_POS = 128
        TYPE_VOCAB = 2
        DOMAIN_VOCAB = 1250
        DOMAIN_DIM = 128
        EPS = 1e-12
        B, S = (64, 128)
        words = word_table[input_ids]
        domain = domain_table[domain_ids]
        types = type_table[token_type_ids]
        pos = pos_table[position_ids]
        domain_proj = jnp.einsum('bsd,hd->bsh', domain, proj_w) + proj_b
        emb = words + domain_proj + types + pos
        mean = jnp.mean(emb, axis=-1, keepdims=True)
        var = jnp.mean(jnp.square(emb - mean), axis=-1, keepdims=True)
        out = (emb - mean) / jnp.sqrt(var + EPS) * ln_gamma + ln_beta
        return out

    def _L0_attn_ref(x, ln1_g, ln1_b, attn_qkv_w, attn_qkv_b, attn_proj_w, attn_proj_b, ssm_qkv_w, ssm_qkv_b, ssm_out_w, ssm_out_b, ssm_ln_g, ssm_ln_b, out_w, out_b, mlp_w1, mlp_b1, mlp_w2, mlp_b2, lnm_g, lnm_b):
        import jax, jax.numpy as jnp
        import numpy as np
        NUM_HEADS = 12
        WINDOW = 64
        LN_EPS = 1e-05

        def _ln(x, g, b):
            m = x.mean(-1, keepdims=True)
            v = x.var(-1, keepdims=True)
            return (x - m) / jnp.sqrt(v + LN_EPS) * g + b
        B, L, D = x.shape
        H = NUM_HEADS
        E = D // H
        xn = _ln(x, ln1_g, ln1_b)
        qkv = (xn @ attn_qkv_w + attn_qkv_b).reshape(B, L, 3, H, E)
        q = jnp.transpose(qkv[:, :, 0], (0, 2, 1, 3))
        k = jnp.transpose(qkv[:, :, 1], (0, 2, 1, 3))
        v = jnp.transpose(qkv[:, :, 2], (0, 2, 1, 3))
        scale = 1.0 / jnp.sqrt(jnp.float32(E))
        scores = jnp.einsum('bhqe,bhke->bhqk', q, k) * scale
        i = jnp.arange(L)[:, None]
        j = jnp.arange(L)[None, :]
        mask = (j > i) | (j <= i - WINDOW)
        scores = jnp.where(mask, jnp.float32(-10000.0), scores)
        attn = jax.nn.softmax(scores, axis=-1)
        ao = jnp.einsum('bhqk,bhke->bhqe', attn, v)
        ao = jnp.transpose(ao, (0, 2, 1, 3)).reshape(B, L, D)
        ao = ao @ attn_proj_w + attn_proj_b
        qkv2 = xn @ ssm_qkv_w + ssm_qkv_b
        q2, k2, v2 = jnp.split(qkv2, 3, axis=-1)
        q2 = q2.reshape(B, L, H, E)
        k2 = k2.reshape(B, L, H, E)
        v2 = v2.reshape(B, L, H, E)
        q2 = jax.nn.elu(q2) + (1.0 + 0.0001)
        k2 = jax.nn.elu(k2) + (1.0 + 0.0001)
        q2 = q2 * scale
        kv = jnp.einsum('blhe,blhf->blhef', k2, v2)
        kv_cumsum = jnp.cumsum(kv, axis=1)
        k_cumsum = jnp.cumsum(k2, axis=1)
        num = jnp.einsum('blhe,blhef->blhf', q2, kv_cumsum)
        den = jnp.einsum('blhe,blhe->blh', q2, k_cumsum)[..., None] + 0.0001
        so = (num / den).reshape(B, L, D)
        so = so @ ssm_out_w + ssm_out_b
        so = _ln(so, ssm_ln_g, ssm_ln_b)
        x2 = x + (ao + so) @ out_w + out_b
        h = _ln(x2, lnm_g, lnm_b)
        h = jax.nn.gelu(h @ mlp_w1 + mlp_b1, approximate=False)
        return x2 + (h @ mlp_w2 + mlp_b2)

    def _L0_ffn_ref(hidden_states, gate_w, shared_wg, shared_wu, shared_wd, wg, wu, wd):
        import jax, jax.numpy as jnp
        import numpy as np
        H, I, E, S, K = (192, 768, 16, 2, 2)
        SCALE = 1.0
        B, T, _ = hidden_states.shape
        x = hidden_states.reshape(-1, H)
        N = x.shape[0]
        g = jnp.einsum('nh,shi->sni', x, shared_wg)
        u = jnp.einsum('nh,shi->sni', x, shared_wu)
        shared_out = jnp.einsum('sni,sih->snh', jax.nn.silu(g) * u, shared_wd).mean(axis=0)
        router_logits = x @ gate_w.T
        routing_weights = jax.nn.softmax(router_logits, axis=-1)
        topk_w, topk_idx = jax.lax.top_k(routing_weights, K)
        topk_w = topk_w / (topk_w.sum(axis=-1, keepdims=True) + 1e-08)
        topk_w = topk_w * SCALE
        combine = jnp.zeros((N, E), x.dtype).at[jnp.arange(N)[:, None], topk_idx].add(topk_w)
        ge = jnp.einsum('nh,ehi->eni', x, wg)
        ue = jnp.einsum('nh,ehi->eni', x, wu)
        ye = jnp.einsum('eni,eih->enh', jax.nn.silu(ge) * ue, wd)
        routed_out = jnp.einsum('ne,enh->nh', combine, ye)
        return (shared_out + routed_out).reshape(B, T, H)
    h = _L0_tok_ref(x, L0_tok_patch_w, L0_tok_patch_b, L0_tok_ln_g, L0_tok_ln_b, L0_tok_qkv_w, L0_tok_qkv_b, L0_tok_proj_w, L0_tok_proj_b, L0_tok_ff1_w, L0_tok_ff1_b, L0_tok_ff2_w, L0_tok_ff2_b)
    h = jnp.concatenate([h, _L0_txt_ref(x_txt, itok_BS_0_4999, mask_BS_i0_1, pos_BS, L0_txt_word_table, L0_txt_domain_table, L0_txt_pos_table, L0_txt_type_table, L0_txt_proj_w, L0_txt_proj_b, L0_txt_ln_gamma, L0_txt_ln_beta)], axis=1)
    h = h + _L0_attn_ref(_layernorm(h, axis=-1), L0_attn_ln1_g, L0_attn_ln1_b, L0_attn_attn_qkv_w, L0_attn_attn_qkv_b, L0_attn_attn_proj_w, L0_attn_attn_proj_b, L0_attn_ssm_qkv_w, L0_attn_ssm_qkv_b, L0_attn_ssm_out_w, L0_attn_ssm_out_b, L0_attn_ssm_ln_g, L0_attn_ssm_ln_b, L0_attn_out_w, L0_attn_out_b, L0_attn_mlp_w1, L0_attn_mlp_b1, L0_attn_mlp_w2, L0_attn_mlp_b2, L0_attn_lnm_g, L0_attn_lnm_b)
    h = h + _L0_ffn_ref(_layernorm(h, axis=-1), L0_ffn_gate_w, L0_ffn_shared_wg, L0_ffn_shared_wu, L0_ffn_shared_wd, L0_ffn_wg, L0_ffn_wu, L0_ffn_wd)
    return h

_drawn_inputs = setup_inputs


def setup_inputs(seed=0):
    import zlib

    import numpy as np

    out = dict(_drawn_inputs(seed))
    spreads = {'L0_tok_patch_b': (0.0, 0.1),
     'L0_tok_ln_g': (1.0, 0.2),
     'L0_tok_ln_b': (0.0, 0.1),
     'L0_tok_qkv_b': (0.0, 0.645),
     'L0_tok_proj_b': (0.0, 0.1),
     'L0_tok_ff1_b': (0.0, 0.53),
     'L0_tok_ff2_b': (0.0, 0.1),
     'L0_txt_proj_b': (0.0, 0.1),
     'L0_txt_ln_gamma': (1.0, 0.2),
     'L0_txt_ln_beta': (0.0, 0.1),
     'L0_attn_ln1_g': (1.0, 0.6),
     'L0_attn_ln1_b': (0.0, 0.8),
     'L0_attn_attn_qkv_b': (0.0, 0.8),
     'L0_attn_attn_proj_b': (0.0, 0.563),
     'L0_attn_ssm_qkv_b': (0.0, 0.1),
     'L0_attn_ssm_out_b': (0.0, 0.1),
     'L0_attn_ssm_ln_g': (1.0, 0.585),
     'L0_attn_ssm_ln_b': (0.0, 0.603),
     'L0_attn_out_b': (0.0, 0.1),
     'L0_attn_mlp_b1': (0.0, 0.598),
     'L0_attn_mlp_b2': (0.0, 0.1),
     'L0_attn_lnm_g': (1.0, 0.6),
     'L0_attn_lnm_b': (0.0, 0.8)}
    factors = {'L0_tok_qkv_w': 8.0,
     'L0_tok_proj_w': 4.145,
     'L0_attn_attn_qkv_w': 8.0,
     'L0_attn_attn_proj_w': 8.0,
     'L0_ffn_gate_w': 8.0,
     'L0_ffn_shared_wg': 7.907,
     'L0_ffn_shared_wu': 7.742,
     'L0_ffn_shared_wd': 7.785,
     'L0_ffn_wg': 7.845,
     'L0_ffn_wu': 8.0,
     'L0_ffn_wd': 7.746}
    for name, (base, spread) in spreads.items():
        noise = np.random.default_rng([zlib.crc32(name.encode()), seed]).standard_normal(out[name].shape)
        drawn = base * np.exp(spread * noise) if base else spread * noise
        out[name] = jnp.asarray(drawn.astype(out[name].dtype))
    for name, factor in factors.items():
        out[name] = (out[name] * factor).astype(out[name].dtype)
    return out
```

```python
import numpy as np
import concourse.bass as bass
from concourse import mybir
from contextlib import ExitStack

F32 = mybir.dt.float32
I32 = mybir.dt.int32
U32 = mybir.dt.uint32
ALU = mybir.AluOpType
ACT = mybir.ActivationFunctionType
AX = mybir.AxisListType

B = 8
IMG = 64
TXT = 128
L = IMG + TXT
D = 192
KC = 2
DC = D // KC
FF = 768
FM = FF // 128
NH, DH = 12, 16
HG = NH // 4
NI = B * IMG
IT = NI // 128
PAIRS = B // 2
PT = 2 * L
TP = PT // 128
NT = PAIRS * TP
NTOK = B * L
QC = L // 2
E_R, E_S = 16, 2
NE = E_R + E_S
NEG = -10000.0
WINDOW = 64
HA = DH + 1

COLS = {}
_c = 0
for _name, _n in [("tok_ln_g", KC), ("tok_ln_b", KC), ("tok_ff1_b", FM), ("tok_ff2_b", KC), ("tok_q_b", HG),
                  ("tok_k_b", HG), ("tok_proj_b", KC), ("ln1_g", KC), ("ln1_b", KC), ("q_b", HG), ("k_b", HG),
                  ("q2_b", HG), ("k2_b", HG), ("attn_proj_b", KC), ("ssm_ln_g", KC), ("ssm_ln_b", KC),
                  ("lnm_g", KC), ("lnm_b", KC), ("mlp_b1", FM)]:
    COLS[_name] = _c
    _c += _n
NCOL = _c
ROWS = {}
_c = 0
for _name, _n in [("patch_b", D), ("tok_v_b", D), ("tok_ff2_b", D), ("txt_proj_b", D), ("v_b", 2 * D),
                  ("ssm_out_b", D), ("out_b", D), ("mlp_b2", D)]:
    ROWS[_name] = _c
    _c += _n
NROW = _c


def build(nc, a, out):
    ctx = ExitStack()
    with ctx:
        def sb(name, shape, dt=F32):
            return ctx.enter_context(nc.sbuf_tensor(name, shape, dt))

        def sem(name):
            return ctx.enter_context(nc.semaphore(name))

        ident = sb("ident", [128, 128])
        ones = sb("ones", [1, 512])
        cols = sb("cols", [128, NCOL])
        rows = sb("rows", [1, NROW])
        pe_tab = sb("pe_tab", [DC, KC, IMG])
        keep = sb("keep", [QC, 2, L], I32)
        causal = sb("causal", [QC, L + QC])
        rank = sb("rank", [128, TP, E_R])
        gam_txt = sb("gam_txt", [128, D])
        bet_txt = sb("bet_txt", [128, D])
        w_patch = sb("w_patch", [128, FM, D])
        w_tff1 = sb("w_tff1", [DC, KC, FF])
        w_tff2 = sb("w_tff2", [128, FM, D])
        w_tq = sb("w_tq", [DC, KC, HG * 128])
        w_tk = sb("w_tk", [DC, KC, HG * 128])
        w_tv = sb("w_tv", [DC, KC, D])
        w_tproj = sb("w_tproj", [DC, KC, D])
        w_txt = sb("w_txt", [128, D])
        w_qk = sb("w_qk", [DC, 4, KC, HG * 128])
        w_v = sb("w_v", [DC, KC, 2 * D])
        w_aproj = sb("w_aproj", [DC, KC, D])
        w_sout = sb("w_sout", [DC, KC, D])
        w_out = sb("w_out", [DC, KC, D])
        w_m1 = sb("w_m1", [DC, KC, FF])
        w_m2 = sb("w_m2", [128, FM, D])
        w_gate = sb("w_gate", [DC, KC, E_R])
        minus_half = sb("minus_half", [128, 4])
        phi_b = sb("phi_b", [128, 2 * HG])
        carrier = sb("carrier", [128, 1])
        carrier_p = sb("carrier_p", [128, 1])

        h_sb = sb("h_sb", [128, IT + B, D])
        acc = sb("acc", [128, NT, D])
        x3T = sb("x3T", [DC, KC, NTOK])
        comb = sb("comb", [128, NT, NE])
        st = sb("st", [128, 6])
        mv = sb("mv", [128, 4, 2])
        ve = sb("ve", [128, 4])
        rs = sb("rs", [128, 4])

        PS = ctx.enter_context(nc.psum_tensor("PS", [128, 8, 512], F32))

        ld_const = sem("ld_const")
        ld_patch = sem("ld_patch")
        ld_tok = sem("ld_tok")
        ld_txt = sem("ld_txt")
        ld_attn = sem("ld_attn")
        ld_idx = sem("ld_idx")
        gathered = [sem(f"gathered{b}") for b in range(B)]
        set_up = sem("set_up")
        vs = sem("dve_step")
        stored = sem("stored")
        names = """patch_mm a_ve a_rs a_z a_zT a_xg a_x a_ff1 a_h a_ff2 a_y a_mm a_q a_k a_vmm a_v a_s a_sub a_exp
            a_pT a_ptc a_o a_on a_oT a_at a_pj a_x1 a_hmm h_img
            t_tp t_dT t_dc t_pm t_ve t_rs t_z t_g h_txt
            b_hp b_ve1 b_rs1 b_x b_ve2 b_rs2 b_z b_zT b_xn b_mm b_q b_k b_r b_e b_clip b_phi b_vmm b_v b_s b_att
            b_cp b_nm b_ex b_pT b_ptc b_lin b_o b_on b_oT b_ao b_so
            c_so c_ve1 c_rs1 c_z1 c_z1T c_sl c_pj c_u c_mm c_x2 c_ve2 c_rs2 c_z2 c_z2T c_m c_ff1 c_h c_ff2 c_hx c_h2
            c_ve3 c_rs3 c_x3 c_x3T c_x3s c_lg c_ls c_ex c_cw pair_done
            w_ld0 w_ld1 e_up e_sg e_gu e_dn e_acc""".split()
        S = {n: sem(n) for n in names}

        scr = ExitStack()

        def tb(name, shape, dt=F32):
            return scr.enter_context(nc.sbuf_tensor(name, shape, dt))

        patches = tb("patches", [128, FM, NI])
        zA = tb("zA", [128, IT, D])
        xT = tb("xT", [DC, KC, NI])
        h1T = tb("h1T", [128, FM, NI])
        y1T = tb("y1T", [DC, KC, NI])
        tq = tb("tq", [128, HG, NI])
        tk = tb("tk", [128, HG, NI])
        tv = tb("tv", [IMG, B, NH, HA])
        pA = tb("pA", [128, 2, NH, IMG])
        mxA = tb("mxA", [128, NH])
        ptA = tb("ptA", [IMG, NH, 128])
        rcA = tb("rcA", [128, NH])
        oA = tb("oA", [128, IT, NH, DH])
        aTA = tb("aTA", [DC, KC, NI])
        ids = tb("ids", [128, 4, B], I32)
        words = tb("words", [128, B, D])
        types = tb("types", [128, B, D])
        poss = tb("poss", [128, B, D])
        dom = tb("dom", [128, B, 128])
        domT = tb("domT", [128, 2, 128])
        zT_ = tb("z_txt", [128, 2, D])
        mvT = tb("mvT", [128, B, 2])
        veT = tb("veT", [128, B])
        rsT = tb("rsT", [128, B])
        stT = tb("stT", [128, 6])
        scr.close()
        scr2 = ExitStack()

        def tb2(name, shape, dt=F32):
            return scr2.enter_context(nc.sbuf_tensor(name, shape, dt))

        hp = tb2("hp", [128, TP, D])
        xl = tb2("xl", [128, TP, D])
        z = tb2("z", [128, TP, D])
        xnT = tb2("xnT", [DC, KC, PT])
        qk = tb2("qk", [128, 4, HG, PT])
        ee = tb2("ee", [128, 2, PT])
        va = tb2("va", [QC, 4, 2, NH, HA])
        sm = tb2("sm", [QC, 2, 2, L])
        nm = tb2("nm", [QC, 2, 2])
        pb = tb2("pb", [QC, 2, 2, L])
        pts = tb2("pts", [QC, 2, 2 * L])
        lin = tb2("lin", [QC, 2, L + QC])
        dn = tb2("dn", [QC, 2, 2 * NH])
        oN = tb2("oN", [QC, 2, 2 * NH, DH])
        aoT = tb2("aoT", [DC, KC, PT])
        soT = tb2("soT", [DC, KC, PT])
        slT = tb2("slT", [DC, KC, PT])
        uT = tb2("uT", [DC, KC, PT])
        x2 = tb2("x2", [128, TP, D])
        hx = tb2("hx", [128, TP, D])
        h2 = tb2("h2", [128, TP, D])
        mT = tb2("mT", [DC, KC, PT])
        hT = tb2("hT", [128, FM, PT])
        x3s = tb2("x3s", [DC, KC, PT])
        lg = tb2("lg", [128, TP, E_R])
        r1 = tb2("r1", [128, 6, TP])
        sel = tb2("sel", [128, 3, TP, E_R])
        cw = tb2("cw", [128, TP, NE])
        scr2.close()
        scr3 = ExitStack()

        def tb3(name, shape, dt=F32):
            return scr3.enter_context(nc.sbuf_tensor(name, shape, dt))

        wgu = tb3("wgu", [DC, 2, 2, KC, FF])
        wdn = tb3("wdn", [128, 2, FM, D])
        sg = tb3("sg", [128, 2, 512])
        gu = tb3("gu", [128, 2, FM, 512])
        scr3.close()

        def col(name, i=0, n=128):
            return cols[0:n, COLS[name] + i:COLS[name] + i + 1]

        def row(name, n=D):
            return rows[0:1, ROWS[name]:ROWS[name] + n]

        block = ctx.enter_context(nc.Block())

        @block.sync
        def _(sp):
            for dst, name in ((w_patch, "w_patch"), (patches, "patches")):
                sp.dma_start(dst[:, :, :], a[name]).then_inc(ld_patch, 16)
            for dst, name in ((ident, "ident"), (cols, "cols"), (rows, "rows")):
                sp.dma_start(dst[:, :], a[name]).then_inc(ld_const, 16)
            for dst, name in ((pe_tab, "pe_tab"), (w_tff1, "w_tff1"), (w_tff2, "w_tff2"), (w_tq, "w_tq"),
                              (w_tk, "w_tk"), (w_tv, "w_tv"), (w_tproj, "w_tproj")):
                sp.dma_start(dst[:, :, :], a[name]).then_inc(ld_tok, 16)
            for dst, name in ((w_txt, "w_txt"), (gam_txt, "gam_txt"), (bet_txt, "bet_txt")):
                sp.dma_start(dst[:, :], a[name]).then_inc(ld_txt, 16)
            sp.dma_start(w_qk[:, :, :, :], a["w_qk"]).then_inc(ld_attn, 16)
            for dst, name in ((keep, "keep"), (rank, "rank"), (w_v, "w_v"), (w_aproj, "w_aproj"), (w_sout, "w_sout"),
                              (w_out, "w_out"), (w_m1, "w_m1"), (w_m2, "w_m2"), (w_gate, "w_gate")):
                sp.dma_start(dst[:, :, :], a[name]).then_inc(ld_attn, 16)
            sp.dma_start(causal[:, :], a["causal"]).then_inc(ld_attn, 16)

            sp.wait_ge(S["pair_done"], PAIRS + 1)
            for buf in range(2):
                ld = S[f"w_ld{buf}"]
                sp.dma_start(wgu[:, buf, 0, :, :], a["wg"][buf]).then_inc(ld, 16)
                sp.dma_start(wgu[:, buf, 1, :, :], a["wu"][buf]).then_inc(ld, 16)
                sp.dma_start(wdn[:, buf, :, :], a["wd"][buf]).then_inc(ld, 16)
            with sp.Fori(0, NE // 2 - 1) as r:
                for buf in range(2):
                    e = r * 2 + (2 + buf)
                    ld = S[f"w_ld{buf}"]
                    sp.wait_ge(S["e_dn"], r * 24 + (8 + 12 * (buf + 1)))
                    sp.dma_start(wgu[:, buf, 0, :, :], a["wg"][bass.ds(e, 1)].rearrange("o p c n -> p (o c) n")).then_inc(ld, 16)
                    sp.dma_start(wgu[:, buf, 1, :, :], a["wu"][bass.ds(e, 1)].rearrange("o p c n -> p (o c) n")).then_inc(ld, 16)
                    sp.dma_start(wdn[:, buf, :, :], a["wd"][bass.ds(e, 1)].rearrange("o p c n -> p (o c) n")).then_inc(ld, 16)

            sp.wait_ge(S["e_acc"], NE * NT + 4)
            for p in range(PAIRS):
                for k in range(2):
                    sp.dma_start(out[2 * p + k, 0:IMG, :], acc[IMG * k:IMG * k + IMG, TP * p, :]).then_inc(stored, 16)
                    sp.dma_start(out[2 * p + k, IMG:L, :], acc[:, TP * p + 1 + k, :]).then_inc(stored, 16)
            sp.wait_ge(stored, 16 * 2 * B)

        @block.gpsimd
        def _(pool):
            pool.memset(ones[:, :], 1.0).then_inc(set_up, 1)
            pool.memset(minus_half[:, :], -0.5).then_inc(set_up, 1)
            pool.wait_ge(set_up, 2)
            pool.memset(tv[:, :, :, DH:HA], 1.0).then_inc(set_up, 1)
            pool.sem_inc(S["pair_done"], 1)

            pool.dma_start(ids[:, :, :], a["ids"]).then_inc(ld_idx, 16)
            pool.wait_ge(ld_idx, 16)
            for b in range(B):
                for j, (dst, table) in enumerate(((words, "word_table"), (types, "type_table"), (poss, "pos_table"),
                                                  (dom, "domain_table"))):
                    pool.indirect_dma_start(dst[:, b, :], None, a[table],
                                            bass.IndirectOffsetOnAxis(ap=ids[:, j, b:b + 1].bitcast(U32), axis=0)
                                            ).then_inc(gathered[b], 16)
            for i in range(IT):
                pool.wait_ge(S["a_ve"], i + 1)
                pool.tensor_tensor(rs[:, i:i + 1], ve[:, i:i + 1], minus_half[:, 0:1], ALU.pow).then_inc(S["a_rs"], 1)
            for b in range(B):
                pool.wait_ge(gathered[b], 64)
                pool.tensor_tensor(types[:, b, :], types[:, b, :], poss[:, b, :], ALU.add).then_inc(S["t_tp"], 1)
            pool.wait_ge(ld_txt, 48)
            for b in range(B):
                pool.wait_ge(S["t_ve"], b + 1)
                pool.tensor_tensor(rsT[:, b:b + 1], veT[:, b:b + 1], minus_half[:, 0:1], ALU.pow).then_inc(S["t_rs"], 1)
                pool.wait_ge(S["t_z"], b + 1)
                pool.tensor_tensor(zT_[:, b % 2, :], zT_[:, b % 2, :], gam_txt[:, :], ALU.mult).then_inc(S["t_g"], 1)
                pool.wait_ge(S["t_g"], b + 1)
                pool.tensor_tensor(h_sb[:, IT + b, :], zT_[:, b % 2, :], bet_txt[:, :], ALU.add).then_inc(S["h_txt"], 1)
            pool.wait_ge(S["h_img"], IT)
            pool.wait_ge(S["h_txt"], B)
            pool.memset(va[:, :, :, :, DH:HA], 1.0).then_inc(set_up, 1)
            pool.memset(sm[:, :, :, :], NEG).then_inc(set_up, 1)
            pool.memset(cw[:, :, :], 1.0 / E_S).then_inc(set_up, 1)

            with pool.Fori(0, PAIRS) as it:
                pool.wait_ge(S["pair_done"], it + 1)
                pool.tensor_copy(hp[:, 0:1, :], h_sb[:, bass.ds(it, 1), :]).then_inc(S["b_hp"], 1)
                pool.tensor_copy(hp[:, 1:3, :], h_sb[:, bass.ds(it * 2 + IT, 2), :]).then_inc(S["b_hp"], 1)

                def deviations(v, r):
                    pool.wait_ge(S[v], it + 1)
                    pool.tensor_tensor(rs[:, 0:TP], ve[:, 0:TP], minus_half[:, 0:TP], ALU.pow).then_inc(S[r], 1)

                deviations("b_ve1", "b_rs1")
                deviations("b_ve2", "b_rs2")
                n = 0
                for g in range(HG):
                    for ty in (2, 3):
                        pool.wait_ge(S["b_e"], it * (2 * HG) + (n + 1))
                        pool.tensor_tensor(carrier_p[:, :], minus_half[:, 0:1], minus_half[:, 1:2], ALU.add)
                        pool.tensor_scalar(ee[:, ty - 2, :], ee[:, ty - 2, :], 1.0, None, ALU.min).then_inc(S["b_clip"], 1)
                        pool.wait_ge(S["b_clip"], it * (2 * HG) + (n + 1))
                        pool.wait_ge(S["b_r"], it * (2 * HG) + (n + 1))
                        pool.tensor_tensor(qk[:, ty, g, :], qk[:, ty, g, :], ee[:, ty - 2, :], ALU.add).then_inc(S["b_phi"], 1)
                        n += 1
                deviations("c_ve1", "c_rs1")
                deviations("c_ve2", "c_rs2")
                pool.tensor_tensor(hx[:, :, :], hp[:, :, :], x2[:, :, :], ALU.add).then_inc(S["c_hx"], 1)
                deviations("c_ve3", "c_rs3")
                pool.tensor_copy(acc[:, bass.ds(it * TP, TP), :], h2[:, :, :])
                pool.wait_ge(S["c_x3s"], it * KC + KC)
                pool.tensor_copy(x3T[:, :, bass.ds(it * PT, PT)], x3s[:, :, :])
                pool.wait_ge(S["c_cw"], it + 1)
                pool.tensor_copy(comb[:, bass.ds(it * TP, TP), :], cw[:, :, :]).then_inc(S["pair_done"], 1)

        @block.scalar
        def _(act):
            act.wait_ge(ld_const, 48)
            act.wait_ge(S["a_zT"], IT)
            for c in range(KC):
                act.activation(xT[:, c, :], PS[0:DC, 4 + c, :], ACT.Identity, bias=col("tok_ln_b", c, DC),
                               scale=col("tok_ln_g", c, DC)).then_inc(S["a_xg"], 1)

            def gelu_tanh(base):
                for m in range(FM):
                    bank = m % 4 if base == 0 else 2 + m % 4
                    act.wait_ge(S["a_ff1"], base + m + 1)
                    act.activation(h1T[:, m, :], PS[:, bank, :], ACT.Gelu_apprx_tanh, bias=col("tok_ff1_b", m)
                                   ).then_inc(S["a_h"], 1)

            gelu_tanh(0)
            for g in range(HG):
                j = 2 * g + 1
                act.wait_ge(S["a_mm"], j + 1)
                act.activation(tk[:, g, :], PS[:, j % 4, :], ACT.Identity, bias=col("tok_k_b", g)).then_inc(S["a_k"], 1)
            for w in range(B):
                act.wait_ge(S["a_vmm"], w + 1)
                act.activation(tv[:, w, :, 0:DH], PS[0:IMG, 6 + w % 2, 0:D].rearrange("p (h e) -> p h e", e=DH),
                               ACT.Copy).then_inc(S["a_v"], 1)
            for i in range(IT):
                act.wait_ge(S["a_sub"], i + 1)
                act.activation(pA[:, i % 2, :, :], pA[:, i % 2, :, :], ACT.Exp).then_inc(S["a_exp"], 1)
                act.wait_ge(S["a_pT"], i + 1)
                if i >= 1:
                    act.wait_ge(S["a_o"], i)
                act.activation(ptA[:, :, :].rearrange("p h q -> p (h q)"),
                               PS[0:IMG, 4:7, :].rearrange("p a b -> p (a b)"), ACT.Copy).then_inc(S["a_ptc"], 1)
                act.wait_ge(S["a_oT"], i + 1)
                act.activation(aTA[:, :, 128 * i:128 * i + 128], PS[0:DC, 7, 256:512].rearrange("p (c t) -> p c t", c=KC),
                               ACT.Copy).then_inc(S["a_at"], 1)
            gelu_tanh(FM)
            for i in range(IT):
                act.wait_ge(S["a_hmm"], i + 1)
                act.activation(h_sb[:, i, :], PS[:, 6 + i % 2, 0:D], ACT.Copy).then_inc(S["h_img"], 1)
            for b in range(B):
                act.wait_ge(S["t_dT"], b + 1)
                if b >= 2:
                    act.wait_ge(S["t_pm"], b - 1)
                act.activation(domT[:, b % 2, :], PS[:, b % 2, 0:128], ACT.Copy).then_inc(S["t_dc"], 1)

            act.wait_ge(set_up, 6)
            with act.Fori(0, PAIRS) as it:
                act.wait_ge(S["pair_done"], it + 1)
                act.wait_ge(S["b_zT"], it * TP + TP)
                for c in range(KC):
                    seq = xnT[:, c, :].rearrange("p (b s) -> p b s", b=2)
                    for lo, hi, src in ((0, IMG, PS[0:DC, c, 0:128]), (IMG, L, PS[0:DC, c, 128:PT])):
                        act.activation(seq[:, :, lo:hi], src.rearrange("p (b s) -> p b s", b=2), ACT.Identity,
                                       bias=col("ln1_b", c, DC), scale=col("ln1_g", c, DC)).then_inc(S["b_xn"], 1)
                for g in range(HG):
                    act.wait_ge(S["b_mm"], it * (4 * HG) + (4 * g + 2))
                    act.activation(qk[:, 1, g, :], PS[:, 1, 0:PT], ACT.Identity, bias=col("k_b", g)).then_inc(S["b_k"], 1)
                    for ty, bias in ((2, "q2_b"), (3, "k2_b")):
                        act.wait_ge(S["b_r"], it * (2 * HG) + (2 * g + ty - 1))
                        if g >= 1:
                            act.wait_ge(S["b_phi"], it * (2 * HG) + (2 * (g - 1) + ty - 1))
                        act.activation(ee[:, ty - 2, :], PS[:, ty, 0:PT], ACT.Exp, bias=col(bias, g)).then_inc(S["b_e"], 1)
                for k in range(4):
                    act.wait_ge(S["b_vmm"], it * 4 + (k + 1))
                    act.activation(va[:, k, :, :, 0:DH].rearrange("p t h e -> p (t h) e"),
                                   PS[0:QC, 4 + k % 2, 0:2 * D].rearrange("p (h e) -> p h e", e=DH), ACT.Copy
                                   ).then_inc(S["b_v"], 1)

                def weights_out(u):
                    act.wait_ge(S["b_pT"], it * (2 * NH) + (u + 1))
                    if u >= 2:
                        act.wait_ge(S["b_o"], it * (2 * NH) + (u - 1))
                    act.activation(pts[:, u % 2, :], PS[0:QC, 4, 0:2 * L], ACT.Copy).then_inc(S["b_ptc"], 1)

                for bb in range(2):
                    for h in range(NH):
                        u = NH * bb + h
                        act.wait_ge(S["b_nm"], it * (2 * NH) + (u + 1))
                        if u >= 2:
                            act.wait_ge(S["b_pT"], it * (2 * NH) + (u - 1))
                        for q in range(2):
                            e = act.activation(pb[:, u % 2, q, :], sm[:, u % 2, q, :], ACT.Exp, bias=nm[:, u % 2, q:q + 1])
                        e.then_inc(S["b_ex"], 1)
                        if h >= 1:
                            weights_out(u - 1)
                    weights_out(NH * bb + NH - 1)
                    act.wait_ge(S["b_oT"], it * 2 + (bb + 1))
                    src = PS[0:DC, 4, 0:PT].rearrange("p (c s) -> p c s", c=KC)
                    act.activation(aoT[:, :, IMG * bb:IMG * bb + IMG], src[:, :, 0:IMG], ACT.Copy)
                    act.activation(aoT[:, :, 128 + TXT * bb:128 + TXT * bb + TXT], src[:, :, IMG:L], ACT.Copy
                                   ).then_inc(S["b_ao"], 1)

                def gain(done, ready, dst, g_name, b_name, bank):
                    act.wait_ge(S[ready], it * TP + TP)
                    for c in range(KC):
                        act.activation(dst[:, c, :], PS[0:DC, bank + c, 0:PT], ACT.Identity, bias=col(b_name, c, DC),
                                       scale=col(g_name, c, DC)).then_inc(S[done], 1)

                gain("c_sl", "c_z1T", slT, "ssm_ln_g", "ssm_ln_b", 4)
                gain("c_m", "c_z2T", mT, "lnm_g", "lnm_b", 4)
                for m in range(FM):
                    act.wait_ge(S["c_ff1"], it * FM + (m + 1))
                    act.activation(hT[:, m, :], PS[:, m % 4, 0:PT], ACT.Gelu, bias=col("mlp_b1", m)).then_inc(S["c_h"], 1)
                act.wait_ge(S["c_x3T"], it * TP + TP)
                for c in range(KC):
                    act.activation(x3s[:, c, :], PS[0:DC, c, 0:PT], ACT.Copy).then_inc(S["c_x3s"], 1)
                act.wait_ge(S["c_ls"], it + 1)
                act.activation(lg[:, :, :], lg[:, :, :], ACT.Exp).then_inc(S["c_ex"], 1)

            act.wait_ge(S["pair_done"], PAIRS + 1)
            with act.Fori(0, NE // 2) as r:
                for half in range(2):
                    for s in range(3):
                        for m in range(FM):
                            n = (half * 3 + s) * FM + m
                            act.wait_ge(S["e_up"], r * (6 * FM) + (n + 1))
                            act.wait_ge(S["e_gu"], r * (6 * FM) + (n + 1))
                            act.activation(sg[:, n % 2, :], PS[:, n % 2, :], ACT.Silu).then_inc(S["e_sg"], 1)

        @block.vector
        def _(dve):
            links = [0, 0]

            def carry():
                dve.memset(carrier[:, :], 0.0)

            def link(ins, alone=False):
                links[0] += 1
                ins.then_inc(vs, 1)
                dve.wait_ge(vs, links[1] + links[0])
                if alone:
                    carry()

            def statistics(src, k, eps, s, m, v):
                link(dve.bn_stats(s[:, :], src), True)
                link(dve.bn_aggr(m[:, k, :], s[:, :]))
                return dve.tensor_scalar(v[:, k:k + 1], m[:, k, 1:2], eps, None, ALU.add)

            dve.wait_ge(ld_const, 48)
            dve.tensor_scalar(phi_b[:, :], cols[:, COLS["q2_b"]:COLS["q2_b"] + 2 * HG], 1e-4, None, ALU.add)
            for i in range(IT):
                dve.wait_ge(S["patch_mm"], i + 1)
                statistics(PS[:, i, 0:D], i, 1e-5, st, mv, ve).then_inc(S["a_ve"], 1)
            for i in range(IT):
                dve.wait_ge(S["a_rs"], i + 1)
                dve.tensor_scalar(zA[:, i, :], PS[:, i, 0:D], mv[:, i, 0:1], rs[:, i:i + 1], ALU.subtract, ALU.mult
                                  ).then_inc(S["a_z"], 1)
            dve.wait_ge(ld_tok, 7 * 16)
            for c in range(KC):
                dve.wait_ge(S["a_xg"], c + 1)
                v = xT[:, c, :].rearrange("p (b s) -> p b s", s=IMG)
                dve.tensor_tensor(v, v, pe_tab[:, c:c + 1, :].broadcast_to([DC, B, IMG]), ALU.add).then_inc(S["a_x"], 1)
            for c in range(KC):
                dve.wait_ge(S["a_ff2"], c + 1)
                dve.tensor_scalar(y1T[:, c, :], PS[0:DC, 4 + c, :], col("tok_ff2_b", c, DC), None, ALU.add
                                  ).then_inc(S["a_y"], 1)
            for g in range(HG):
                dve.wait_ge(S["a_mm"], 2 * g + 1)
                dve.tensor_scalar(tq[:, g, :], PS[:, (2 * g) % 4, :], col("tok_q_b", g), DH ** -0.5, ALU.add, ALU.mult
                                  ).then_inc(S["a_q"], 1)
            for i in range(IT):
                dve.wait_ge(S["a_s"], i + 1)
                sc = PS[:, 0:4, 0:HG * IMG].rearrange("p r (g k) -> p r g k", k=IMG)
                link(dve.reduce_max(mxA[:, :].rearrange("p (r g) -> p r g", r=4), sc, AX.X))
                if i >= 2:
                    dve.wait_ge(S["a_pT"], i - 1)
                dve.tensor_tensor(pA[:, i % 2, :, :].rearrange("p (r g) k -> p r g k", r=4), sc,
                                  mxA[:, :].rearrange("p (r g o) -> p r g o", r=4, o=1).broadcast_to([128, 4, HG, IMG]),
                                  ALU.subtract).then_inc(S["a_sub"], 1)
                dve.wait_ge(S["a_o"], i + 1)
                o = PS[:, 7, 0:NH * HA].rearrange("p (h e) -> p h e", e=HA)
                link(dve.reciprocal(rcA[:, :].rearrange("p (h o) -> p h o", o=1), o[:, :, DH:HA]))
                dve.tensor_tensor(oA[:, i, :, :], o[:, :, 0:DH],
                                  rcA[:, :].rearrange("p (h o) -> p h o", o=1).broadcast_to([128, NH, DH]), ALU.mult
                                  ).then_inc(S["a_on"], 1)
            for c in range(KC):
                dve.wait_ge(S["a_pj"], c + 1)
                dve.scalar_tensor_tensor(y1T[:, c, :], PS[0:DC, c, :], col("tok_proj_b", c, DC), xT[:, c, :],
                                         ALU.add, ALU.add).then_inc(S["a_x1"], 1)
            for b in range(B):
                dve.wait_ge(S["t_pm"], b + 1)
                link(dve.tensor_tensor(words[:, b, :], PS[:, 2 + b % 2, 0:D], words[:, b, :], ALU.add))
                dve.wait_ge(S["t_tp"], b + 1)
                link(dve.tensor_tensor(words[:, b, :], words[:, b, :], types[:, b, :], ALU.add))
                statistics(words[:, b, :], b, 1e-12, stT, mvT, veT).then_inc(S["t_ve"], 1)
                dve.wait_ge(S["t_rs"], b + 1)
                if b >= 2:
                    dve.wait_ge(S["h_txt"], b - 1)
                dve.tensor_scalar(zT_[:, b % 2, :], words[:, b, :], mvT[:, b, 0:1], rsT[:, b:b + 1], ALU.subtract, ALU.mult
                                  ).then_inc(S["t_z"], 1)

            dve.wait_ge(set_up, 6)
            dve.wait_ge(ld_attn, 11 * 16)
            straight = links[0]
            with dve.Fori(0, PAIRS) as it:
                links[0], links[1] = 0, it * LINKS_PER_PAIR + straight
                dve.wait_ge(S["pair_done"], it + 1)

                def norm(src, dst, v, r, done, eps=1e-5):
                    for t in range(TP):
                        ins = statistics(src(t), t, eps, st, mv, ve)
                        if t < TP - 1:
                            link(ins)
                    ins.then_inc(S[v], 1)
                    dve.wait_ge(S[r], it + 1)
                    for t in range(TP):
                        dve.tensor_scalar(dst[:, t, :], src(t), mv[:, t, 0:1], rs[:, t:t + 1], ALU.subtract, ALU.mult
                                          ).then_inc(S[done], 1)

                dve.wait_ge(S["b_hp"], it * 2 + 2)
                norm(lambda t: hp[:, t, :], xl, "b_ve1", "b_rs1", "b_x")
                dve.wait_ge(S["b_x"], it * TP + TP)
                norm(lambda t: xl[:, t, :], z, "b_ve2", "b_rs2", "b_z")
                for g in range(HG):
                    dve.wait_ge(S["b_mm"], it * (4 * HG) + (4 * g + 1))
                    dve.tensor_scalar(qk[:, 0, g, :], PS[:, 0, 0:PT], col("q_b", g), DH ** -0.5, ALU.add, ALU.mult
                                      ).then_inc(S["b_q"], 1)
                    for ty in (2, 3):
                        dve.wait_ge(S["b_mm"], it * (4 * HG) + (4 * g + ty + 1))
                        dve.tensor_scalar(qk[:, ty, g, :], PS[:, ty, 0:PT], phi_b[:, HG * (ty - 2) + g:HG * (ty - 2) + g + 1], 1e-4,
                                          ALU.add, ALU.max
                                          ).then_inc(S["b_r"], 1)
                for bb in range(2):
                    for h in range(NH):
                        u = NH * bb + h
                        dve.wait_ge(S["b_s"], it * (2 * NH) + (u + 1))
                        if u >= 2:
                            dve.wait_ge(S["b_ex"], it * (2 * NH) + (u - 1))
                        carry()
                        dve.copy_predicated(sm[:, u % 2, :, :].rearrange("p a b -> p (a b)"),
                                            keep[:, :, :].rearrange("p a b -> p (a b)"),
                                            PS[0:QC, h % 4, 0:2 * L]).then_inc(S["b_cp"], 1)
                        dve.wait_ge(S["b_cp"], it * (2 * NH) + (u + 1))
                        dve.reduce_max(nm[:, u % 2, :], sm[:, u % 2, :, :], AX.X, negate=True).then_inc(S["b_nm"], 1)
                        dve.wait_ge(S["b_att"], it * (2 * NH) + (u + 1))
                        if u >= 2:
                            dve.wait_ge(S["b_o"], it * (2 * NH) + (u - 1))
                        dve.tensor_tensor(lin[:, u % 2, :], PS[0:QC, 5, 0:L + QC], causal[:, :], ALU.mult
                                          ).then_inc(S["b_lin"], 1)
                    dve.wait_ge(S["b_o"], it * (2 * NH) + NH * (bb + 1))
                    o = PS[0:QC, 6:8, 0:2 * NH * HA].rearrange("p q (h e) -> p q h e", e=HA)
                    link(dve.tensor_copy(dn[:, :, :], o[:, :, :, DH]))
                    link(dve.tensor_scalar(dn[:, :, NH:2 * NH], dn[:, :, NH:2 * NH], 1e-4, None, ALU.add))
                    link(dve.reciprocal(dn[:, :, :], dn[:, :, :]))
                    dve.tensor_tensor(oN[:, :, :, :], o[:, :, :, 0:DH],
                                      dn[:, :, :].rearrange("p q (h o) -> p q h o", o=1).broadcast_to([QC, 2, 2 * NH, DH]),
                                      ALU.mult).then_inc(S["b_on"], 1)
                    dve.wait_ge(S["b_oT"], it * 2 + (bb + 1))
                    src = PS[0:DC, 5, 0:PT].rearrange("p (c s) -> p c s", c=KC)
                    dve.tensor_copy(soT[:, :, IMG * bb:IMG * bb + IMG], src[:, :, 0:IMG])
                    dve.tensor_copy(soT[:, :, 128 + TXT * bb:128 + TXT * bb + TXT], src[:, :, IMG:L]).then_inc(S["b_so"], 1)
                dve.wait_ge(S["c_so"], it * TP + TP)
                norm(lambda t: PS[:, t, 0:D], z, "c_ve1", "c_rs1", "c_z1")
                for c in range(KC):
                    dve.wait_ge(S["c_pj"], it * KC + (c + 1))
                    dve.wait_ge(S["c_sl"], it * KC + (c + 1))
                    dve.scalar_tensor_tensor(uT[:, c, :], PS[0:DC, 6 + c, 0:PT], col("attn_proj_b", c, DC), slT[:, c, :],
                                             ALU.add, ALU.add).then_inc(S["c_u"], 1)
                for t in range(TP):
                    dve.wait_ge(S["c_mm"], it * TP + (t + 1))
                    dve.tensor_tensor(x2[:, t, :], PS[:, t, 0:D], xl[:, t, :], ALU.add).then_inc(S["c_x2"], 1)
                dve.wait_ge(S["c_x2"], it * TP + TP)
                norm(lambda t: x2[:, t, :], z, "c_ve2", "c_rs2", "c_z2")
                dve.wait_ge(S["c_hx"], it + 1)
                for t in range(TP):
                    dve.wait_ge(S["c_ff2"], it * TP + (t + 1))
                    dve.tensor_tensor(h2[:, t, :], PS[:, 4 + t, 0:D], hx[:, t, :], ALU.add).then_inc(S["c_h2"], 1)
                dve.wait_ge(S["c_h2"], it * TP + TP)
                norm(lambda t: h2[:, t, :], z, "c_ve3", "c_rs3", "c_x3")
                dve.wait_ge(S["c_lg"], it + 1)

                def over(v):
                    return v.rearrange("p (t o) -> p t o", o=1).broadcast_to([128, TP, E_R])

                logits = PS[:, 2, 0:TP * E_R].rearrange("p (t e) -> p t e", e=E_R)
                link(dve.reduce_max(r1[:, 0, :], logits, AX.X))
                dve.tensor_tensor(lg[:, :, :], logits, over(r1[:, 0, :]), ALU.subtract).then_inc(S["c_ls"], 1)
                dve.wait_ge(S["c_ex"], it + 1)
                link(dve.reduce_sum(r1[:, 1, :], lg[:, :, :], AX.X))
                link(dve.reciprocal(r1[:, 1, :], r1[:, 1, :]))
                link(dve.tensor_tensor(lg[:, :, :], lg[:, :, :], over(r1[:, 1, :]), ALU.mult))
                for k in range(2):
                    top, first, hot = r1[:, 2 + k, :], r1[:, 4, :], sel[:, k, :, :]
                    link(dve.reduce_max(top, lg[:, :, :], AX.X))
                    link(dve.tensor_tensor(hot, lg[:, :, :], over(top), ALU.is_equal))
                    link(dve.tensor_tensor(hot, hot, rank[:, :, :], ALU.mult))
                    link(dve.reduce_max(first, hot, AX.X))
                    link(dve.tensor_tensor(hot, rank[:, :, :], over(first), ALU.is_equal))
                    if k == 0:
                        link(dve.scalar_tensor_tensor(lg[:, :, :], hot, -2.0, lg[:, :, :], ALU.mult, ALU.add))
                link(dve.tensor_tensor(r1[:, 4, :], r1[:, 2, :], r1[:, 3, :], ALU.add))
                link(dve.tensor_scalar(r1[:, 4, :], r1[:, 4, :], 1e-8, None, ALU.add))
                link(dve.reciprocal(r1[:, 4, :], r1[:, 4, :]))
                for k in range(2):
                    link(dve.tensor_tensor(r1[:, 2 + k, :], r1[:, 2 + k, :], r1[:, 4, :], ALU.mult))
                    link(dve.tensor_tensor(sel[:, k, :, :], sel[:, k, :, :], over(r1[:, 2 + k, :]), ALU.mult))
                dve.tensor_tensor(cw[:, :, E_S:NE], sel[:, 0, :, :], sel[:, 1, :, :], ALU.add).then_inc(S["c_cw"], 1)
                assert links[0] == LINKS_PER_PAIR, links

            dve.wait_ge(S["pair_done"], PAIRS + 1)
            dve.sem_inc(S["e_gu"], 2)
            dve.sem_inc(S["e_acc"], 0 + 4)
            with dve.Fori(0, NE // 2) as r:
                for half in range(2):
                    for s in range(3):
                        for m in range(FM):
                            n = (half * 3 + s) * FM + m
                            dve.wait_ge(S["e_sg"], r * (6 * FM) + (n + 1))
                            if m == 0:
                                dve.wait_ge(S["e_dn"], r * 24 + (4 * (half * 3 + s) + 4))
                            dve.tensor_tensor(gu[:, s_buf(half, s), m, :], sg[:, n % 2, :], PS[:, 2 + n % 2, :], ALU.mult
                                              ).then_inc(S["e_gu"], 1)
                        for t in range(4):
                            k = (half * 3 + s) * 4 + t
                            dve.wait_ge(S["e_dn"], r * 24 + (k + 9))
                            e = r * 2 + half
                            tile = 4 * s + t
                            dve.scalar_tensor_tensor(acc[:, tile, :], PS[:, 4 + t, 0:D],
                                                     comb[:, tile, bass.ds(e, 1)], acc[:, tile, :], ALU.mult, ALU.add
                                                     ).then_inc(S["e_acc"], 1)

        @block.tensor
        def _(pe):
            def accumulate(dst, pairs):
                for k, (lhs, rhs) in enumerate(pairs):
                    mm = pe.matmul(dst, lhs, rhs, start=(k == 0), stop=(k == len(pairs) - 1))
                return mm

            pe.wait_ge(ld_patch, 32)
            pe.wait_ge(ld_const, 48)
            pe.wait_ge(set_up, 3)
            for i in range(IT):
                accumulate(PS[:, i, 0:D], [(patches[:, j, 128 * i:128 * i + 128], w_patch[:, j, :]) for j in range(FM)]
                           + [(ones[:, 0:128], row("patch_b"))]).then_inc(S["patch_mm"], 1)
            for i in range(IT):
                pe.wait_ge(S["a_z"], i + 1)
                for c in range(KC):
                    mm = pe.transpose(PS[0:DC, 4 + c, 128 * i:128 * i + 128], zA[:, i, DC * c:DC * c + DC], ident[:, :])
                mm.then_inc(S["a_zT"], 1)
            pe.wait_ge(ld_tok, 7 * 16)

            def tok_up(src, base, bank0):
                for m in range(FM):
                    if m >= 4:
                        pe.wait_ge(S["a_h"], base + m - 3)
                    accumulate(PS[:, bank0 + m % 4, :], [(w_tff1[:, c, 128 * m:128 * m + 128], src[:, c, :]) for c in range(KC)]
                               ).then_inc(S["a_ff1"], 1)

            pe.wait_ge(S["a_x"], KC)
            tok_up(xT, 0, 0)
            pe.wait_ge(S["a_h"], FM)
            for c in range(KC):
                accumulate(PS[0:DC, 4 + c, :], [(w_tff2[:, m, DC * c:DC * c + DC], h1T[:, m, :]) for m in range(FM)]
                           ).then_inc(S["a_ff2"], 1)
            pe.wait_ge(S["a_y"], KC)
            for g in range(HG):
                for w, done in ((w_tq, "a_q"), (w_tk, "a_k")):
                    j = 2 * g + (w is w_tk)
                    if g == 2:
                        pe.wait_ge(S[done], 1)
                    accumulate(PS[:, j % 4, :], [(w[:, c, 128 * g:128 * g + 128], y1T[:, c, :]) for c in range(KC)]
                               ).then_inc(S["a_mm"], 1)
            for w in range(B):
                if w >= 2:
                    pe.wait_ge(S["a_v"], w - 1)
                accumulate(PS[0:IMG, 6 + w % 2, 0:D],
                           [(y1T[:, c, IMG * w:IMG * w + IMG], w_tv[:, c, :]) for c in range(KC)]
                           + [(ones[:, 0:IMG], row("tok_v_b"))]).then_inc(S["a_vmm"], 1)

            def img_scores(i):
                if i >= 1:
                    pe.wait_ge(S["a_sub"], i)
                for w in range(2):
                    at = 128 * i + IMG * w
                    for g in range(HG):
                        for r in range(4):
                            mm = pe.matmul(PS[IMG * w:IMG * w + IMG, r, IMG * g:IMG * g + IMG],
                                           tq[32 * r:32 * r + DH, g, at:at + IMG], tk[32 * r:32 * r + DH, g, at:at + IMG],
                                           start=True, stop=True)
                mm.then_inc(S["a_s"], 1)

            pe.wait_ge(S["a_q"], HG)
            pe.wait_ge(S["a_k"], HG)
            img_scores(0)
            pe.wait_ge(S["a_v"], B)
            for i in range(IT):
                if i + 1 < IT:
                    img_scores(i + 1)
                pe.wait_ge(S["a_exp"], i + 1)
                if i >= 1:
                    pe.wait_ge(S["a_ptc"], i)
                for k in range(NH):
                    mm = pe.transpose(PS[0:IMG, 4 + k // 4, 128 * (k % 4):128 * (k % 4) + 128], pA[:, i % 2, k, :],
                                      ident[:, :])
                mm.then_inc(S["a_pT"], 1)
                pe.wait_ge(S["a_ptc"], i + 1)
                if i >= 1:
                    pe.wait_ge(S["a_at"], i)
                for w in range(2):
                    for k in range(NH):
                        h = 4 * (k % HG) + k // HG
                        mm = pe.matmul(PS[IMG * w:IMG * w + IMG, 7, HA * h:HA * h + HA],
                                       ptA[:, k, IMG * w:IMG * w + IMG], tv[:, 2 * i + w, h, :], start=True, stop=True)
                mm.then_inc(S["a_o"], 1)
                pe.wait_ge(S["a_on"], i + 1)
                for c in range(KC):
                    mm = pe.transpose(PS[0:DC, 7, 256 + 128 * c:384 + 128 * c],
                                      oA[:, i, 6 * c:6 * c + 6, :].rearrange("p h e -> p (h e)"), ident[:, :])
                mm.then_inc(S["a_oT"], 1)
            pe.wait_ge(S["a_at"], IT)
            for c in range(KC):
                accumulate(PS[0:DC, c, :], [(w_tproj[:, k, DC * c:DC * c + DC], aTA[:, k, :]) for k in range(KC)]
                           ).then_inc(S["a_pj"], 1)
            pe.wait_ge(S["a_x1"], KC)
            tok_up(y1T, FM, 2)
            pe.wait_ge(S["a_h"], 2 * FM)
            for i in range(IT):
                if i >= 2:
                    pe.wait_ge(S["h_img"], i - 1)
                at = slice(128 * i, 128 * i + 128)
                dst = PS[:, 6 + i % 2, :]
                for k, (lhs, rhs) in enumerate([(h1T[:, m, at], w_tff2[:, m, :]) for m in range(FM)]
                                               + [(ones[:, 0:128], row("tok_ff2_b"))]):
                    pe.matmul(dst[:, 0:D], lhs, rhs, start=(k == 0), stop=False)
                for c in range(KC):
                    mm = pe.matmul(dst[:, DC * c:DC * c + DC], y1T[:, c, at], ident[0:DC, 0:DC], start=False, stop=(c == KC - 1))
                mm.then_inc(S["a_hmm"], 1)
            pe.wait_ge(ld_txt, 48)
            for b in range(B):
                pe.wait_ge(gathered[b], 64)
                if b >= 2:
                    pe.wait_ge(S["t_dc"], b - 1)
                pe.transpose(PS[:, b % 2, 0:128], dom[:, b, :], ident[:, :]).then_inc(S["t_dT"], 1)
                pe.wait_ge(S["t_dc"], b + 1)
                if b >= 2:
                    pe.wait_ge(S["t_ve"], b - 1)
                accumulate(PS[:, 2 + b % 2, 0:D], [(domT[:, b % 2, :], w_txt[:, :]), (ones[:, 0:128], row("txt_proj_b"))]
                           ).then_inc(S["t_pm"], 1)

            pe.wait_ge(set_up, 6)
            pe.wait_ge(ld_attn, 11 * 16)
            with pe.Fori(0, PAIRS) as it:
                pe.wait_ge(S["pair_done"], it + 1)

                def turned(ready, done, bank):
                    for t in range(TP):
                        pe.wait_ge(S[ready], it * TP + (t + 1))
                        for c in range(KC):
                            mm = pe.transpose(PS[0:DC, bank + c, 128 * t:128 * t + 128], z[:, t, DC * c:DC * c + DC], ident[:, :])
                        mm.then_inc(S[done], 1)

                turned("b_z", "b_zT", 0)
                pe.wait_ge(S["b_xn"], it * 4 + 4)
                for g in range(HG):
                    for ty in range(4):
                        if g >= 1:
                            if ty == 0:
                                pe.wait_ge(S["b_q"], it * HG + g)
                            elif ty == 1:
                                pe.wait_ge(S["b_k"], it * HG + g)
                            else:
                                pe.wait_ge(S["b_e"], it * (2 * HG) + (2 * g + ty - 3))
                                pe.wait_ge(S["b_r"], it * (2 * HG) + (2 * g + ty - 3))
                        accumulate(PS[:, ty, 0:PT], [(w_qk[:, ty, c, 128 * g:128 * g + 128], xnT[:, c, :]) for c in range(KC)]
                                   ).then_inc(S["b_mm"], 1)
                for k in range(4):
                    if k >= 2:
                        pe.wait_ge(S["b_v"], it * 4 + (k - 1))
                    accumulate(PS[0:QC, 4 + k % 2, 0:2 * D],
                               [(xnT[:, c, QC * k:QC * k + QC], w_v[:, c, :]) for c in range(KC)]
                               + [(ones[:, 0:QC], row("v_b", 2 * D))]).then_inc(S["b_vmm"], 1)
                pe.wait_ge(S["b_q"], it * HG + HG)
                pe.wait_ge(S["b_k"], it * HG + HG)
                pe.wait_ge(S["b_e"], it * (2 * HG) + 2 * HG)
                pe.wait_ge(S["b_phi"], it * (2 * HG) + 2 * HG)
                pe.wait_ge(S["b_v"], it * 4 + 4)

                def scores(u):
                    bb, h = divmod(u, NH)
                    r, g = h % 4, h // 4
                    hr = slice(32 * r, 32 * r + DH)
                    if u >= 4:
                        pe.wait_ge(S["b_cp"], it * (2 * NH) + (u - 3))
                    for q in range(2):
                        at = L * bb + QC * q
                        mm = pe.matmul(PS[0:QC, r, L * q:L * q + L], qk[hr, 0, g, at:at + QC], qk[hr, 1, g, L * bb:L * bb + L],
                                       start=True, stop=True)
                    mm.then_inc(S["b_s"], 1)
                    if h >= 1:
                        pe.wait_ge(S["b_lin"], it * (2 * NH) + u)
                    elif bb == 1:
                        pe.wait_ge(S["b_so"], it * 2 + 1)
                    for k in range(2):
                        at = L * bb + QC * k
                        mm = pe.matmul(PS[0:QC, 5, L * k:L * k + L - QC * k], qk[hr, 3, g, at:at + QC],
                                       qk[hr, 2, g, at:L * bb + L], start=True, stop=True)
                    mm.then_inc(S["b_att"], 1)

                def turn(u):
                    pe.wait_ge(S["b_ex"], it * (2 * NH) + (u + 1))
                    if u % NH >= 1:
                        pe.wait_ge(S["b_ptc"], it * (2 * NH) + u)
                    elif u:
                        pe.wait_ge(S["b_ao"], it * 2 + 1)
                    for k in range(2):
                        for q in range(2):
                            mm = pe.transpose(PS[0:QC, 4, L * k + QC * q:L * k + QC * q + QC],
                                              pb[:, u % 2, q, QC * k:QC * k + QC], ident[0:QC, 0:QC])
                    mm.then_inc(S["b_pT"], 1)

                def values(u):
                    bb, h = divmod(u, NH)
                    pe.wait_ge(S["b_ptc"], it * (2 * NH) + (u + 1))
                    pe.wait_ge(S["b_lin"], it * (2 * NH) + (u + 1))
                    if h == 0 and bb == 1:
                        pe.wait_ge(S["b_on"], it * 2 + 1)
                    for q in range(2):
                        accumulate(PS[0:QC, 6 + q, HA * h:HA * h + HA],
                                   [(pts[:, u % 2, L * k + QC * q:L * k + QC * q + QC], va[:, 2 * bb + k, 0, h, :]) for k in range(2)])
                        at = HA * (NH + h)
                        mm = accumulate(PS[0:QC, 6 + q, at:at + HA],
                                        [(lin[:, u % 2, L * k + QC * (q - k):L * k + QC * (q - k) + QC], va[:, 2 * bb + k, 1, h, :])
                                         for k in range(q + 1)])
                    mm.then_inc(S["b_o"], 1)

                for bb in range(2):
                    u0 = NH * bb
                    scores(u0)
                    for u in range(u0, u0 + NH):
                        if u + 1 < u0 + NH:
                            scores(u + 1)
                        turn(u)
                        if u > u0:
                            values(u - 1)
                    values(u0 + NH - 1)
                    pe.wait_ge(S["b_on"], it * 2 + (bb + 1))
                    for ty in range(2):
                        for c in range(KC):
                            for q in range(2):
                                mm = pe.transpose(PS[0:DC, 4 + ty, L * c + QC * q:L * c + QC * q + QC],
                                                  oN[:, q, NH * ty + 6 * c:NH * ty + 6 * c + 6, :].rearrange("p h e -> p (h e)"),
                                                  ident[0:QC, 0:QC])
                    mm.then_inc(S["b_oT"], 1)
                tiles = [slice(128 * t, 128 * t + 128) for t in range(TP)]
                pe.wait_ge(S["b_so"], it * 2 + 2)
                for t in range(TP):
                    accumulate(PS[:, t, 0:D], [(soT[:, c, tiles[t]], w_sout[:, c, :]) for c in range(KC)]
                               + [(ones[:, 0:128], row("ssm_out_b"))]).then_inc(S["c_so"], 1)
                pe.wait_ge(S["b_ao"], it * 2 + 2)
                for c in range(KC):
                    accumulate(PS[0:DC, 6 + c, 0:PT], [(w_aproj[:, k, DC * c:DC * c + DC], aoT[:, k, :]) for k in range(KC)]
                               ).then_inc(S["c_pj"], 1)
                turned("c_z1", "c_z1T", 4)
                pe.wait_ge(S["c_u"], it * KC + KC)
                for t in range(TP):
                    accumulate(PS[:, t, 0:D], [(uT[:, c, tiles[t]], w_out[:, c, :]) for c in range(KC)]
                               + [(ones[:, 0:128], row("out_b"))]).then_inc(S["c_mm"], 1)
                turned("c_z2", "c_z2T", 4)
                pe.wait_ge(S["c_m"], it * KC + KC)
                for m in range(FM):
                    if m >= 4:
                        pe.wait_ge(S["c_h"], it * FM + (m - 3))
                    accumulate(PS[:, m % 4, 0:PT], [(w_m1[:, c, 128 * m:128 * m + 128], mT[:, c, :]) for c in range(KC)]
                               ).then_inc(S["c_ff1"], 1)
                pe.wait_ge(S["c_h"], it * FM + FM)
                for t in range(TP):
                    accumulate(PS[:, 4 + t, 0:D], [(hT[:, m, tiles[t]], w_m2[:, m, :]) for m in range(FM)]
                               + [(ones[:, 0:128], row("mlp_b2"))]).then_inc(S["c_ff2"], 1)
                turned("c_x3", "c_x3T", 0)
                pe.wait_ge(S["c_x3s"], it * KC + KC)
                for t in range(TP):
                    mm = accumulate(PS[:, 2, E_R * t:E_R * t + E_R], [(x3s[:, c, tiles[t]], w_gate[:, c, :]) for c in range(KC)])
                mm.then_inc(S["c_lg"], 1)

            pe.wait_ge(S["pair_done"], PAIRS + 1)
            pe.sem_inc(S["e_dn"], 8)
            with pe.Fori(0, NE // 2) as r:
                for half in range(2):
                    pe.wait_ge(S[f"w_ld{half}"], r * 48 + 48)
                    for s in range(3):
                        at = slice(512 * s, 512 * s + 512)
                        for m in range(FM):
                            n = (half * 3 + s) * FM + m
                            pe.wait_ge(S["e_gu"], r * (6 * FM) + (n + 1))
                            for k in range(2):
                                mm = accumulate(PS[:, 2 * k + n % 2, :],
                                                [(wgu[:, half, k, c, 128 * m:128 * m + 128], x3T[:, c, at]) for c in range(KC)])
                            mm.then_inc(S["e_up"], 1)
                        pe.wait_ge(S["e_gu"], r * (6 * FM) + ((half * 3 + s) * FM + FM + 2))
                        for t in range(4):
                            pe.wait_ge(S["e_acc"], r * 24 + ((half * 3 + s) * 4 + t + 1))
                            mm = accumulate(PS[:, 4 + t, 0:D],
                                            [(gu[:, s_buf(half, s), m, 128 * t:128 * t + 128], wdn[:, half, m, :]) for m in range(FM)])
                            mm.then_inc(S["e_dn"], 1)


LINKS_PER_PAIR = 68


def s_buf(half, s):
    return (half * 3 + s) % 2


def layout(i):
    f = np.float32

    def chunks(w, p):
        return np.ascontiguousarray(w.reshape(-1, p, w.shape[-1]).transpose(1, 0, 2))

    def spread(w):
        o = np.zeros(w.shape[:-1] + (NH, 32), f)
        o[..., :DH] = w.reshape(w.shape[:-1] + (NH, DH))
        return o.reshape(w.shape[:-1] + (NH * 32,))

    def vec(v, p):
        o = np.zeros((128, v.size // p), f)
        o[:p] = v.reshape(-1, p).T
        return o

    a = {}
    x = i["x"].reshape(B, 3, 8, 16, 8, 16).transpose(1, 3, 5, 0, 2, 4).reshape(FF, NI)
    a["patches"] = chunks(x, 128)
    a["w_patch"] = chunks(i["L0_tok_patch_w"].reshape(D, FF).T, 128)
    tqkv, tb = i["L0_tok_qkv_w"], i["L0_tok_qkv_b"]
    a["w_tff1"] = chunks(i["L0_tok_ff1_w"], DC)
    a["w_tff2"] = chunks(i["L0_tok_ff2_w"], 128)
    a["w_tq"] = chunks(spread(tqkv[:, 0:D]), DC)
    a["w_tk"] = chunks(spread(tqkv[:, D:2 * D]), DC)
    a["w_tv"] = chunks(tqkv[:, 2 * D:], DC)
    a["w_tproj"] = chunks(i["L0_tok_proj_w"], DC)
    a["w_txt"] = np.ascontiguousarray(i["L0_txt_proj_w"].T)
    a["gam_txt"] = np.ascontiguousarray(np.broadcast_to(i["L0_txt_ln_gamma"], (128, D)))
    a["bet_txt"] = np.ascontiguousarray(np.broadcast_to(i["L0_txt_ln_beta"], (128, D)))
    w1, b1 = i["L0_attn_attn_qkv_w"], i["L0_attn_attn_qkv_b"]
    w2, b2 = i["L0_attn_ssm_qkv_w"], i["L0_attn_ssm_qkv_b"]
    a["w_qk"] = np.ascontiguousarray(np.stack([chunks(spread(w[:, k * D:k * D + D]), DC) for w in (w1, w2) for k in (0, 1)], 1))
    a["w_v"] = chunks(np.concatenate([w1[:, 2 * D:], w2[:, 2 * D:]], 1), DC)
    a["w_aproj"] = chunks(i["L0_attn_attn_proj_w"], DC)
    a["w_sout"] = chunks(i["L0_attn_ssm_out_w"], DC)
    a["w_out"] = chunks(i["L0_attn_out_w"], DC)
    a["w_m1"] = chunks(i["L0_attn_mlp_w1"], DC)
    a["w_m2"] = chunks(i["L0_attn_mlp_w2"], 128)
    a["w_gate"] = chunks(i["L0_ffn_gate_w"].T, DC)
    v = {"tok_ln_g": (i["L0_tok_ln_g"], DC), "tok_ln_b": (i["L0_tok_ln_b"], DC), "tok_ff1_b": (i["L0_tok_ff1_b"], 128),
         "tok_ff2_b": (i["L0_tok_ff2_b"], DC), "tok_q_b": (spread(tb[0:D]), 128), "tok_k_b": (spread(tb[D:2 * D]), 128),
         "tok_proj_b": (i["L0_tok_proj_b"], DC), "ln1_g": (i["L0_attn_ln1_g"], DC), "ln1_b": (i["L0_attn_ln1_b"], DC),
         "q_b": (spread(b1[0:D]), 128), "k_b": (spread(b1[D:2 * D]), 128), "q2_b": (spread(b2[0:D]), 128),
         "k2_b": (spread(b2[D:2 * D]), 128), "attn_proj_b": (i["L0_attn_attn_proj_b"], DC),
         "ssm_ln_g": (i["L0_attn_ssm_ln_g"], DC), "ssm_ln_b": (i["L0_attn_ssm_ln_b"], DC),
         "lnm_g": (i["L0_attn_lnm_g"], DC), "lnm_b": (i["L0_attn_lnm_b"], DC), "mlp_b1": (i["L0_attn_mlp_b1"], 128)}
    a["cols"] = np.concatenate([vec(*v[n]) for n in COLS], 1)
    r = {"patch_b": i["L0_tok_patch_b"], "tok_v_b": tb[2 * D:], "tok_ff2_b": i["L0_tok_ff2_b"], "txt_proj_b": i["L0_txt_proj_b"],
         "v_b": np.concatenate([b1[2 * D:], b2[2 * D:]]), "ssm_out_b": i["L0_attn_ssm_out_b"], "out_b": i["L0_attn_out_b"],
         "mlp_b2": i["L0_attn_mlp_b2"]}
    a["rows"] = np.concatenate([r[n] for n in ROWS])[None]
    a["word_table"], a["type_table"] = i["L0_txt_word_table"], i["L0_txt_type_table"]
    a["pos_table"], a["domain_table"] = i["L0_txt_pos_table"], i["L0_txt_domain_table"]
    a["ids"] = np.ascontiguousarray(np.stack([i["x_txt"].T, i["mask_BS_i0_1"].T, i["pos_BS"].T, i["itok_BS_0_4999"].T], 1))
    for n, s, rt in (("wg", "shared_wg", "wg"), ("wu", "shared_wu", "wu")):
        w = np.concatenate([i["L0_ffn_" + s], i["L0_ffn_" + rt]])
        a[n] = np.ascontiguousarray(w.reshape(NE, KC, DC, FF).transpose(0, 2, 1, 3))
    w = np.concatenate([i["L0_ffn_shared_wd"], i["L0_ffn_wd"]])
    a["wd"] = np.ascontiguousarray(w.reshape(NE, FM, 128, D).transpose(0, 2, 1, 3))
    a["ident"] = np.eye(128, dtype=f)
    q, k = np.arange(L)[:, None], np.arange(L)[None]
    near = (k <= q) & (k > q - WINDOW)
    a["keep"] = np.ascontiguousarray(near.reshape(2, QC, L).transpose(1, 0, 2)).astype(np.int32)
    past = np.where(k.T <= q.T, f(DH ** -0.5), f(0))
    a["causal"] = np.concatenate([past[0:QC], past[QC:, QC:]], 1)
    a["rank"] = np.ascontiguousarray(np.broadcast_to(np.arange(E_R, 0, -1, dtype=f), (128, TP, E_R)))
    ang = np.arange(IMG, dtype=f)[:, None] / np.power(f(10000.0), f(2.0) * np.arange(D // 2, dtype=f)[None] / f(D))
    pe = np.zeros((IMG, D), f)
    pe[:, 0::2], pe[:, 1::2] = np.sin(ang), np.cos(ang)
    a["pe_tab"] = chunks(np.ascontiguousarray(pe.T), DC)
    return a


def kernel(**inputs):
    import concourse.bacc as bacc
    from concourse.bass_utils import run_bass_kernel_spmd

    nc = bacc.Bacc("TRN2", target_bir_lowering=False, num_devices=1)
    arrays = layout({k: np.asarray(v) for k, v in inputs.items()})
    args = {n: nc.dram_tensor(f"in_{n}", v.shape, mybir.dt.from_np(v.dtype), kind="ExternalInput").ap()
            for n, v in arrays.items()}
    out = nc.dram_tensor("out_h", (B, L, D), F32, kind="ExternalOutput").ap()
    build(nc, args, out)
    r = run_bass_kernel_spmd(nc, [{f"in_{n}": v for n, v in arrays.items()}], core_ids=[0])
    return r.results[0]["out_h"]
```

```python
import numpy as np
import concourse.bass as bass
from concourse import mybir
from contextlib import ExitStack

F32 = mybir.dt.float32
I32 = mybir.dt.int32
U32 = mybir.dt.uint32
ALU = mybir.AluOpType
ACT = mybir.ActivationFunctionType
AX = mybir.AxisListType

B = 8
IMG = 64
TXT = 128
L = IMG + TXT
D = 192
KC = 2
DC = D // KC
FF = 768
FM = FF // 128
NH, DH = 12, 16
HG = NH // 4
NI = B * IMG
IT = NI // 128
PAIRS = B // 2
PT = 2 * L
TP = PT // 128
NT = PAIRS * TP
NTOK = B * L
QC = L // 2
E_R, E_S = 16, 2
NE = E_R + E_S
TOPK = 2
RT = (TOPK * NTOK + E_R * 127) // 128
NEG = -10000.0
WINDOW = 64
HA = DH + 1

COLS = {}
_c = 0
for _name, _n in [("tok_ln_g", KC), ("tok_ln_b", KC), ("tok_ff1_b", FM), ("tok_ff2_b", KC), ("tok_q_b", HG),
                  ("tok_k_b", HG), ("tok_proj_b", KC), ("ln1_g", KC), ("ln1_b", KC), ("q_b", HG), ("k_b", HG),
                  ("q2_b", HG), ("k2_b", HG), ("attn_proj_b", KC), ("ssm_ln_g", KC), ("ssm_ln_b", KC),
                  ("lnm_g", KC), ("lnm_b", KC), ("mlp_b1", FM)]:
    COLS[_name] = _c
    _c += _n
NCOL = _c
ROWS = {}
_c = 0
for _name, _n in [("patch_b", D), ("tok_v_b", D), ("tok_ff2_b", D), ("txt_proj_b", D), ("v_b", 2 * D),
                  ("ssm_out_b", D), ("out_b", D), ("mlp_b2", D)]:
    ROWS[_name] = _c
    _c += _n
NROW = _c


def build(nc, a, out):
    ctx = ExitStack()
    with ctx:
        def sb(name, shape, dt=F32):
            return ctx.enter_context(nc.sbuf_tensor(name, shape, dt))

        def sem(name):
            return ctx.enter_context(nc.semaphore(name))

        ident = sb("ident", [128, 128])
        ones = sb("ones", [1, 512])
        cols = sb("cols", [128, NCOL])
        rows = sb("rows", [1, NROW])
        keep = sb("keep", [QC, 2, L], I32)
        causal = sb("causal", [QC, L + QC])
        rank = sb("rank", [128, TP, E_R])
        w_qk = sb("w_qk", [DC, 4, KC, HG * 128])
        w_v = sb("w_v", [DC, KC, 2 * D])
        w_aproj = sb("w_aproj", [DC, KC, D])
        w_sout = sb("w_sout", [DC, KC, D])
        w_out = sb("w_out", [DC, KC, D])
        w_m1 = sb("w_m1", [DC, KC, FF])
        w_m2 = sb("w_m2", [128, FM, D])
        w_gate = sb("w_gate", [DC, KC, E_R])
        minus_half = sb("minus_half", [128, 4])
        phi_b = sb("phi_b", [128, 2 * HG])
        zeros = sb("zeros", [128, D])
        carrier = sb("carrier", [128, 1])
        carrier_p = sb("carrier_p", [128, 1])

        h_sb = sb("h_sb", [128, IT + B, D])
        acc = sb("acc", [128, NT, D])
        x3T = sb("x3T", [DC, KC, NTOK])
        chosen = sb("chosen", [128, TOPK, NT, E_R])
        weight = sb("weight", [128, TOPK, NT])
        earlier = sb("earlier", [128, 128])
        ones_sq = sb("ones_sq", [128, 128])
        steps = sb("steps", [128, NT])
        tile_no = sb("tile_no", [1, RT])
        st = sb("st", [128, 6])
        mv = sb("mv", [128, 4, 2])
        ve = sb("ve", [128, 4])
        rs = sb("rs", [128, 4])

        PS = ctx.enter_context(nc.psum_tensor("PS", [128, 8, 512], F32))

        ld_const = sem("ld_const")
        ld_patch = sem("ld_patch")
        ld_tok = sem("ld_tok")
        ld_txt = sem("ld_txt")
        ld_attn = sem("ld_attn")
        ld_moe = sem("ld_moe")
        ld_idx = sem("ld_idx")
        gathered = [sem(f"gathered{b}") for b in range(B)]
        set_up = sem("set_up")
        vs = sem("dve_step")
        stored = sem("stored")
        names = """patch_mm a_ve a_rs a_z a_zT a_xg a_x a_ff1 a_h a_ff2 a_y a_mm a_q a_k a_vmm a_v a_s a_sub a_exp
            a_pT a_ptc a_o a_on a_oT a_at a_pj a_x1 a_hmm h_img
            t_tp t_dT t_dc t_pm t_ve t_rs t_z t_g h_txt
            b_hp b_ve1 b_rs1 b_x b_ve2 b_rs2 b_z b_zT b_xn b_mm b_q b_k b_r b_e b_clip b_phi b_vmm b_v b_s b_att
            b_cp b_nm b_ex b_pT b_ptc b_lin b_o b_on b_oT b_ao b_so
            c_so c_ve1 c_rs1 c_z1 c_z1T c_sl c_pj c_u c_mm c_x2 c_ve2 c_rs2 c_z2 c_z2T c_m c_ff1 c_h c_ff2 c_hx c_h2
            c_ve3 c_rs3 c_x3 c_x3T c_x3s c_lg c_ls c_ex c_cw pair_done
            d_m d_cnt d_slot zeroed scattered
            e_up e_sg e_gu e_dn e_acc
            r_w0 r_w1 r_d0 r_d1 r_x0 r_x1 r_xT r_xe r_g r_sg r_u r_h r_y r_ye r_st0 r_st1 fetched0 fetched1 fetched2 final""".split()
        S = {n: sem(n) for n in names}

        scr = ExitStack()

        def tb(name, shape, dt=F32):
            return scr.enter_context(nc.sbuf_tensor(name, shape, dt))

        w_patch = tb("w_patch", [128, FM, D])
        w_tff1 = tb("w_tff1", [DC, KC, FF])
        w_tff2 = tb("w_tff2", [128, FM, D])
        w_tq = tb("w_tq", [DC, KC, HG * 128])
        w_tk = tb("w_tk", [DC, KC, HG * 128])
        w_tv = tb("w_tv", [DC, KC, D])
        w_tproj = tb("w_tproj", [DC, KC, D])
        w_txt = tb("w_txt", [128, D])
        pe_tab = tb("pe_tab", [DC, KC, IMG])
        gam_txt = tb("gam_txt", [128, D])
        bet_txt = tb("bet_txt", [128, D])
        patches = tb("patches", [128, FM, NI])
        zA = tb("zA", [128, IT, D])
        xT = tb("xT", [DC, KC, NI])
        h1T = tb("h1T", [128, FM, NI])
        y1T = tb("y1T", [DC, KC, NI])
        tq = tb("tq", [128, HG, NI])
        tk = tb("tk", [128, HG, NI])
        tv = tb("tv", [IMG, B, NH, HA])
        pA = tb("pA", [128, 2, NH, IMG])
        mxA = tb("mxA", [128, NH])
        ptA = tb("ptA", [IMG, NH, 128])
        rcA = tb("rcA", [128, NH])
        oA = tb("oA", [128, IT, NH, DH])
        aTA = tb("aTA", [DC, KC, NI])
        ids = tb("ids", [128, 4, B], I32)
        words = tb("words", [128, B, D])
        types = tb("types", [128, B, D])
        poss = tb("poss", [128, B, D])
        dom = tb("dom", [128, B, 128])
        domT = tb("domT", [128, 2, 128])
        zT_ = tb("z_txt", [128, 2, D])
        mvT = tb("mvT", [128, B, 2])
        veT = tb("veT", [128, B])
        rsT = tb("rsT", [128, B])
        stT = tb("stT", [128, 6])
        scr.close()
        x3 = sb("x3", [128, NT, D])
        w_sgu = sb("w_sgu", [DC, E_S, 2, KC, FF])
        w_sdn = sb("w_sdn", [128, E_S, FM, D])
        scr2 = ExitStack()

        def tb2(name, shape, dt=F32):
            return scr2.enter_context(nc.sbuf_tensor(name, shape, dt))

        hp = tb2("hp", [128, TP, D])
        xl = tb2("xl", [128, TP, D])
        z = tb2("z", [128, TP, D])
        xnT = tb2("xnT", [DC, KC, PT])
        qk = tb2("qk", [128, 4, HG, PT])
        ee = tb2("ee", [128, 2, PT])
        va = tb2("va", [QC, 4, 2, NH, HA])
        sm = tb2("sm", [QC, 2, 2, L])
        nm = tb2("nm", [QC, 2, 2])
        pb = tb2("pb", [QC, 2, 2, L])
        pts = tb2("pts", [QC, 2, 2 * L])
        lin = tb2("lin", [QC, 2, L + QC])
        dn = tb2("dn", [QC, 2, 2 * NH])
        oN = tb2("oN", [QC, 2, 2 * NH, DH])
        aoT = tb2("aoT", [DC, KC, PT])
        soT = tb2("soT", [DC, KC, PT])
        slT = tb2("slT", [DC, KC, PT])
        uT = tb2("uT", [DC, KC, PT])
        x2 = tb2("x2", [128, TP, D])
        hx = tb2("hx", [128, TP, D])
        h2 = tb2("h2", [128, TP, D])
        mT = tb2("mT", [DC, KC, PT])
        hT = tb2("hT", [128, FM, PT])
        x3s = tb2("x3s", [DC, KC, PT])
        lg = tb2("lg", [128, TP, E_R])
        r1 = tb2("r1", [128, 6, TP])
        sel = tb2("sel", [128, 3, TP, E_R])
        wt = tb2("wt", [128, TOPK, TP])
        scr2.close()
        scr3 = ExitStack()

        def tb3(name, shape, dt=F32):
            return scr3.enter_context(nc.sbuf_tensor(name, shape, dt))

        mask = tb3("mask", [128, NT, E_R])
        before = tb3("before", [128, NT, E_R])
        count = tb3("count", [128, E_R])
        beyond = tb3("beyond", [128, E_R, NT])
        tiles_of = tb3("tiles_of", [128, E_R])
        ends = tb3("ends", [128, E_R])
        ones_e = tb3("ones_e", [128, E_R])
        base = tb3("base", [128, E_R])
        at_slot = tb3("at_slot", [128, NT, E_R])
        pick = tb3("pick", [128, NT, E_R])
        slot_f = tb3("slot_f", [128, TOPK, NT])
        slot = tb3("slot", [128, TOPK, NT], I32)
        passed = tb3("passed", [1, RT, E_R])
        expert_f = tb3("expert_f", [1, RT])
        expert = tb3("expert", [1, RT], I32)
        w_rgu = tb3("w_rgu", [DC, 2, 2, KC, FF])
        w_rdn = tb3("w_rdn", [128, 2, FM, D])
        xs = tb3("xs", [128, 2, D])
        xt = tb3("xt", [DC, 2, KC, 128])
        rsg = tb3("rsg", [128, 2, FF])
        rh = tb3("rh", [128, 2, FF])
        ys = tb3("ys", [128, 2, D])
        yg = (h_sb, tb3("yg", [128, NT, D]))
        sg = tb3("sg", [128, 2, 512])
        gu = tb3("gu", [128, FM, 512])
        scr3.close()

        def col(name, i=0, n=128):
            return cols[0:n, COLS[name] + i:COLS[name] + i + 1]

        def row(name, n=D):
            return rows[0:1, ROWS[name]:ROWS[name] + n]

        x_slots = nc.dram_tensor("x_slots", (RT * 128, D), F32, kind="Internal").ap()
        y_slots = nc.dram_tensor("y_slots", (RT * 128, D), F32, kind="Internal").ap()
        x_tiles = x_slots.rearrange("(i p) d -> i p d", p=128)
        y_tiles = y_slots.rearrange("(i p) d -> i p d", p=128)

        def in_order(tile):
            def outer(eng, first, last):
                for i in range(first):
                    tile(i, i // 2, i % 2)
                rounds = (RT - first - last) // 2
                with eng.Fori(0, rounds) as r:
                    for k in range(2):
                        i = first + k
                        tile(r * 2 + i, r + i // 2, i % 2)
                for i in range(first + 2 * rounds, RT):
                    tile(i, i // 2, i % 2)
            return outer

        block = ctx.enter_context(nc.Block())

        @block.sync
        def _(sp):
            for dst, name in ((w_patch, "w_patch"), (patches, "patches")):
                sp.dma_start(dst[:, :, :], a[name]).then_inc(ld_patch, 16)
            for dst, name in ((ident, "ident"), (cols, "cols"), (rows, "rows")):
                sp.dma_start(dst[:, :], a[name]).then_inc(ld_const, 16)
            for dst, name in ((pe_tab, "pe_tab"), (w_tff1, "w_tff1"), (w_tff2, "w_tff2"), (w_tq, "w_tq"),
                              (w_tk, "w_tk"), (w_tv, "w_tv"), (w_tproj, "w_tproj")):
                sp.dma_start(dst[:, :, :], a[name]).then_inc(ld_tok, 16)
            for dst, name in ((w_txt, "w_txt"), (gam_txt, "gam_txt"), (bet_txt, "bet_txt")):
                sp.dma_start(dst[:, :], a[name]).then_inc(ld_txt, 16)
            sp.dma_start(w_qk[:, :, :, :], a["w_qk"]).then_inc(ld_attn, 16)
            for dst, name in ((keep, "keep"), (rank, "rank"), (w_v, "w_v"), (w_aproj, "w_aproj"), (w_sout, "w_sout"),
                              (w_out, "w_out"), (w_m1, "w_m1"), (w_m2, "w_m2"), (w_gate, "w_gate")):
                sp.dma_start(dst[:, :, :], a[name]).then_inc(ld_attn, 16)
            sp.dma_start(causal[:, :], a["causal"]).then_inc(ld_attn, 16)

            sp.wait_ge(set_up, 3)
            sp.dma_start(x_slots.rearrange("(i p) d -> p i d", p=128),
                         zeros[:, :].rearrange("p (o d) -> p o d", o=1).broadcast_to([128, RT, D])).then_inc(S["zeroed"], 16)
            for dst, name in ((earlier, "earlier"), (steps, "steps"), (tile_no, "tile_no")):
                sp.dma_start(dst[:, :], a[name]).then_inc(ld_moe, 16)
            sp.wait_ge(S["h_img"], IT)
            sp.wait_ge(S["h_txt"], B)
            for e in range(E_S):
                sp.dma_start(w_sgu[:, e, 0, :, :], a["shared_wg"][e]).then_inc(ld_moe, 16)
                sp.dma_start(w_sgu[:, e, 1, :, :], a["shared_wu"][e]).then_inc(ld_moe, 16)
                sp.dma_start(w_sdn[:, e, :, :], a["shared_wd"][e]).then_inc(ld_moe, 16)

            sp.wait_ge(S["d_slot"], 1)
            sp.wait_ge(S["scattered"], 16 * TOPK * NT)

            def load(i, n, j):
                static = isinstance(i, int)
                if not static or i >= 2:
                    sp.wait_ge(S["r_u"], i - 1)
                at = slice(i, i + 1) if static else bass.ds(i, 1)
                e = sp.value_load(expert[0:1, at], min_val=0, max_val=E_R - 1)
                for k, name in enumerate(("wg", "wu")):
                    sp.dma_start(w_rgu[:, j, k, :, :], a[name][bass.ds(e, 1)].rearrange("o p c n -> p (o c) n")).then_inc(S[f"r_w{j}"], 16)
                if not static or i >= 2:
                    sp.wait_ge(S["r_xT"], i - 1)
                sp.dma_start(xs[:, j:j + 1, :], x_tiles[at].rearrange("o p d -> p o d")).then_inc(S[f"r_x{j}"], 16)

            in_order(load)(sp, 2, 1)

            for s in range(3):
                sp.wait_ge(S["final"], 4 * (s + 1))
                for t in range(4 * s, 4 * s + 4):
                    p, t = divmod(t, TP)
                    if t == 0:
                        for k in range(2):
                            sp.dma_start(out[2 * p + k, 0:IMG, :], acc[IMG * k:IMG * k + IMG, TP * p, :]).then_inc(stored, 16)
                    else:
                        sp.dma_start(out[2 * p + t - 1, IMG:L, :], acc[:, TP * p + t, :]).then_inc(stored, 16)
            sp.wait_ge(stored, 16 * 2 * B)

        @block.gpsimd
        def _(pool):
            pool.memset(ones[:, :], 1.0).then_inc(set_up, 1)
            pool.memset(minus_half[:, :], -0.5).then_inc(set_up, 1)
            pool.wait_ge(set_up, 2)
            pool.memset(zeros[:, :], 0.0)
            pool.memset(ones_sq[:, :], 1.0)
            pool.memset(tv[:, :, :, DH:HA], 1.0).then_inc(set_up, 1)
            pool.sem_inc(S["pair_done"], 1)

            pool.dma_start(ids[:, :, :], a["ids"]).then_inc(ld_idx, 16)
            pool.wait_ge(ld_idx, 16)
            for b in range(B):
                for j, (dst, table) in enumerate(((words, "word_table"), (types, "type_table"), (poss, "pos_table"),
                                                  (dom, "domain_table"))):
                    pool.indirect_dma_start(dst[:, b, :], None, a[table],
                                            bass.IndirectOffsetOnAxis(ap=ids[:, j, b:b + 1].bitcast(U32), axis=0)
                                            ).then_inc(gathered[b], 16)
            for i in range(IT):
                pool.wait_ge(S["a_ve"], i + 1)
                pool.tensor_tensor(rs[:, i:i + 1], ve[:, i:i + 1], minus_half[:, 0:1], ALU.pow).then_inc(S["a_rs"], 1)
            for b in range(B):
                pool.wait_ge(gathered[b], 64)
                pool.tensor_tensor(types[:, b, :], types[:, b, :], poss[:, b, :], ALU.add).then_inc(S["t_tp"], 1)
            pool.wait_ge(ld_txt, 48)
            for b in range(B):
                pool.wait_ge(S["t_ve"], b + 1)
                pool.tensor_tensor(rsT[:, b:b + 1], veT[:, b:b + 1], minus_half[:, 0:1], ALU.pow).then_inc(S["t_rs"], 1)
                pool.wait_ge(S["t_z"], b + 1)
                pool.tensor_tensor(zT_[:, b % 2, :], zT_[:, b % 2, :], gam_txt[:, :], ALU.mult).then_inc(S["t_g"], 1)
                pool.wait_ge(S["t_g"], b + 1)
                pool.tensor_tensor(h_sb[:, IT + b, :], zT_[:, b % 2, :], bet_txt[:, :], ALU.add).then_inc(S["h_txt"], 1)
            pool.wait_ge(S["h_img"], IT)
            pool.wait_ge(S["h_txt"], B)
            pool.memset(va[:, :, :, :, DH:HA], 1.0).then_inc(set_up, 1)
            pool.memset(sm[:, :, :, :], NEG).then_inc(set_up, 1)
            pool.sem_inc(set_up, 1)

            with pool.Fori(0, PAIRS) as it:
                pool.wait_ge(S["pair_done"], it + 1)
                pool.tensor_copy(hp[:, 0:1, :], h_sb[:, bass.ds(it, 1), :]).then_inc(S["b_hp"], 1)
                pool.tensor_copy(hp[:, 1:3, :], h_sb[:, bass.ds(it * 2 + IT, 2), :]).then_inc(S["b_hp"], 1)

                def deviations(v, r):
                    pool.wait_ge(S[v], it + 1)
                    pool.tensor_tensor(rs[:, 0:TP], ve[:, 0:TP], minus_half[:, 0:TP], ALU.pow).then_inc(S[r], 1)

                deviations("b_ve1", "b_rs1")
                deviations("b_ve2", "b_rs2")
                n = 0
                for g in range(HG):
                    for ty in (2, 3):
                        pool.wait_ge(S["b_e"], it * (2 * HG) + (n + 1))
                        pool.tensor_tensor(carrier_p[:, :], minus_half[:, 0:1], minus_half[:, 1:2], ALU.add)
                        pool.tensor_scalar(ee[:, ty - 2, :], ee[:, ty - 2, :], 1.0, None, ALU.min).then_inc(S["b_clip"], 1)
                        pool.wait_ge(S["b_clip"], it * (2 * HG) + (n + 1))
                        pool.wait_ge(S["b_r"], it * (2 * HG) + (n + 1))
                        pool.tensor_tensor(qk[:, ty, g, :], qk[:, ty, g, :], ee[:, ty - 2, :], ALU.add).then_inc(S["b_phi"], 1)
                        n += 1
                deviations("c_ve1", "c_rs1")
                deviations("c_ve2", "c_rs2")
                pool.tensor_tensor(hx[:, :, :], hp[:, :, :], x2[:, :, :], ALU.add).then_inc(S["c_hx"], 1)
                deviations("c_ve3", "c_rs3")
                pool.tensor_copy(acc[:, bass.ds(it * TP, TP), :], h2[:, :, :])
                pool.wait_ge(S["c_x3s"], it * KC + KC)
                pool.tensor_copy(x3T[:, :, bass.ds(it * PT, PT)], x3s[:, :, :])
                pool.wait_ge(S["c_cw"], it + 1)
                pool.tensor_copy(x3[:, bass.ds(it * TP, TP), :], z[:, :, :])
                for k in range(TOPK):
                    pool.tensor_copy(weight[:, k, bass.ds(it * TP, TP)], wt[:, k, :])
                    ins = pool.tensor_copy(chosen[:, k, bass.ds(it * TP, TP), :], sel[:, k, :, :])
                ins.then_inc(S["pair_done"], 1)

            pool.wait_ge(S["d_slot"], 1)
            pool.wait_ge(S["zeroed"], 16)
            for t in range(NT):
                for k in range(TOPK):
                    pool.indirect_dma_start(x_slots, bass.IndirectOffsetOnAxis(ap=slot[:, k, t:t + 1].bitcast(U32), axis=0),
                                            x3[:, t, :], None).then_inc(S["scattered"], 16)

            def store(i, n, j):
                pool.wait_ge(S["r_ye"], i + 3)
                at = slice(i, i + 1) if isinstance(i, int) else bass.ds(i, 1)
                pool.dma_start(y_tiles[at].rearrange("o p d -> p o d"), ys[:, j:j + 1, :]).then_inc(S[f"r_st{j}"], 16)

            in_order(store)(pool, 1, 0)
            pool.wait_ge(S["r_st0"], 16 * ((RT + 1) // 2))
            pool.wait_ge(S["r_st1"], 16 * (RT // 2))
            for t in range(NT):
                for k in range(TOPK):
                    pool.indirect_dma_start(yg[k][:, t, :], None, y_slots,
                                            bass.IndirectOffsetOnAxis(ap=slot[:, k, t:t + 1].bitcast(U32), axis=0)
                                            ).then_inc(S[f"fetched{t // 4}"], 16)

        @block.scalar
        def _(act):
            act.wait_ge(ld_const, 48)
            act.wait_ge(S["a_zT"], IT)
            for c in range(KC):
                act.activation(xT[:, c, :], PS[0:DC, 4 + c, :], ACT.Identity, bias=col("tok_ln_b", c, DC),
                               scale=col("tok_ln_g", c, DC)).then_inc(S["a_xg"], 1)

            def gelu_tanh(base):
                for m in range(FM):
                    bank = m % 4 if base == 0 else 2 + m % 4
                    act.wait_ge(S["a_ff1"], base + m + 1)
                    act.activation(h1T[:, m, :], PS[:, bank, :], ACT.Gelu_apprx_tanh, bias=col("tok_ff1_b", m)
                                   ).then_inc(S["a_h"], 1)

            gelu_tanh(0)
            for g in range(HG):
                j = 2 * g + 1
                act.wait_ge(S["a_mm"], j + 1)
                act.activation(tk[:, g, :], PS[:, j % 4, :], ACT.Identity, bias=col("tok_k_b", g)).then_inc(S["a_k"], 1)
            for w in range(B):
                act.wait_ge(S["a_vmm"], w + 1)
                act.activation(tv[:, w, :, 0:DH], PS[0:IMG, 6 + w % 2, 0:D].rearrange("p (h e) -> p h e", e=DH),
                               ACT.Copy).then_inc(S["a_v"], 1)
            for i in range(IT):
                act.wait_ge(S["a_sub"], i + 1)
                act.activation(pA[:, i % 2, :, :], pA[:, i % 2, :, :], ACT.Exp).then_inc(S["a_exp"], 1)
                act.wait_ge(S["a_pT"], i + 1)
                if i >= 1:
                    act.wait_ge(S["a_o"], i)
                act.activation(ptA[:, :, :].rearrange("p h q -> p (h q)"),
                               PS[0:IMG, 4:7, :].rearrange("p a b -> p (a b)"), ACT.Copy).then_inc(S["a_ptc"], 1)
                act.wait_ge(S["a_oT"], i + 1)
                act.activation(aTA[:, :, 128 * i:128 * i + 128], PS[0:DC, 7, 256:512].rearrange("p (c t) -> p c t", c=KC),
                               ACT.Copy).then_inc(S["a_at"], 1)
            gelu_tanh(FM)
            for i in range(IT):
                act.wait_ge(S["a_hmm"], i + 1)
                act.activation(h_sb[:, i, :], PS[:, 6 + i % 2, 0:D], ACT.Copy).then_inc(S["h_img"], 1)
            for b in range(B):
                act.wait_ge(S["t_dT"], b + 1)
                if b >= 2:
                    act.wait_ge(S["t_pm"], b - 1)
                act.activation(domT[:, b % 2, :], PS[:, b % 2, 0:128], ACT.Copy).then_inc(S["t_dc"], 1)

            act.wait_ge(set_up, 6)
            with act.Fori(0, PAIRS) as it:
                act.wait_ge(S["pair_done"], it + 1)
                act.wait_ge(S["b_zT"], it * TP + TP)
                for c in range(KC):
                    seq = xnT[:, c, :].rearrange("p (b s) -> p b s", b=2)
                    for lo, hi, src in ((0, IMG, PS[0:DC, c, 0:128]), (IMG, L, PS[0:DC, c, 128:PT])):
                        act.activation(seq[:, :, lo:hi], src.rearrange("p (b s) -> p b s", b=2), ACT.Identity,
                                       bias=col("ln1_b", c, DC), scale=col("ln1_g", c, DC)).then_inc(S["b_xn"], 1)
                for g in range(HG):
                    act.wait_ge(S["b_mm"], it * (4 * HG) + (4 * g + 2))
                    act.activation(qk[:, 1, g, :], PS[:, 1, 0:PT], ACT.Identity, bias=col("k_b", g)).then_inc(S["b_k"], 1)
                    for ty, bias in ((2, "q2_b"), (3, "k2_b")):
                        act.wait_ge(S["b_r"], it * (2 * HG) + (2 * g + ty - 1))
                        if g >= 1:
                            act.wait_ge(S["b_phi"], it * (2 * HG) + (2 * (g - 1) + ty - 1))
                        act.activation(ee[:, ty - 2, :], PS[:, ty, 0:PT], ACT.Exp, bias=col(bias, g)).then_inc(S["b_e"], 1)
                for k in range(4):
                    act.wait_ge(S["b_vmm"], it * 4 + (k + 1))
                    act.activation(va[:, k, :, :, 0:DH].rearrange("p t h e -> p (t h) e"),
                                   PS[0:QC, 4 + k % 2, 0:2 * D].rearrange("p (h e) -> p h e", e=DH), ACT.Copy
                                   ).then_inc(S["b_v"], 1)

                def weights_out(u):
                    act.wait_ge(S["b_pT"], it * (2 * NH) + (u + 1))
                    if u >= 2:
                        act.wait_ge(S["b_o"], it * (2 * NH) + (u - 1))
                    act.activation(pts[:, u % 2, :], PS[0:QC, 4, 0:2 * L], ACT.Copy).then_inc(S["b_ptc"], 1)

                for bb in range(2):
                    for h in range(NH):
                        u = NH * bb + h
                        act.wait_ge(S["b_nm"], it * (2 * NH) + (u + 1))
                        if u >= 2:
                            act.wait_ge(S["b_pT"], it * (2 * NH) + (u - 1))
                        for q in range(2):
                            e = act.activation(pb[:, u % 2, q, :], sm[:, u % 2, q, :], ACT.Exp, bias=nm[:, u % 2, q:q + 1])
                        e.then_inc(S["b_ex"], 1)
                        if h >= 1:
                            weights_out(u - 1)
                    weights_out(NH * bb + NH - 1)
                    act.wait_ge(S["b_oT"], it * 2 + (bb + 1))
                    src = PS[0:DC, 4, 0:PT].rearrange("p (c s) -> p c s", c=KC)
                    act.activation(aoT[:, :, IMG * bb:IMG * bb + IMG], src[:, :, 0:IMG], ACT.Copy)
                    act.activation(aoT[:, :, 128 + TXT * bb:128 + TXT * bb + TXT], src[:, :, IMG:L], ACT.Copy
                                   ).then_inc(S["b_ao"], 1)

                def gain(done, ready, dst, g_name, b_name, bank):
                    act.wait_ge(S[ready], it * TP + TP)
                    for c in range(KC):
                        act.activation(dst[:, c, :], PS[0:DC, bank + c, 0:PT], ACT.Identity, bias=col(b_name, c, DC),
                                       scale=col(g_name, c, DC)).then_inc(S[done], 1)

                gain("c_sl", "c_z1T", slT, "ssm_ln_g", "ssm_ln_b", 4)
                gain("c_m", "c_z2T", mT, "lnm_g", "lnm_b", 4)
                for m in range(FM):
                    act.wait_ge(S["c_ff1"], it * FM + (m + 1))
                    act.activation(hT[:, m, :], PS[:, m % 4, 0:PT], ACT.Gelu, bias=col("mlp_b1", m)).then_inc(S["c_h"], 1)
                act.wait_ge(S["c_x3T"], it * TP + TP)
                for c in range(KC):
                    act.activation(x3s[:, c, :], PS[0:DC, c, 0:PT], ACT.Copy).then_inc(S["c_x3s"], 1)
                act.wait_ge(S["c_ls"], it + 1)
                act.activation(lg[:, :, :], lg[:, :, :], ACT.Exp).then_inc(S["c_ex"], 1)

            act.wait_ge(S["pair_done"], PAIRS + 1)

            def shared(e):
                with act.Fori(0, 3) as s:
                    for m in range(FM):
                        n = e * 3 * FM + m
                        act.wait_ge(S["e_up"], s * FM + (n + 1))
                        act.wait_ge(S["e_gu"], s * FM + (n + 1))
                        act.activation(sg[:, m % 2, :], PS[:, m % 2, :], ACT.Silu).then_inc(S["e_sg"], 1)

            shared(0)
            act.sem_inc(S["r_ye"], 2)

            def tokens_out(i, j):
                act.wait_ge(S["r_xT"], i + 1)
                act.activation(xt[:, j, :, :], PS[0:DC, 6 + j, 0:KC * 128].rearrange("p (c t) -> p c t", c=KC), ACT.Copy
                               ).then_inc(S["r_xe"], 1)

            def results_out(i, n, j):
                act.wait_ge(S["r_y"], i + 3)
                if not isinstance(i, int) or i >= 2:
                    act.wait_ge(S[f"r_st{j}"], n * 16)
                act.activation(ys[:, j, :], PS[:, 4 + j, 0:D], ACT.Copy).then_inc(S["r_ye"], 1)

            tokens_out(0, 0)

            def gate(i, n, j):
                static = isinstance(i, int)
                e = act.value_load(expert[0:1, slice(i, i + 1) if static else bass.ds(i, 1)], min_val=0, max_val=E_R - 1)
                act.wait_ge(S["r_g"], i + 1)
                act.activation(rsg[:, j, :], PS[:, 0:2, :].rearrange("p a b -> p (a b)")[:, 0:FF], ACT.Silu).then_inc(S["r_sg"], 1)
                act.wait_ge(S["r_y"], i + 1)
                act.dma_start(w_rdn[:, j, :, :], a["wd"][bass.ds(e, 1)].rearrange("o p c n -> p (o c) n")).then_inc(S[f"r_d{j}"], 16)
                if not static or i + 1 < RT:
                    tokens_out(i + 1, 1 - j)
                if not static or i >= 1:
                    results_out(i - 1, n - 1 + j, 1 - j)

            in_order(gate)(act, 3, 2)
            results_out(RT - 1, (RT - 1) // 2, (RT - 1) % 2)
            shared(1)

        @block.vector
        def _(dve):
            links = [0, 0]

            def carry():
                dve.memset(carrier[:, :], 0.0)

            def link(ins, alone=False):
                links[0] += 1
                ins.then_inc(vs, 1)
                dve.wait_ge(vs, links[1] + links[0])
                if alone:
                    carry()

            def statistics(src, k, eps, s, m, v):
                link(dve.bn_stats(s[:, :], src), True)
                link(dve.bn_aggr(m[:, k, :], s[:, :]))
                return dve.tensor_scalar(v[:, k:k + 1], m[:, k, 1:2], eps, None, ALU.add)

            dve.wait_ge(ld_const, 48)
            dve.tensor_scalar(phi_b[:, :], cols[:, COLS["q2_b"]:COLS["q2_b"] + 2 * HG], 1e-4, None, ALU.add)
            for i in range(IT):
                dve.wait_ge(S["patch_mm"], i + 1)
                statistics(PS[:, i, 0:D], i, 1e-5, st, mv, ve).then_inc(S["a_ve"], 1)
            for i in range(IT):
                dve.wait_ge(S["a_rs"], i + 1)
                dve.tensor_scalar(zA[:, i, :], PS[:, i, 0:D], mv[:, i, 0:1], rs[:, i:i + 1], ALU.subtract, ALU.mult
                                  ).then_inc(S["a_z"], 1)
            dve.wait_ge(ld_tok, 7 * 16)
            for c in range(KC):
                dve.wait_ge(S["a_xg"], c + 1)
                v = xT[:, c, :].rearrange("p (b s) -> p b s", s=IMG)
                dve.tensor_tensor(v, v, pe_tab[:, c:c + 1, :].broadcast_to([DC, B, IMG]), ALU.add).then_inc(S["a_x"], 1)
            for c in range(KC):
                dve.wait_ge(S["a_ff2"], c + 1)
                dve.tensor_scalar(y1T[:, c, :], PS[0:DC, 4 + c, :], col("tok_ff2_b", c, DC), None, ALU.add
                                  ).then_inc(S["a_y"], 1)
            for g in range(HG):
                dve.wait_ge(S["a_mm"], 2 * g + 1)
                dve.tensor_scalar(tq[:, g, :], PS[:, (2 * g) % 4, :], col("tok_q_b", g), DH ** -0.5, ALU.add, ALU.mult
                                  ).then_inc(S["a_q"], 1)
            for i in range(IT):
                dve.wait_ge(S["a_s"], i + 1)
                sc = PS[:, 0:4, 0:HG * IMG].rearrange("p r (g k) -> p r g k", k=IMG)
                link(dve.reduce_max(mxA[:, :].rearrange("p (r g) -> p r g", r=4), sc, AX.X))
                if i >= 2:
                    dve.wait_ge(S["a_pT"], i - 1)
                dve.tensor_tensor(pA[:, i % 2, :, :].rearrange("p (r g) k -> p r g k", r=4), sc,
                                  mxA[:, :].rearrange("p (r g o) -> p r g o", r=4, o=1).broadcast_to([128, 4, HG, IMG]),
                                  ALU.subtract).then_inc(S["a_sub"], 1)
                dve.wait_ge(S["a_o"], i + 1)
                o = PS[:, 7, 0:NH * HA].rearrange("p (h e) -> p h e", e=HA)
                link(dve.reciprocal(rcA[:, :].rearrange("p (h o) -> p h o", o=1), o[:, :, DH:HA]))
                dve.tensor_tensor(oA[:, i, :, :], o[:, :, 0:DH],
                                  rcA[:, :].rearrange("p (h o) -> p h o", o=1).broadcast_to([128, NH, DH]), ALU.mult
                                  ).then_inc(S["a_on"], 1)
            for c in range(KC):
                dve.wait_ge(S["a_pj"], c + 1)
                dve.scalar_tensor_tensor(y1T[:, c, :], PS[0:DC, c, :], col("tok_proj_b", c, DC), xT[:, c, :],
                                         ALU.add, ALU.add).then_inc(S["a_x1"], 1)
            for b in range(B):
                dve.wait_ge(S["t_pm"], b + 1)
                link(dve.tensor_tensor(words[:, b, :], PS[:, 2 + b % 2, 0:D], words[:, b, :], ALU.add))
                dve.wait_ge(S["t_tp"], b + 1)
                link(dve.tensor_tensor(words[:, b, :], words[:, b, :], types[:, b, :], ALU.add))
                statistics(words[:, b, :], b, 1e-12, stT, mvT, veT).then_inc(S["t_ve"], 1)
                dve.wait_ge(S["t_rs"], b + 1)
                if b >= 2:
                    dve.wait_ge(S["h_txt"], b - 1)
                dve.tensor_scalar(zT_[:, b % 2, :], words[:, b, :], mvT[:, b, 0:1], rsT[:, b:b + 1], ALU.subtract, ALU.mult
                                  ).then_inc(S["t_z"], 1)

            dve.wait_ge(set_up, 6)
            dve.wait_ge(ld_attn, 11 * 16)
            straight = links[0]
            with dve.Fori(0, PAIRS) as it:
                links[0], links[1] = 0, it * LINKS_PER_PAIR + straight
                dve.wait_ge(S["pair_done"], it + 1)

                def norm(src, dst, v, r, done, eps=1e-5):
                    for t in range(TP):
                        ins = statistics(src(t), t, eps, st, mv, ve)
                        if t < TP - 1:
                            link(ins)
                    ins.then_inc(S[v], 1)
                    dve.wait_ge(S[r], it + 1)
                    for t in range(TP):
                        dve.tensor_scalar(dst[:, t, :], src(t), mv[:, t, 0:1], rs[:, t:t + 1], ALU.subtract, ALU.mult
                                          ).then_inc(S[done], 1)

                dve.wait_ge(S["b_hp"], it * 2 + 2)
                norm(lambda t: hp[:, t, :], xl, "b_ve1", "b_rs1", "b_x")
                dve.wait_ge(S["b_x"], it * TP + TP)
                norm(lambda t: xl[:, t, :], z, "b_ve2", "b_rs2", "b_z")
                for g in range(HG):
                    dve.wait_ge(S["b_mm"], it * (4 * HG) + (4 * g + 1))
                    dve.tensor_scalar(qk[:, 0, g, :], PS[:, 0, 0:PT], col("q_b", g), DH ** -0.5, ALU.add, ALU.mult
                                      ).then_inc(S["b_q"], 1)
                    for ty in (2, 3):
                        dve.wait_ge(S["b_mm"], it * (4 * HG) + (4 * g + ty + 1))
                        dve.tensor_scalar(qk[:, ty, g, :], PS[:, ty, 0:PT], phi_b[:, HG * (ty - 2) + g:HG * (ty - 2) + g + 1], 1e-4,
                                          ALU.add, ALU.max
                                          ).then_inc(S["b_r"], 1)
                for bb in range(2):
                    for h in range(NH):
                        u = NH * bb + h
                        dve.wait_ge(S["b_s"], it * (2 * NH) + (u + 1))
                        if u >= 2:
                            dve.wait_ge(S["b_ex"], it * (2 * NH) + (u - 1))
                        carry()
                        dve.copy_predicated(sm[:, u % 2, :, :].rearrange("p a b -> p (a b)"),
                                            keep[:, :, :].rearrange("p a b -> p (a b)"),
                                            PS[0:QC, h % 4, 0:2 * L]).then_inc(S["b_cp"], 1)
                        dve.wait_ge(S["b_cp"], it * (2 * NH) + (u + 1))
                        dve.reduce_max(nm[:, u % 2, :], sm[:, u % 2, :, :], AX.X, negate=True).then_inc(S["b_nm"], 1)
                        dve.wait_ge(S["b_att"], it * (2 * NH) + (u + 1))
                        if u >= 2:
                            dve.wait_ge(S["b_o"], it * (2 * NH) + (u - 1))
                        dve.tensor_tensor(lin[:, u % 2, :], PS[0:QC, 5, 0:L + QC], causal[:, :], ALU.mult
                                          ).then_inc(S["b_lin"], 1)
                    dve.wait_ge(S["b_o"], it * (2 * NH) + NH * (bb + 1))
                    o = PS[0:QC, 6:8, 0:2 * NH * HA].rearrange("p q (h e) -> p q h e", e=HA)
                    link(dve.tensor_copy(dn[:, :, :], o[:, :, :, DH]))
                    link(dve.tensor_scalar(dn[:, :, NH:2 * NH], dn[:, :, NH:2 * NH], 1e-4, None, ALU.add))
                    link(dve.reciprocal(dn[:, :, :], dn[:, :, :]))
                    dve.tensor_tensor(oN[:, :, :, :], o[:, :, :, 0:DH],
                                      dn[:, :, :].rearrange("p q (h o) -> p q h o", o=1).broadcast_to([QC, 2, 2 * NH, DH]),
                                      ALU.mult).then_inc(S["b_on"], 1)
                    dve.wait_ge(S["b_oT"], it * 2 + (bb + 1))
                    src = PS[0:DC, 5, 0:PT].rearrange("p (c s) -> p c s", c=KC)
                    dve.tensor_copy(soT[:, :, IMG * bb:IMG * bb + IMG], src[:, :, 0:IMG])
                    dve.tensor_copy(soT[:, :, 128 + TXT * bb:128 + TXT * bb + TXT], src[:, :, IMG:L]).then_inc(S["b_so"], 1)
                dve.wait_ge(S["c_so"], it * TP + TP)
                norm(lambda t: PS[:, t, 0:D], z, "c_ve1", "c_rs1", "c_z1")
                for c in range(KC):
                    dve.wait_ge(S["c_pj"], it * KC + (c + 1))
                    dve.wait_ge(S["c_sl"], it * KC + (c + 1))
                    dve.scalar_tensor_tensor(uT[:, c, :], PS[0:DC, 6 + c, 0:PT], col("attn_proj_b", c, DC), slT[:, c, :],
                                             ALU.add, ALU.add).then_inc(S["c_u"], 1)
                for t in range(TP):
                    dve.wait_ge(S["c_mm"], it * TP + (t + 1))
                    dve.tensor_tensor(x2[:, t, :], PS[:, t, 0:D], xl[:, t, :], ALU.add).then_inc(S["c_x2"], 1)
                dve.wait_ge(S["c_x2"], it * TP + TP)
                norm(lambda t: x2[:, t, :], z, "c_ve2", "c_rs2", "c_z2")
                dve.wait_ge(S["c_hx"], it + 1)
                for t in range(TP):
                    dve.wait_ge(S["c_ff2"], it * TP + (t + 1))
                    dve.tensor_tensor(h2[:, t, :], PS[:, 4 + t, 0:D], hx[:, t, :], ALU.add).then_inc(S["c_h2"], 1)
                dve.wait_ge(S["c_h2"], it * TP + TP)
                norm(lambda t: h2[:, t, :], z, "c_ve3", "c_rs3", "c_x3")
                dve.wait_ge(S["c_lg"], it + 1)

                def over(v):
                    return v.rearrange("p (t o) -> p t o", o=1).broadcast_to([128, TP, E_R])

                logits = PS[:, 2, 0:TP * E_R].rearrange("p (t e) -> p t e", e=E_R)
                link(dve.reduce_max(r1[:, 0, :], logits, AX.X))
                dve.tensor_tensor(lg[:, :, :], logits, over(r1[:, 0, :]), ALU.subtract).then_inc(S["c_ls"], 1)
                dve.wait_ge(S["c_ex"], it + 1)
                link(dve.reduce_sum(r1[:, 1, :], lg[:, :, :], AX.X))
                link(dve.reciprocal(r1[:, 1, :], r1[:, 1, :]))
                link(dve.tensor_tensor(lg[:, :, :], lg[:, :, :], over(r1[:, 1, :]), ALU.mult))
                for k in range(2):
                    top, first, hot = r1[:, 2 + k, :], r1[:, 4, :], sel[:, k, :, :]
                    link(dve.reduce_max(top, lg[:, :, :], AX.X))
                    link(dve.tensor_tensor(hot, lg[:, :, :], over(top), ALU.is_equal))
                    link(dve.tensor_tensor(hot, hot, rank[:, :, :], ALU.mult))
                    link(dve.reduce_max(first, hot, AX.X))
                    link(dve.tensor_tensor(hot, rank[:, :, :], over(first), ALU.is_equal))
                    if k == 0:
                        link(dve.scalar_tensor_tensor(lg[:, :, :], hot, -2.0, lg[:, :, :], ALU.mult, ALU.add))
                link(dve.tensor_tensor(r1[:, 4, :], r1[:, 2, :], r1[:, 3, :], ALU.add))
                link(dve.tensor_scalar(r1[:, 4, :], r1[:, 4, :], 1e-8, None, ALU.add))
                link(dve.reciprocal(r1[:, 4, :], r1[:, 4, :]))
                for k in range(TOPK):
                    ins = dve.tensor_tensor(wt[:, k, :], r1[:, 2 + k, :], r1[:, 4, :], ALU.mult)
                ins.then_inc(S["c_cw"], 1)
                assert links[0] == LINKS_PER_PAIR, links

            links[0], links[1] = 0, straight + PAIRS * LINKS_PER_PAIR
            dve.wait_ge(S["pair_done"], PAIRS + 1)
            dve.wait_ge(ld_moe, 16 * (3 + 3 * E_S))
            dve.tensor_tensor(mask[:, :, :], chosen[:, 0, :, :], chosen[:, 1, :, :], ALU.add).then_inc(S["d_m"], 1)
            dve.memset(ones_e[:, :], 1.0)
            link(dve.memset(before[:, 0, :], 0.0))
            dve.wait_ge(S["d_cnt"], 2)
            in_tile = PS[:, 5, 0:NT * E_R].rearrange("p (t e) -> p t e", e=E_R)
            for t in range(NT):
                dst = before[:, t + 1, :] if t + 1 < NT else count[:, :]
                link(dve.tensor_tensor(dst, before[:, t, :], in_tile[:, t, :], ALU.add))

            def per_expert(v, n):
                return v.rearrange("p (e o) -> p e o", o=1).broadcast_to([v.shape[0], E_R, n])

            def to_all(v, n):
                return v.rearrange("p (o e) -> p o e", o=1).broadcast_to([v.shape[0], n, v.shape[1]])

            link(dve.tensor_tensor(beyond[:, :, :], per_expert(count[:, :], NT), to_all(steps[:, :], E_R), ALU.is_gt))
            link(dve.reduce_sum(tiles_of[:, :], beyond[:, :, :], AX.X))
            link(dve.tensor_tensor_scan(ends[:, :], ones_e[:, :], tiles_of[:, :], 0.0, ALU.mult, ALU.add))
            link(dve.tensor_tensor(base[:, :], ends[:, :], tiles_of[:, :], ALU.subtract))
            link(dve.tensor_scalar(base[:, :], base[:, :], 128.0, None, ALU.mult))
            rank_in = PS[:, 4, 0:NT * E_R].rearrange("p (t e) -> p t e", e=E_R)
            link(dve.tensor_tensor(at_slot[:, :, :], rank_in, before[:, :, :], ALU.add))
            link(dve.tensor_tensor(at_slot[:, :, :], at_slot[:, :, :], to_all(base[:, :], NT), ALU.add))
            for k in range(TOPK):
                link(dve.tensor_tensor(pick[:, :, :], at_slot[:, :, :], chosen[:, k, :, :], ALU.mult))
                link(dve.reduce_sum(slot_f[:, k, :], pick[:, :, :], AX.X))
            link(dve.tensor_copy(slot[:, :, :], slot_f[:, :, :]))
            link(dve.tensor_tensor(passed[:, :, :], to_all(ends[0:1, :], RT),
                                   tile_no[:, :].rearrange("p (i o) -> p i o", o=1).broadcast_to([1, RT, E_R]), ALU.is_le))
            link(dve.reduce_sum(expert_f[:, :], passed[:, :, :], AX.X))
            link(dve.tensor_scalar(expert_f[:, :], expert_f[:, :], float(E_R - 1), None, ALU.min))
            dve.tensor_copy(expert[:, :], expert_f[:, :]).then_inc(S["d_slot"], 1)

            dve.sem_inc(S["e_gu"], 2)
            dve.sem_inc(S["e_acc"], 4)

            def shared(e):
                with dve.Fori(0, 3) as s:
                    for m in range(FM):
                        n = e * 3 * FM + m
                        dve.wait_ge(S["e_sg"], s * FM + (n + 1))
                        dve.tensor_tensor(gu[:, m, :], sg[:, m % 2, :], PS[:, 2 + m % 2, :], ALU.mult).then_inc(S["e_gu"], 1)
                    for t in range(4):
                        dve.wait_ge(S["e_dn"], s * 4 + (12 * e + t + 1))
                        res = acc[:, bass.ds(s * 4 + t, 1), :]
                        dve.scalar_tensor_tensor(res, PS[:, 4 + t:5 + t, 0:D], 1.0 / E_S, res, ALU.mult, ALU.add
                                                 ).then_inc(S["e_acc"], 1)

            def routed_sum(s):
                dve.wait_ge(S[f"fetched{s}"], 16 * TOPK * 4)
                dve.wait_ge(S["e_acc"], 4 + NT + 4 * (s + 1))
                for t in range(4 * s, 4 * s + 4):
                    for k in range(TOPK):
                        ins = dve.scalar_tensor_tensor(acc[:, t, :], yg[k][:, t, :], weight[:, k, t:t + 1], acc[:, t, :],
                                                       ALU.mult, ALU.add)
                        if k == 0:
                            link(ins)
                    ins.then_inc(S["final"], 1)

            shared(0)

            def hidden(i, n, j):
                dve.wait_ge(S["r_sg"], i + 1)
                dve.wait_ge(S["r_u"], i + 1)
                dve.tensor_tensor(rh[:, j, :], rsg[:, j, :], PS[:, 2:4, :].rearrange("p a b -> p (a b)")[:, 0:FF], ALU.mult
                                  ).then_inc(S["r_h"], 1)

            in_order(hidden)(dve, 1, 0)
            shared(1)
            for s in range(3):
                routed_sum(s)

        @block.tensor
        def _(pe):
            def accumulate(dst, pairs):
                for k, (lhs, rhs) in enumerate(pairs):
                    mm = pe.matmul(dst, lhs, rhs, start=(k == 0), stop=(k == len(pairs) - 1))
                return mm

            pe.wait_ge(ld_patch, 32)
            pe.wait_ge(ld_const, 48)
            pe.wait_ge(set_up, 3)
            for i in range(IT):
                accumulate(PS[:, i, 0:D], [(patches[:, j, 128 * i:128 * i + 128], w_patch[:, j, :]) for j in range(FM)]
                           + [(ones[:, 0:128], row("patch_b"))]).then_inc(S["patch_mm"], 1)
            for i in range(IT):
                pe.wait_ge(S["a_z"], i + 1)
                for c in range(KC):
                    mm = pe.transpose(PS[0:DC, 4 + c, 128 * i:128 * i + 128], zA[:, i, DC * c:DC * c + DC], ident[:, :])
                mm.then_inc(S["a_zT"], 1)
            pe.wait_ge(ld_tok, 7 * 16)

            def tok_up(src, base, bank0):
                for m in range(FM):
                    if m >= 4:
                        pe.wait_ge(S["a_h"], base + m - 3)
                    accumulate(PS[:, bank0 + m % 4, :], [(w_tff1[:, c, 128 * m:128 * m + 128], src[:, c, :]) for c in range(KC)]
                               ).then_inc(S["a_ff1"], 1)

            pe.wait_ge(S["a_x"], KC)
            tok_up(xT, 0, 0)
            pe.wait_ge(S["a_h"], FM)
            for c in range(KC):
                accumulate(PS[0:DC, 4 + c, :], [(w_tff2[:, m, DC * c:DC * c + DC], h1T[:, m, :]) for m in range(FM)]
                           ).then_inc(S["a_ff2"], 1)
            pe.wait_ge(S["a_y"], KC)
            for g in range(HG):
                for w, done in ((w_tq, "a_q"), (w_tk, "a_k")):
                    j = 2 * g + (w is w_tk)
                    if g == 2:
                        pe.wait_ge(S[done], 1)
                    accumulate(PS[:, j % 4, :], [(w[:, c, 128 * g:128 * g + 128], y1T[:, c, :]) for c in range(KC)]
                               ).then_inc(S["a_mm"], 1)
            for w in range(B):
                if w >= 2:
                    pe.wait_ge(S["a_v"], w - 1)
                accumulate(PS[0:IMG, 6 + w % 2, 0:D],
                           [(y1T[:, c, IMG * w:IMG * w + IMG], w_tv[:, c, :]) for c in range(KC)]
                           + [(ones[:, 0:IMG], row("tok_v_b"))]).then_inc(S["a_vmm"], 1)

            def img_scores(i):
                if i >= 1:
                    pe.wait_ge(S["a_sub"], i)
                for w in range(2):
                    at = 128 * i + IMG * w
                    for g in range(HG):
                        for r in range(4):
                            mm = pe.matmul(PS[IMG * w:IMG * w + IMG, r, IMG * g:IMG * g + IMG],
                                           tq[32 * r:32 * r + DH, g, at:at + IMG], tk[32 * r:32 * r + DH, g, at:at + IMG],
                                           start=True, stop=True)
                mm.then_inc(S["a_s"], 1)

            pe.wait_ge(S["a_q"], HG)
            pe.wait_ge(S["a_k"], HG)
            img_scores(0)
            pe.wait_ge(S["a_v"], B)
            for i in range(IT):
                if i + 1 < IT:
                    img_scores(i + 1)
                pe.wait_ge(S["a_exp"], i + 1)
                if i >= 1:
                    pe.wait_ge(S["a_ptc"], i)
                for k in range(NH):
                    mm = pe.transpose(PS[0:IMG, 4 + k // 4, 128 * (k % 4):128 * (k % 4) + 128], pA[:, i % 2, k, :],
                                      ident[:, :])
                mm.then_inc(S["a_pT"], 1)
                pe.wait_ge(S["a_ptc"], i + 1)
                if i >= 1:
                    pe.wait_ge(S["a_at"], i)
                for w in range(2):
                    for k in range(NH):
                        h = 4 * (k % HG) + k // HG
                        mm = pe.matmul(PS[IMG * w:IMG * w + IMG, 7, HA * h:HA * h + HA],
                                       ptA[:, k, IMG * w:IMG * w + IMG], tv[:, 2 * i + w, h, :], start=True, stop=True)
                mm.then_inc(S["a_o"], 1)
                pe.wait_ge(S["a_on"], i + 1)
                for c in range(KC):
                    mm = pe.transpose(PS[0:DC, 7, 256 + 128 * c:384 + 128 * c],
                                      oA[:, i, 6 * c:6 * c + 6, :].rearrange("p h e -> p (h e)"), ident[:, :])
                mm.then_inc(S["a_oT"], 1)
            pe.wait_ge(S["a_at"], IT)
            for c in range(KC):
                accumulate(PS[0:DC, c, :], [(w_tproj[:, k, DC * c:DC * c + DC], aTA[:, k, :]) for k in range(KC)]
                           ).then_inc(S["a_pj"], 1)
            pe.wait_ge(S["a_x1"], KC)
            tok_up(y1T, FM, 2)
            pe.wait_ge(S["a_h"], 2 * FM)
            for i in range(IT):
                if i >= 2:
                    pe.wait_ge(S["h_img"], i - 1)
                at = slice(128 * i, 128 * i + 128)
                dst = PS[:, 6 + i % 2, :]
                for k, (lhs, rhs) in enumerate([(h1T[:, m, at], w_tff2[:, m, :]) for m in range(FM)]
                                               + [(ones[:, 0:128], row("tok_ff2_b"))]):
                    pe.matmul(dst[:, 0:D], lhs, rhs, start=(k == 0), stop=False)
                for c in range(KC):
                    mm = pe.matmul(dst[:, DC * c:DC * c + DC], y1T[:, c, at], ident[0:DC, 0:DC], start=False, stop=(c == KC - 1))
                mm.then_inc(S["a_hmm"], 1)
            pe.wait_ge(ld_txt, 48)
            for b in range(B):
                pe.wait_ge(gathered[b], 64)
                if b >= 2:
                    pe.wait_ge(S["t_dc"], b - 1)
                pe.transpose(PS[:, b % 2, 0:128], dom[:, b, :], ident[:, :]).then_inc(S["t_dT"], 1)
                pe.wait_ge(S["t_dc"], b + 1)
                if b >= 2:
                    pe.wait_ge(S["t_ve"], b - 1)
                accumulate(PS[:, 2 + b % 2, 0:D], [(domT[:, b % 2, :], w_txt[:, :]), (ones[:, 0:128], row("txt_proj_b"))]
                           ).then_inc(S["t_pm"], 1)

            pe.wait_ge(set_up, 6)
            pe.wait_ge(ld_attn, 11 * 16)
            with pe.Fori(0, PAIRS) as it:
                pe.wait_ge(S["pair_done"], it + 1)

                def turned(ready, done, bank):
                    for t in range(TP):
                        pe.wait_ge(S[ready], it * TP + (t + 1))
                        for c in range(KC):
                            mm = pe.transpose(PS[0:DC, bank + c, 128 * t:128 * t + 128], z[:, t, DC * c:DC * c + DC], ident[:, :])
                        mm.then_inc(S[done], 1)

                turned("b_z", "b_zT", 0)
                pe.wait_ge(S["b_xn"], it * 4 + 4)
                for g in range(HG):
                    for ty in range(4):
                        if g >= 1:
                            if ty == 0:
                                pe.wait_ge(S["b_q"], it * HG + g)
                            elif ty == 1:
                                pe.wait_ge(S["b_k"], it * HG + g)
                            else:
                                pe.wait_ge(S["b_e"], it * (2 * HG) + (2 * g + ty - 3))
                                pe.wait_ge(S["b_r"], it * (2 * HG) + (2 * g + ty - 3))
                        accumulate(PS[:, ty, 0:PT], [(w_qk[:, ty, c, 128 * g:128 * g + 128], xnT[:, c, :]) for c in range(KC)]
                                   ).then_inc(S["b_mm"], 1)
                for k in range(4):
                    if k >= 2:
                        pe.wait_ge(S["b_v"], it * 4 + (k - 1))
                    accumulate(PS[0:QC, 4 + k % 2, 0:2 * D],
                               [(xnT[:, c, QC * k:QC * k + QC], w_v[:, c, :]) for c in range(KC)]
                               + [(ones[:, 0:QC], row("v_b", 2 * D))]).then_inc(S["b_vmm"], 1)
                pe.wait_ge(S["b_q"], it * HG + HG)
                pe.wait_ge(S["b_k"], it * HG + HG)
                pe.wait_ge(S["b_e"], it * (2 * HG) + 2 * HG)
                pe.wait_ge(S["b_phi"], it * (2 * HG) + 2 * HG)
                pe.wait_ge(S["b_v"], it * 4 + 4)

                def scores(u):
                    bb, h = divmod(u, NH)
                    r, g = h % 4, h // 4
                    hr = slice(32 * r, 32 * r + DH)
                    if u >= 4:
                        pe.wait_ge(S["b_cp"], it * (2 * NH) + (u - 3))
                    for q in range(2):
                        at = L * bb + QC * q
                        mm = pe.matmul(PS[0:QC, r, L * q:L * q + L], qk[hr, 0, g, at:at + QC], qk[hr, 1, g, L * bb:L * bb + L],
                                       start=True, stop=True)
                    mm.then_inc(S["b_s"], 1)
                    if h >= 1:
                        pe.wait_ge(S["b_lin"], it * (2 * NH) + u)
                    elif bb == 1:
                        pe.wait_ge(S["b_so"], it * 2 + 1)
                    for k in range(2):
                        at = L * bb + QC * k
                        mm = pe.matmul(PS[0:QC, 5, L * k:L * k + L - QC * k], qk[hr, 3, g, at:at + QC],
                                       qk[hr, 2, g, at:L * bb + L], start=True, stop=True)
                    mm.then_inc(S["b_att"], 1)

                def turn(u):
                    pe.wait_ge(S["b_ex"], it * (2 * NH) + (u + 1))
                    if u % NH >= 1:
                        pe.wait_ge(S["b_ptc"], it * (2 * NH) + u)
                    elif u:
                        pe.wait_ge(S["b_ao"], it * 2 + 1)
                    for k in range(2):
                        for q in range(2):
                            mm = pe.transpose(PS[0:QC, 4, L * k + QC * q:L * k + QC * q + QC],
                                              pb[:, u % 2, q, QC * k:QC * k + QC], ident[0:QC, 0:QC])
                    mm.then_inc(S["b_pT"], 1)

                def values(u):
                    bb, h = divmod(u, NH)
                    pe.wait_ge(S["b_ptc"], it * (2 * NH) + (u + 1))
                    pe.wait_ge(S["b_lin"], it * (2 * NH) + (u + 1))
                    if h == 0 and bb == 1:
                        pe.wait_ge(S["b_on"], it * 2 + 1)
                    for q in range(2):
                        accumulate(PS[0:QC, 6 + q, HA * h:HA * h + HA],
                                   [(pts[:, u % 2, L * k + QC * q:L * k + QC * q + QC], va[:, 2 * bb + k, 0, h, :]) for k in range(2)])
                        at = HA * (NH + h)
                        mm = accumulate(PS[0:QC, 6 + q, at:at + HA],
                                        [(lin[:, u % 2, L * k + QC * (q - k):L * k + QC * (q - k) + QC], va[:, 2 * bb + k, 1, h, :])
                                         for k in range(q + 1)])
                    mm.then_inc(S["b_o"], 1)

                for bb in range(2):
                    u0 = NH * bb
                    scores(u0)
                    for u in range(u0, u0 + NH):
                        if u + 1 < u0 + NH:
                            scores(u + 1)
                        turn(u)
                        if u > u0:
                            values(u - 1)
                    values(u0 + NH - 1)
                    pe.wait_ge(S["b_on"], it * 2 + (bb + 1))
                    for ty in range(2):
                        for c in range(KC):
                            for q in range(2):
                                mm = pe.transpose(PS[0:DC, 4 + ty, L * c + QC * q:L * c + QC * q + QC],
                                                  oN[:, q, NH * ty + 6 * c:NH * ty + 6 * c + 6, :].rearrange("p h e -> p (h e)"),
                                                  ident[0:QC, 0:QC])
                    mm.then_inc(S["b_oT"], 1)
                tiles = [slice(128 * t, 128 * t + 128) for t in range(TP)]
                pe.wait_ge(S["b_so"], it * 2 + 2)
                for t in range(TP):
                    accumulate(PS[:, t, 0:D], [(soT[:, c, tiles[t]], w_sout[:, c, :]) for c in range(KC)]
                               + [(ones[:, 0:128], row("ssm_out_b"))]).then_inc(S["c_so"], 1)
                pe.wait_ge(S["b_ao"], it * 2 + 2)
                for c in range(KC):
                    accumulate(PS[0:DC, 6 + c, 0:PT], [(w_aproj[:, k, DC * c:DC * c + DC], aoT[:, k, :]) for k in range(KC)]
                               ).then_inc(S["c_pj"], 1)
                turned("c_z1", "c_z1T", 4)
                pe.wait_ge(S["c_u"], it * KC + KC)
                for t in range(TP):
                    accumulate(PS[:, t, 0:D], [(uT[:, c, tiles[t]], w_out[:, c, :]) for c in range(KC)]
                               + [(ones[:, 0:128], row("out_b"))]).then_inc(S["c_mm"], 1)
                turned("c_z2", "c_z2T", 4)
                pe.wait_ge(S["c_m"], it * KC + KC)
                for m in range(FM):
                    if m >= 4:
                        pe.wait_ge(S["c_h"], it * FM + (m - 3))
                    accumulate(PS[:, m % 4, 0:PT], [(w_m1[:, c, 128 * m:128 * m + 128], mT[:, c, :]) for c in range(KC)]
                               ).then_inc(S["c_ff1"], 1)
                pe.wait_ge(S["c_h"], it * FM + FM)
                for t in range(TP):
                    accumulate(PS[:, 4 + t, 0:D], [(hT[:, m, tiles[t]], w_m2[:, m, :]) for m in range(FM)]
                               + [(ones[:, 0:128], row("mlp_b2"))]).then_inc(S["c_ff2"], 1)
                turned("c_x3", "c_x3T", 0)
                pe.wait_ge(S["c_x3s"], it * KC + KC)
                for t in range(TP):
                    mm = accumulate(PS[:, 2, E_R * t:E_R * t + E_R], [(x3s[:, c, tiles[t]], w_gate[:, c, :]) for c in range(KC)])
                mm.then_inc(S["c_lg"], 1)

            pe.wait_ge(ld_moe, 16 * (3 + 3 * E_S))
            pe.wait_ge(S["d_m"], 1)
            for k, w in enumerate((earlier, ones_sq)):
                pe.matmul(PS[:, 4 + k, 0:NT * E_R], w[:, :], mask[:, :, :].rearrange("p t e -> p (t e)"), start=True, stop=True
                          ).then_inc(S["d_cnt"], 1)
            pe.wait_ge(S["d_slot"], 1)

            def shared(e):
                with pe.Fori(0, 3) as s:
                    x = x3T[:, :, bass.ds(s * 512, 512)]
                    for m in range(FM):
                        n = e * 3 * FM + m
                        pe.wait_ge(S["e_gu"], s * FM + (n + 1))
                        for k in range(2):
                            mm = accumulate(PS[:, 2 * k + m % 2, :],
                                            [(w_sgu[:, e, k, c, 128 * m:128 * m + 128], x[:, c, :]) for c in range(KC)])
                        mm.then_inc(S["e_up"], 1)
                    pe.wait_ge(S["e_gu"], s * FM + ((e * 3 + 1) * FM + 2))
                    for t in range(4):
                        pe.wait_ge(S["e_acc"], s * 4 + (12 * e + t + 1))
                        accumulate(PS[:, 4 + t, 0:D], [(gu[:, m, 128 * t:128 * t + 128], w_sdn[:, e, m, :]) for m in range(FM)]
                                   ).then_inc(S["e_dn"], 1)

            shared(0)
            pe.wait_ge(S["e_acc"], 4 + NT)
            pe.sem_inc(S["r_y"], 2)

            def turn_tokens(n, j):
                pe.wait_ge(S[f"r_x{j}"], n * 16 + 16)
                for c in range(KC):
                    mm = pe.transpose(PS[0:DC, 6 + j, 128 * c:128 * c + 128], xs[:, j, DC * c:DC * c + DC], ident[:, :])
                mm.then_inc(S["r_xT"], 1)

            def down(i, n, j):
                pe.wait_ge(S["r_h"], i + 1)
                pe.wait_ge(S[f"r_d{j}"], n * 16 + 16)
                pe.wait_ge(S["r_ye"], i + 1)
                accumulate(PS[:, 4 + j, 0:D], [(rh[:, j, 128 * m:128 * m + 128], w_rdn[:, j, m, :]) for m in range(FM)]
                           ).then_inc(S["r_y"], 1)

            turn_tokens(0, 0)

            def up(i, n, j):
                static = isinstance(i, int)
                pe.wait_ge(S["r_xe"], i + 1)
                pe.wait_ge(S[f"r_w{j}"], n * 32 + 32)
                for k, (done, read) in enumerate((("r_g", "r_sg"), ("r_u", "r_h"))):
                    if not static or i >= 1:
                        pe.wait_ge(S[read], i)
                    for m in range(FM):
                        mm = accumulate(PS[:, 2 * k + m // 4, 128 * (m % 4):128 * (m % 4) + 128],
                                        [(w_rgu[:, j, k, c, 128 * m:128 * m + 128], xt[:, j, c, :]) for c in range(KC)])
                    mm.then_inc(S[done], 1)
                if not static or i + 1 < RT:
                    turn_tokens(n + j, 1 - j)
                if not static or i >= 1:
                    down(i - 1, n - 1 + j, 1 - j)

            in_order(up)(pe, 1, 2)
            down(RT - 1, (RT - 1) // 2, (RT - 1) % 2)
            shared(1)


LINKS_PER_PAIR = 64


def layout(i):
    f = np.float32

    def chunks(w, p):
        return np.ascontiguousarray(w.reshape(-1, p, w.shape[-1]).transpose(1, 0, 2))

    def spread(w):
        o = np.zeros(w.shape[:-1] + (NH, 32), f)
        o[..., :DH] = w.reshape(w.shape[:-1] + (NH, DH))
        return o.reshape(w.shape[:-1] + (NH * 32,))

    def vec(v, p):
        o = np.zeros((128, v.size // p), f)
        o[:p] = v.reshape(-1, p).T
        return o

    a = {}
    x = i["x"].reshape(B, 3, 8, 16, 8, 16).transpose(1, 3, 5, 0, 2, 4).reshape(FF, NI)
    a["patches"] = chunks(x, 128)
    a["w_patch"] = chunks(i["L0_tok_patch_w"].reshape(D, FF).T, 128)
    tqkv, tb = i["L0_tok_qkv_w"], i["L0_tok_qkv_b"]
    a["w_tff1"] = chunks(i["L0_tok_ff1_w"], DC)
    a["w_tff2"] = chunks(i["L0_tok_ff2_w"], 128)
    a["w_tq"] = chunks(spread(tqkv[:, 0:D]), DC)
    a["w_tk"] = chunks(spread(tqkv[:, D:2 * D]), DC)
    a["w_tv"] = chunks(tqkv[:, 2 * D:], DC)
    a["w_tproj"] = chunks(i["L0_tok_proj_w"], DC)
    a["w_txt"] = np.ascontiguousarray(i["L0_txt_proj_w"].T)
    a["gam_txt"] = np.ascontiguousarray(np.broadcast_to(i["L0_txt_ln_gamma"], (128, D)))
    a["bet_txt"] = np.ascontiguousarray(np.broadcast_to(i["L0_txt_ln_beta"], (128, D)))
    w1, b1 = i["L0_attn_attn_qkv_w"], i["L0_attn_attn_qkv_b"]
    w2, b2 = i["L0_attn_ssm_qkv_w"], i["L0_attn_ssm_qkv_b"]
    a["w_qk"] = np.ascontiguousarray(np.stack([chunks(spread(w[:, k * D:k * D + D]), DC) for w in (w1, w2) for k in (0, 1)], 1))
    a["w_v"] = chunks(np.concatenate([w1[:, 2 * D:], w2[:, 2 * D:]], 1), DC)
    a["w_aproj"] = chunks(i["L0_attn_attn_proj_w"], DC)
    a["w_sout"] = chunks(i["L0_attn_ssm_out_w"], DC)
    a["w_out"] = chunks(i["L0_attn_out_w"], DC)
    a["w_m1"] = chunks(i["L0_attn_mlp_w1"], DC)
    a["w_m2"] = chunks(i["L0_attn_mlp_w2"], 128)
    a["w_gate"] = chunks(i["L0_ffn_gate_w"].T, DC)
    v = {"tok_ln_g": (i["L0_tok_ln_g"], DC), "tok_ln_b": (i["L0_tok_ln_b"], DC), "tok_ff1_b": (i["L0_tok_ff1_b"], 128),
         "tok_ff2_b": (i["L0_tok_ff2_b"], DC), "tok_q_b": (spread(tb[0:D]), 128), "tok_k_b": (spread(tb[D:2 * D]), 128),
         "tok_proj_b": (i["L0_tok_proj_b"], DC), "ln1_g": (i["L0_attn_ln1_g"], DC), "ln1_b": (i["L0_attn_ln1_b"], DC),
         "q_b": (spread(b1[0:D]), 128), "k_b": (spread(b1[D:2 * D]), 128), "q2_b": (spread(b2[0:D]), 128),
         "k2_b": (spread(b2[D:2 * D]), 128), "attn_proj_b": (i["L0_attn_attn_proj_b"], DC),
         "ssm_ln_g": (i["L0_attn_ssm_ln_g"], DC), "ssm_ln_b": (i["L0_attn_ssm_ln_b"], DC),
         "lnm_g": (i["L0_attn_lnm_g"], DC), "lnm_b": (i["L0_attn_lnm_b"], DC), "mlp_b1": (i["L0_attn_mlp_b1"], 128)}
    a["cols"] = np.concatenate([vec(*v[n]) for n in COLS], 1)
    r = {"patch_b": i["L0_tok_patch_b"], "tok_v_b": tb[2 * D:], "tok_ff2_b": i["L0_tok_ff2_b"], "txt_proj_b": i["L0_txt_proj_b"],
         "v_b": np.concatenate([b1[2 * D:], b2[2 * D:]]), "ssm_out_b": i["L0_attn_ssm_out_b"], "out_b": i["L0_attn_out_b"],
         "mlp_b2": i["L0_attn_mlp_b2"]}
    a["rows"] = np.concatenate([r[n] for n in ROWS])[None]
    a["word_table"], a["type_table"] = i["L0_txt_word_table"], i["L0_txt_type_table"]
    a["pos_table"], a["domain_table"] = i["L0_txt_pos_table"], i["L0_txt_domain_table"]
    a["ids"] = np.ascontiguousarray(np.stack([i["x_txt"].T, i["mask_BS_i0_1"].T, i["pos_BS"].T, i["itok_BS_0_4999"].T], 1))
    for n in ("wg", "wu", "shared_wg", "shared_wu"):
        a[n] = np.ascontiguousarray(i["L0_ffn_" + n].reshape(-1, KC, DC, FF).transpose(0, 2, 1, 3))
    for n in ("wd", "shared_wd"):
        a[n] = np.ascontiguousarray(i["L0_ffn_" + n].reshape(-1, FM, 128, D).transpose(0, 2, 1, 3))
    a["ident"] = np.eye(128, dtype=f)
    a["earlier"] = np.triu(np.ones((128, 128), f), 1)
    a["steps"] = np.ascontiguousarray(np.broadcast_to(np.arange(NT, dtype=f) * f(128), (128, NT)))
    a["tile_no"] = np.arange(RT, dtype=f)[None]
    q, k = np.arange(L)[:, None], np.arange(L)[None]
    near = (k <= q) & (k > q - WINDOW)
    a["keep"] = np.ascontiguousarray(near.reshape(2, QC, L).transpose(1, 0, 2)).astype(np.int32)
    past = np.where(k.T <= q.T, f(DH ** -0.5), f(0))
    a["causal"] = np.concatenate([past[0:QC], past[QC:, QC:]], 1)
    a["rank"] = np.ascontiguousarray(np.broadcast_to(np.arange(E_R, 0, -1, dtype=f), (128, TP, E_R)))
    ang = np.arange(IMG, dtype=f)[:, None] / np.power(f(10000.0), f(2.0) * np.arange(D // 2, dtype=f)[None] / f(D))
    pe = np.zeros((IMG, D), f)
    pe[:, 0::2], pe[:, 1::2] = np.sin(ang), np.cos(ang)
    a["pe_tab"] = chunks(np.ascontiguousarray(pe.T), DC)
    return a


def kernel(**inputs):
    import concourse.bacc as bacc
    from concourse.bass_utils import run_bass_kernel_spmd

    nc = bacc.Bacc("TRN2", target_bir_lowering=False, num_devices=1)
    arrays = layout({k: np.asarray(v) for k, v in inputs.items()})
    args = {n: nc.dram_tensor(f"in_{n}", v.shape, mybir.dt.from_np(v.dtype), kind="ExternalInput").ap()
            for n, v in arrays.items()}
    out = nc.dram_tensor("out_h", (B, L, D), F32, kind="ExternalOutput").ap()
    build(nc, args, out)
    r = run_bass_kernel_spmd(nc, [{f"in_{n}": v for n, v in arrays.items()}], core_ids=[0])
    return r.results[0]["out_h"]
```

```python
import numpy as np
import concourse.bass as bass
from concourse import mybir
from contextlib import ExitStack

F32 = mybir.dt.float32
I32 = mybir.dt.int32
U32 = mybir.dt.uint32
ALU = mybir.AluOpType
ACT = mybir.ActivationFunctionType
AX = mybir.AxisListType

B = 8
IMG = 64
TXT = 128
L = IMG + TXT
D = 192
KC = 2
DC = D // KC
FF = 768
FM = FF // 128
NH, DH = 12, 16
HG = NH // 4
NI = B * IMG
IT = NI // 128
PAIRS = B // 2
PT = 2 * L
TP = PT // 128
NT = PAIRS * TP
NTOK = B * L
QC = L // 2
E_R, E_S = 16, 2
NE = E_R + E_S
TOPK = 2
RT = (TOPK * NTOK + E_R * 127) // 128
NEG = -10000.0
WINDOW = 64
SQ = 3 * QC + 1
Q0 = 2 * QC + 1
HS = 32

PROJECTIONS = ((2, 0, 3), (3, 0, 5), (2, 1, 3), (3, 1, 7), (0, 0, 6), (1, 0, 3), (0, 1, 7), (2, 2, 3), (3, 2, 7),
               (1, 1, 2), (0, 2, 3), (1, 2, 7))

COLS = {}
_c = 0
for _name, _n in [("tok_ln_g", KC), ("tok_ln_b", KC), ("tok_ff1_b", FM), ("tok_ff2_b", KC), ("tok_q_b", HG),
                  ("tok_k_b", HG), ("tok_proj_b", KC), ("ln1_g", KC), ("ln1_b", KC), ("q_b", HG), ("k_b", HG),
                  ("q2_b", HG), ("k2_b", HG), ("attn_proj_b", KC), ("ssm_ln_g", KC), ("ssm_ln_b", KC),
                  ("lnm_g", KC), ("lnm_b", KC), ("mlp_b1", FM)]:
    COLS[_name] = _c
    _c += _n
NCOL = _c
ROWS = {}
_c = 0
for _name, _n in [("patch_b", D), ("tok_v_b", D), ("tok_ff2_b", D), ("txt_proj_b", D), ("v_b", 2 * D),
                  ("ssm_out_b", D), ("out_b", D), ("mlp_b2", D)]:
    ROWS[_name] = _c
    _c += _n
NROW = _c


def build(nc, a, out):
    ctx = ExitStack()
    with ctx:
        def sb(name, shape, dt=F32):
            return ctx.enter_context(nc.sbuf_tensor(name, shape, dt))

        def sem(name):
            return ctx.enter_context(nc.semaphore(name))

        ident = sb("ident", [128, 128])
        ones = sb("ones", [1, 512])
        cols = sb("cols", [128, NCOL])
        rows = sb("rows", [1, NROW])
        keep = sb("keep", [QC, SQ], I32)
        causal = sb("causal", [QC, L + QC])
        rank = sb("rank", [128, NT, E_R])
        w_qk = sb("w_qk", [DC, 4, KC, HG * 128])
        w_v = sb("w_v", [DC, KC, 2 * D])
        FG = 4 * DH
        w_heads = sb("w_heads", [2 * FG, HG, D])
        eps_sum = sb("eps_sum", [QC, 16])
        head_rows = sb("head_rows", [128, 4])
        w_out = sb("w_out", [DC, KC, D])
        w_m1 = sb("w_m1", [DC, KC, FF])
        w_m2 = sb("w_m2", [128, FM, D])
        w_gate = sb("w_gate", [DC, KC, E_R])
        minus_half = sb("minus_half", [128, 4])
        phi_b = sb("phi_b", [128, 2 * HG])
        zeros = sb("zeros", [128, D])
        carrier = sb("carrier", [128, 1])
        carrier_p = sb("carrier_p", [128, 1])
        carrier_a = sb("carrier_a", [128, 1])

        h_sb = sb("h_sb", [128, IT + B, D])
        acc = sb("acc", [128, NT, D])
        x3T = sb("x3T", [DC, KC, NTOK])
        chosen = sb("chosen", [128, TOPK, NT, E_R])
        weight = sb("weight", [128, TOPK, NT])
        earlier = sb("earlier", [128, 128])
        ones_sq = sb("ones_sq", [128, 128])
        steps = sb("steps", [128, NT])
        tile_no = sb("tile_no", [1, RT])
        st = sb("st", [128, TP, 6])
        st_in = sb("st_in", [128, IT + B, 6])
        mv_in = sb("mv_in", [128, IT + B, 2])
        ve_in = sb("ve_in", [128, IT + B])
        rs_in = sb("rs_in", [128, IT + B])
        mv = sb("mv", [128, 4, 2])
        ve = sb("ve", [128, 4])
        rs = sb("rs", [128, 4])

        PS = ctx.enter_context(nc.psum_tensor("PS", [128, 8, 512], F32))

        ld_const = sem("ld_const")
        ld_patch = sem("ld_patch")
        ld_tok = sem("ld_tok")
        ld_txt = sem("ld_txt")
        ld_attn = sem("ld_attn")
        ld_moe = sem("ld_moe")
        ld_idx = sem("ld_idx")
        gathered = [sem(f"gathered{b}") for b in range(B)]
        set_up = sem("set_up")
        vs = sem("dve_step")
        stored = sem("stored")
        names = """patch_mm a_ve a_rs a_z a_zT a_xg a_x a_ff1 a_h a_ff2 a_y a_mm a_q a_k a_vmm a_v a_s a_sub a_exp
            a_pT a_ptc a_o a_on a_oT a_at a_pj a_x1 a_hmm h_img
            t_tp t_dT t_dc t_pm t_ve t_rs t_z t_g h_txt
            p_ve1 p_rs1 p_x p_ve2 p_rs2 p_z p_zT p_xn b_xc b_mm b_q b_k b_r b_e b_clip b_phi b_vmm b_v b_vs b_vc b_s b_att
            b_cp b_nm b_ex b_pT b_ptc b_qx b_lin b_o b_oc b_dn b_sm b_rc b_on b_oT b_ao
            c_so c_ve1 c_rs1 c_z1 c_z1T c_sl c_pj c_u c_mm c_x2 c_ve2 c_rs2 c_z2 c_z2T c_m c_ff1 c_h c_ff2 c_hx c_h2
            c_ve3 c_rs3 c_x3 c_x3T c_x3s c_lg c_ls c_ex c_cw c_x3c
            d_m d_cnt d_slot zeroed scattered
            e_up e_sg e_su e_gu e_dn e_acc
            r_w0 r_w1 r_d0 r_d1 r_x0 r_x1 r_xT r_xe r_g r_sg r_u r_h r_y r_ye r_st0 r_st1 fetched0 fetched1 fetched2""".split()
        S = {n: sem(n) for n in names}

        scr = ExitStack()

        def tb(name, shape, dt=F32):
            return scr.enter_context(nc.sbuf_tensor(name, shape, dt))

        w_patch = tb("w_patch", [128, FM, D])
        w_tff1 = tb("w_tff1", [DC, KC, FF])
        w_tff2 = tb("w_tff2", [128, FM, D])
        w_tq = tb("w_tq", [DC, KC, HG * 128])
        w_tk = tb("w_tk", [DC, KC, HG * 128])
        w_tv = tb("w_tv", [DC, KC, D])
        w_tproj = tb("w_tproj", [DC, KC, D])
        w_txt = tb("w_txt", [128, D])
        pe_tab = tb("pe_tab", [DC, KC, IMG])
        gam_txt = tb("gam_txt", [128, D])
        bet_txt = tb("bet_txt", [128, D])
        patches = tb("patches", [128, FM, NI])
        zA = tb("zA", [128, IT, D])
        xT = tb("xT", [DC, KC, NI])
        h1T = tb("h1T", [128, FM, NI])
        y1T = tb("y1T", [DC, KC, NI])
        tq = tb("tq", [128, HG, NI])
        tk = tb("tk", [128, HG, NI])
        tv = tb("tv", [IMG, B, NH, DH + 1])
        pA = tb("pA", [128, 2, NH, IMG])
        mxA = tb("mxA", [128, NH])
        ptA = tb("ptA", [IMG, NH, 128])
        rcA = tb("rcA", [128, NH])
        oA = tb("oA", [128, IT, NH, DH])
        aTA = tb("aTA", [DC, KC, NI])
        ids = tb("ids", [128, 4, B], I32)
        words = tb("words", [128, B, D])
        types = tb("types", [128, B, D])
        poss = tb("poss", [128, B, D])
        dom = tb("dom", [128, B, 128])
        domT = tb("domT", [128, 2, 128])
        zT_ = tb("z_txt", [128, 2, D])
        mvT = tb("mvT", [128, B, 2])
        veT = tb("veT", [128, B])
        rsT = tb("rsT", [128, B])
        stT = tb("stT", [128, 6])
        scr.close()
        x3 = sb("x3", [128, NT, D])
        w_sgu = sb("w_sgu", [DC, E_S, 2, KC, FF])
        w_sdn = sb("w_sdn", [128, E_S, FM, D])
        scr2 = ExitStack()

        def tb2(name, shape, dt=F32):
            return scr2.enter_context(nc.sbuf_tensor(name, shape, dt))

        z = tb2("z", [128, TP, D])
        xnT = tb2("xnT", [DC, KC, PT])
        qk = tb2("qk", [128, 4, HG, PT])
        hT = tb2("hT", [128, FM, PT])
        o_raw = hT[:, 0:2, :]
        ee = tb2("ee", [128, 2, PT])
        va = tb2("va", [QC + 1, 4, 2, NH, HS])
        qx = tb2("qx", [128, 2, 2, L])
        sm = tb2("sm", [QC, 2, SQ + 1])
        nm = tb2("nm", [QC, 2, 2])
        pb = tb2("pb", [QC, 2, SQ + 1])
        pts = tb2("pts", [QC + 1, 2, 3 * QC])
        lin = tb2("lin", [QC, 2, L + QC])
        rd = tb2("rd", [QC, 16])
        oN = tb2("oN", [QC, 16, DH])
        aoT = tb2("aoT", [2 * FG, HG, PT])
        slT = tb2("slT", [DC, KC, PT])
        uT = slT
        x2 = tb2("x2", [128, TP, D])
        hx = tb2("hx", [128, TP, D])
        mT = tb2("mT", [DC, KC, PT])
        scr2.close()
        scr3 = ExitStack()

        def tb3(name, shape, dt=F32):
            return scr3.enter_context(nc.sbuf_tensor(name, shape, dt))

        lg = tb3("lg", [128, NT, E_R])
        r1 = tb3("r1", [128, 4, NT])
        mask = tb3("mask", [128, NT, E_R])
        before = tb3("before", [128, NT, E_R])
        count = tb3("count", [128, E_R])
        beyond = tb3("beyond", [128, E_R, NT])
        tiles_of = tb3("tiles_of", [128, E_R])
        ends = tb3("ends", [128, E_R])
        ones_e = tb3("ones_e", [128, E_R])
        base = tb3("base", [128, E_R])
        at_slot = tb3("at_slot", [128, NT, E_R])
        pick = tb3("pick", [128, NT, E_R])
        slot_f = tb3("slot_f", [128, TOPK, NT])
        slot = tb3("slot", [128, TOPK, NT], I32)
        passed = tb3("passed", [1, RT, E_R])
        expert_f = tb3("expert_f", [1, RT])
        expert = tb3("expert", [1, RT], I32)
        w_rgu = tb3("w_rgu", [DC, 2, 2, KC, FF])
        w_rdn = tb3("w_rdn", [128, 2, FM, D])
        xs = tb3("xs", [128, 2, D])
        xt = tb3("xt", [DC, 2, KC, 128])
        rsg = tb3("rsg", [128, 2, FF])
        rh = tb3("rh", [128, 2, FF])
        ys = tb3("ys", [128, 2, D])
        yg = (h_sb, tb3("yg", [128, NT, D]))
        sg = tb3("sg", [128, 2, 512])
        su = rsg[:, :, 0:512]
        gu = tb3("gu", [128, FM, 512])
        scr3.close()

        def col(name, i=0, n=128):
            return cols[0:n, COLS[name] + i:COLS[name] + i + 1]

        def row(name, n=D):
            return rows[0:1, ROWS[name]:ROWS[name] + n]

        x_slots = nc.dram_tensor("x_slots", (RT * 128, D), F32, kind="Internal").ap()
        y_slots = nc.dram_tensor("y_slots", (RT * 128, D), F32, kind="Internal").ap()
        x_tiles = x_slots.rearrange("(i p) d -> i p d", p=128)
        y_tiles = y_slots.rearrange("(i p) d -> i p d", p=128)

        def in_order(tile):
            def outer(eng, first, last):
                for i in range(first):
                    tile(i, i // 2, i % 2)
                rounds = (RT - first - last) // 2
                with eng.Fori(0, rounds) as r:
                    for k in range(2):
                        i = first + k
                        tile(r * 2 + i, r + i // 2, i % 2)
                for i in range(first + 2 * rounds, RT):
                    tile(i, i // 2, i % 2)
            return outer

        block = ctx.enter_context(nc.Block())

        @block.sync
        def _(sp):
            for dst, name in ((w_patch, "w_patch"), (patches, "patches")):
                sp.dma_start(dst[:, :, :], a[name]).then_inc(ld_patch, 16)
            for dst, name in ((ident, "ident"), (cols, "cols"), (rows, "rows")):
                sp.dma_start(dst[:, :], a[name]).then_inc(ld_const, 16)
            for dst, name in ((w_txt, "w_txt"), (gam_txt, "gam_txt"), (bet_txt, "bet_txt")):
                sp.dma_start(dst[:, :], a[name]).then_inc(ld_txt, 16)
            for dst, name in ((pe_tab, "pe_tab"), (w_tff1, "w_tff1"), (w_tff2, "w_tff2"), (w_tq, "w_tq"),
                              (w_tk, "w_tk"), (w_tv, "w_tv"), (w_tproj, "w_tproj")):
                sp.dma_start(dst[:, :, :], a[name]).then_inc(ld_tok, 16)
            sp.dma_start(w_qk[:, :, :, :], a["w_qk"]).then_inc(ld_attn, 16)
            for dst, name in ((rank, "rank"), (w_v, "w_v"), (w_heads, "w_heads"),
                              (w_out, "w_out"), (w_m1, "w_m1"), (w_m2, "w_m2"), (w_gate, "w_gate")):
                sp.dma_start(dst[:, :, :], a[name]).then_inc(ld_attn, 16)
            sp.dma_start(causal[:, :], a["causal"]).then_inc(ld_attn, 16)
            for dst, name in ((keep, "keep"), (head_rows, "head_rows")):
                sp.dma_start(dst[:, :], a[name]).then_inc(ld_attn, 16)

            for dst, name in ((earlier, "earlier"), (steps, "steps"), (tile_no, "tile_no")):
                sp.dma_start(dst[:, :], a[name]).then_inc(ld_moe, 16)
            sp.wait_ge(set_up, 3)
            sp.dma_start(x_slots.rearrange("(i p) d -> p i d", p=128),
                         zeros[:, :].rearrange("p (o d) -> p o d", o=1).broadcast_to([128, RT, D])).then_inc(S["zeroed"], 16)
            sp.wait_ge(S["p_zT"], 3)
            for e in range(E_S):
                sp.dma_start(w_sgu[:, e, 0, :, :], a["shared_wg"][e]).then_inc(ld_moe, 16)
                sp.dma_start(w_sgu[:, e, 1, :, :], a["shared_wu"][e]).then_inc(ld_moe, 16)
                sp.dma_start(w_sdn[:, e, :, :], a["shared_wd"][e]).then_inc(ld_moe, 16)

            sp.wait_ge(S["d_slot"], 1)
            sp.wait_ge(S["scattered"], 16 * TOPK * NT)

            def load(i, n, j):
                static = isinstance(i, int)
                if not static or i >= 2:
                    sp.wait_ge(S["r_u"], i - 1)
                at = slice(i, i + 1) if static else bass.ds(i, 1)
                e = sp.value_load(expert[0:1, at], min_val=0, max_val=E_R - 1)
                for k, name in enumerate(("wg", "wu")):
                    sp.dma_start(w_rgu[:, j, k, :, :], a[name][bass.ds(e, 1)].rearrange("o p c n -> p (o c) n")).then_inc(S[f"r_w{j}"], 16)
                if not static or i >= 2:
                    sp.wait_ge(S["r_xT"], i - 1)
                sp.dma_start(xs[:, j:j + 1, :], x_tiles[at].rearrange("o p d -> p o d")).then_inc(S[f"r_x{j}"], 16)

            in_order(load)(sp, 2, 1)

            for s in range(3):
                for t in range(4 * s, 4 * s + 4):
                    sp.wait_ge(S["e_acc"], 4 + NT + t + 1)
                    p, t = divmod(t, TP)
                    if t == 0:
                        for k in range(2):
                            sp.dma_start(out[2 * p + k, 0:IMG, :], acc[IMG * k:IMG * k + IMG, TP * p, :]).then_inc(stored, 16)
                    else:
                        sp.dma_start(out[2 * p + t - 1, IMG:L, :], acc[:, TP * p + t, :]).then_inc(stored, 16)
            sp.wait_ge(stored, 16 * 2 * B)

        @block.gpsimd
        def _(pool):
            pool.memset(ones[:, :], 1.0).then_inc(set_up, 1)
            pool.memset(minus_half[:, :], -0.5).then_inc(set_up, 1)
            pool.wait_ge(set_up, 2)
            pool.memset(zeros[:, :], 0.0)
            pool.memset(ones_sq[:, :], 1.0)
            pool.memset(tv[:, :, :, DH:DH + 1], 1.0).then_inc(set_up, 1)

            pool.dma_start(ids[:, :, :], a["ids"]).then_inc(ld_idx, 16)
            pool.wait_ge(ld_idx, 16)
            for b in range(B):
                for j, (dst, table) in enumerate(((words, "word_table"), (types, "type_table"), (poss, "pos_table"),
                                                  (dom, "domain_table"))):
                    pool.indirect_dma_start(dst[:, b, :], None, a[table],
                                            bass.IndirectOffsetOnAxis(ap=ids[:, j, b:b + 1].bitcast(U32), axis=0)
                                            ).then_inc(gathered[b], 16)
                if b == 3:
                    for i in range(IT):
                        pool.wait_ge(S["a_ve"], i + 1)
                        pool.tensor_tensor(rs[:, i:i + 1], ve[:, i:i + 1], minus_half[:, 0:1], ALU.pow).then_inc(S["a_rs"], 1)
            for b in range(B):
                pool.wait_ge(gathered[b], 64)
                pool.tensor_tensor(types[:, b, :], types[:, b, :], poss[:, b, :], ALU.add).then_inc(S["t_tp"], 1)
            pool.wait_ge(ld_txt, 48)

            def text_gain(b):
                pool.wait_ge(S["t_z"], b + 1)
                pool.tensor_tensor(zT_[:, b % 2, :], zT_[:, b % 2, :], gam_txt[:, :], ALU.mult).then_inc(S["t_g"], 1)
                pool.wait_ge(S["t_g"], b + 1)
                pool.tensor_tensor(h_sb[:, IT + b, :], zT_[:, b % 2, :], bet_txt[:, :], ALU.add).then_inc(S["h_txt"], 1)

            for b in range(B):
                pool.wait_ge(S["t_ve"], b + 1)
                pool.tensor_tensor(rsT[:, b:b + 1], veT[:, b:b + 1], minus_half[:, 0:1], ALU.pow).then_inc(S["t_rs"], 1)
                if b >= 1:
                    text_gain(b - 1)
            text_gain(B - 1)
            for n, at in enumerate((slice(IT, IT + B), slice(0, IT))):
                for v, r in (("p_ve1", "p_rs1"), ("p_ve2", "p_rs2")):
                    pool.wait_ge(S[v], n + 1)
                    pool.tensor_tensor(rs_in[:, at], ve_in[:, at], minus_half[:, 0:1].broadcast_to([128, at.stop - at.start]),
                                       ALU.pow).then_inc(S[r], 1)
            pool.wait_ge(S["h_img"], IT)
            pool.memset(va[:, :, :, :, DH:DH + 1], 1.0)
            pool.memset(va[:, :, :, :, DH + 1:HS], 0.0).then_inc(set_up, 1)
            pool.memset(sm[:, :, :], NEG).then_inc(set_up, 1)
            pool.memset(pb[:, :, Q0 - 1:Q0], 0.0)
            for y, eps in enumerate((0.0, 1e-4)):
                ins = pool.memset(eps_sum[:, :].rearrange("p (c y r) -> p c y r", c=2, y=2)[:, :, y, :], eps)
            ins.then_inc(set_up, 1)
            pool.wait_ge(ld_attn, 11 * 16)

            def deviations(v, r, n):
                pool.wait_ge(S[v], n + 1)
                pool.tensor_tensor(rs[:, 0:TP], ve[:, 0:TP], minus_half[:, 0:TP], ALU.pow).then_inc(S[r], 1)

            def phi(n, g):
                for ty in (2, 3):
                    at = n * (2 * HG) + (2 * g + ty - 1)
                    pool.wait_ge(S["b_e"], at)
                    pool.tensor_tensor(carrier_p[:, :], minus_half[:, 0:1], minus_half[:, 1:2], ALU.add)
                    pool.tensor_scalar(ee[:, ty - 2, :], ee[:, ty - 2, :], 1.0, None, ALU.min).then_inc(S["b_clip"], 1)
                    pool.wait_ge(S["b_clip"], at)
                    pool.wait_ge(S["b_r"], at)
                    pool.tensor_tensor(qk[:, ty, g, :], qk[:, ty, g, :], ee[:, ty - 2, :], ALU.add).then_inc(S["b_phi"], 1)

            for g in range(HG):
                phi(0, g)
            pool.sem_inc(S["c_x3c"], 1)
            def pair(it, last):
                pool.wait_ge(S["b_q"], it * HG + HG)
                pool.wait_ge(S["b_phi"], it * (2 * HG) + 2 * HG)

                for u in range(2 * NH):
                    bb, h = divmod(u, NH)
                    if u >= 2:
                        pool.wait_ge(S["b_att"], it * (2 * NH) + (u - 1))
                    pool.tensor_tensor(qx[:, u % 2, :, :], qk[:, 0:3:2, h // 4, L * bb:L * bb + L],
                                       head_rows[:, h % 4:h % 4 + 1].rearrange("p (a b) -> p a b", a=1).broadcast_to([128, 2, L]),
                                       ALU.mult).then_inc(S["b_qx"], 1)
                    if u == 4 and not last:
                        pool.wait_ge(S["b_vmm"], it * 4 + 4)
                        pool.tensor_copy(xnT[:, :, :], x3T[:, :, bass.ds(it * PT + PT, PT)]).then_inc(S["b_xc"], 1)
                deviations("c_ve1", "c_rs1", it)
                if not last:
                    phi(it + 1, 0)
                deviations("c_ve2", "c_rs2", it)
                pool.tensor_tensor(hx[:, 0:1, :], h_sb[:, bass.ds(it, 1), :], x2[:, 0:1, :], ALU.add)
                pool.tensor_tensor(hx[:, 1:TP, :], h_sb[:, bass.ds(it * 2 + IT, 2), :], x2[:, 1:TP, :], ALU.add).then_inc(S["c_hx"], 1)
                if not last:
                    phi(it + 1, 1)
                deviations("c_ve3", "c_rs3", it)
                pool.wait_ge(S["c_x3"], it * TP + TP)
                pool.tensor_copy(x3[:, bass.ds(it * TP, TP), :], z[:, :, :]).then_inc(S["c_x3c"], 1)
                if not last:
                    phi(it + 1, 2)

            with pool.Fori(0, PAIRS - 1) as it:
                pair(it, False)
            pair(PAIRS - 1, True)

            for m in range(FM):
                pool.wait_ge(S["e_sg"], m + 1)
                pool.wait_ge(S["e_su"], m + 1)
                pool.tensor_tensor(gu[:, m, :], sg[:, m % 2, :], su[:, m % 2, :], ALU.mult).then_inc(S["e_gu"], 1)

            pool.wait_ge(S["d_slot"], 1)
            pool.wait_ge(S["zeroed"], 16)
            for t in range(NT):
                for k in range(TOPK):
                    pool.indirect_dma_start(x_slots, bass.IndirectOffsetOnAxis(ap=slot[:, k, t:t + 1].bitcast(U32), axis=0),
                                            x3[:, t, :], None).then_inc(S["scattered"], 16)

            def store(i, n, j):
                pool.wait_ge(S["r_ye"], i + 3)
                at = slice(i, i + 1) if isinstance(i, int) else bass.ds(i, 1)
                pool.dma_start(y_tiles[at].rearrange("o p d -> p o d"), ys[:, j:j + 1, :]).then_inc(S[f"r_st{j}"], 16)

            in_order(store)(pool, 1, 0)
            pool.wait_ge(S["r_st0"], 16 * ((RT + 1) // 2))
            pool.wait_ge(S["r_st1"], 16 * (RT // 2))
            for t in range(NT):
                for k in range(TOPK):
                    pool.indirect_dma_start(yg[k][:, t, :], None, y_slots,
                                            bass.IndirectOffsetOnAxis(ap=slot[:, k, t:t + 1].bitcast(U32), axis=0)
                                            ).then_inc(S[f"fetched{t // 4}"], 16)

        @block.scalar
        def _(act):
            act.wait_ge(ld_const, 48)
            act.wait_ge(S["a_zT"], IT)
            for c in range(KC):
                act.activation(xT[:, c, :], PS[0:DC, 4 + c, :], ACT.Identity, bias=col("tok_ln_b", c, DC),
                               scale=col("tok_ln_g", c, DC)).then_inc(S["a_xg"], 1)

            def domain_out(b):
                act.wait_ge(S["t_dT"], b + 1)
                if b >= 2:
                    act.wait_ge(S["t_pm"], b - 1)
                act.activation(domT[:, b % 2, :], PS[:, 6, 0:128], ACT.Copy).then_inc(S["t_dc"], 1)

            def gelu_tanh(base):
                for m in range(FM):
                    bank = m % 4 if base == 0 else 2 + m % 4
                    act.wait_ge(S["a_ff1"], base + m + 1)
                    act.activation(h1T[:, m, :], PS[:, bank, :], ACT.Gelu_apprx_tanh, bias=col("tok_ff1_b", m)
                                   ).then_inc(S["a_h"], 1)
                    if base == 0 and m >= 2:
                        domain_out(m - 2)

            gelu_tanh(0)
            domain_out(4)
            domain_out(5)
            for g in range(HG):
                if g <= 1:
                    domain_out(FM + g)
                j = 2 * g + 1
                act.wait_ge(S["a_mm"], j + 1)
                act.activation(tk[:, g, :], PS[:, j % 4, :], ACT.Identity, bias=col("tok_k_b", g)).then_inc(S["a_k"], 1)
            for w in range(B):
                act.wait_ge(S["a_vmm"], w + 1)
                act.activation(tv[:, w, :, 0:DH], PS[0:IMG, 6 + w % 2, 0:D].rearrange("p (h e) -> p h e", e=DH),
                               ACT.Copy).then_inc(S["a_v"], 1)

            def outputs_out(i):
                act.wait_ge(S["a_oT"], i + 1)
                act.activation(aTA[:, :, 128 * i:128 * i + 128], PS[0:DC, 7, 256:512].rearrange("p (c t) -> p c t", c=KC),
                               ACT.Copy).then_inc(S["a_at"], 1)

            for i in range(IT):
                act.wait_ge(S["a_sub"], i + 1)
                act.activation(pA[:, i % 2, :, :], pA[:, i % 2, :, :], ACT.Exp).then_inc(S["a_exp"], 1)
                act.wait_ge(S["a_pT"], i + 1)
                if i >= 1:
                    act.wait_ge(S["a_o"], i)
                act.activation(ptA[:, :, :].rearrange("p h q -> p (h q)"),
                               PS[0:IMG, 4:7, :].rearrange("p a b -> p (a b)"), ACT.Copy).then_inc(S["a_ptc"], 1)
                if i >= 1:
                    outputs_out(i - 1)
            outputs_out(IT - 1)

            def normalised_out(n, src, lo, hi):
                act.wait_ge(S["p_zT"], n + 1)
                first, count = src
                for c in range(KC):
                    seqs = x3T[:, c, 0:NTOK].rearrange("p (b s) -> p b s", s=L)
                    ins = act.activation(seqs[:, first:first + count, lo:hi], PS[0:DC, c, :].rearrange("p (b s) -> p b s", b=count),
                                         ACT.Identity, bias=col("ln1_b", c, DC), scale=col("ln1_g", c, DC))
                ins.then_inc(S["p_xn"], 1)

            normalised_out(0, (0, 4), IMG, L)
            gelu_tanh(FM)
            normalised_out(1, (4, 4), IMG, L)
            for i in range(IT):
                act.wait_ge(S["a_hmm"], i + 1)
                act.activation(h_sb[:, i, :], PS[:, 6 + i % 2, 0:D], ACT.Copy).then_inc(S["h_img"], 1)

            normalised_out(2, (0, B), 0, IMG)

            def projection_out(n, j):
                ty, g, bank = PROJECTIONS[j]
                if ty == 1:
                    act.wait_ge(S["b_mm"], n * len(PROJECTIONS) + (j + 1))
                    act.activation(qk[:, 1, g, :], PS[:, bank, 0:PT], ACT.Identity, bias=col("k_b", g)).then_inc(S["b_k"], 1)
                elif ty >= 2:
                    act.wait_ge(S["b_r"], n * (2 * HG) + (2 * g + ty - 1))
                    if g >= 1:
                        act.wait_ge(S["b_phi"], n * (2 * HG) + (2 * (g - 1) + ty - 1))
                    act.activation(ee[:, ty - 2, :], PS[:, bank, 0:PT], ACT.Exp, bias=col(("q2_b", "k2_b")[ty - 2], g)
                                   ).then_inc(S["b_e"], 1)

            def values_out(n):
                for k in range(4):
                    act.wait_ge(S["b_vmm"], n * 4 + (k + 1))
                    act.activation(va[0:QC, k, :, :, 0:DH].rearrange("p t h e -> p (t h) e"),
                                   PS[0:QC, 4 + k % 2, 0:2 * D].rearrange("p (h e) -> p h e", e=DH), ACT.Copy
                                   ).then_inc(S["b_v"], 1)
                for bb in range(2):
                    act.wait_ge(S["b_vs"], n * 2 + (bb + 1))
                    act.activation(va[QC:QC + 1, 2 * bb, 0, :, :].rearrange("p h e -> p (h e)"), PS[QC:QC + 1, 6 + bb, 0:NH * HS],
                                   ACT.Copy).then_inc(S["b_vc"], 1)

            act.wait_ge(set_up, 6)
            for j in range(len(PROJECTIONS)):
                projection_out(0, j)
            values_out(0)
            def pair(it, last):

                def weights_out(u):
                    act.wait_ge(S["b_pT"], it * (2 * NH) + (u + 1))
                    if u >= 2:
                        act.wait_ge(S["b_o"], it * (2 * NH) + (u - 1))
                    act.activation(pts[:, u % 2, :], PS[0:QC + 1, 3, 0:3 * QC], ACT.Copy).then_inc(S["b_ptc"], 1)

                def group_out(n):
                    act.wait_ge(S["b_o"], it * (2 * NH) + (4 * n + 4))
                    if n >= 2:
                        act.wait_ge(S["b_dn"], it * (2 * HG) + (n - 1))
                    act.activation(o_raw[:, n % 2, :], PS[:, 5 + n % HG, 0:2 * L], ACT.Copy).then_inc(S["b_oc"], 1)

                def outputs_out(n):
                    bb, g = divmod(n, HG)
                    act.wait_ge(S["b_oT"], it * (2 * HG) + (n + 1))
                    act.activation(aoT[:, g, IMG * bb:IMG * bb + IMG], PS[:, 4, 0:IMG], ACT.Copy)
                    act.activation(aoT[:, g, 128 + TXT * bb:128 + TXT * bb + TXT], PS[:, 4, IMG:L], ACT.Copy
                                   ).then_inc(S["b_ao"], 1)

                for u in range(2 * NH):
                    act.wait_ge(S["b_nm"], it * (2 * NH) + (u + 1))
                    if u >= 2:
                        act.wait_ge(S["b_pT"], it * (2 * NH) + (u - 1))
                    for q, at in enumerate((slice(Q0, SQ + 1), slice(0, L))):
                        e = act.activation(pb[:, u % 2, at], sm[:, u % 2, at], ACT.Exp, bias=nm[:, u % 2, q:q + 1])
                    e.then_inc(S["b_ex"], 1)
                    if u >= 1:
                        weights_out(u - 1)
                    if u >= 5 and u % 4 == 1:
                        group_out(u // 4 - 1)
                    if u >= 10 and u % 4 == 2:
                        outputs_out(u // 4 - 2)
                weights_out(2 * NH - 1)
                group_out(2 * HG - 1)
                outputs_out(2 * HG - 2)
                if not last:
                    projection_out(it + 1, 0)
                outputs_out(2 * HG - 1)
                if not last:
                    projection_out(it + 1, 1)

                def gain(done, ready, dst, g_name, b_name, bank):
                    act.wait_ge(S[ready], it * TP + TP)
                    for c in range(KC):
                        act.activation(dst[:, c, :], PS[0:DC, bank + c, 0:PT], ACT.Identity, bias=col(b_name, c, DC),
                                       scale=col(g_name, c, DC)).then_inc(S[done], 1)

                gain("c_sl", "c_z1T", slT, "ssm_ln_g", "ssm_ln_b", 4)
                if not last:
                    projection_out(it + 1, 2)
                gain("c_m", "c_z2T", mT, "lnm_g", "lnm_b", 4)
                for j in () if last else range(3, 7):
                    projection_out(it + 1, j)
                act.activation(carrier_a[:, :], minus_half[:, 0:1], ACT.Gelu)
                for m in range(FM):
                    act.wait_ge(S["c_ff1"], it * FM + (m + 1))
                    act.activation(hT[:, m, :], PS[:, m % 3, 0:PT], ACT.Gelu, bias=col("mlp_b1", m)).then_inc(S["c_h"], 1)
                act.activation(carrier_a[:, :], minus_half[:, 0:1], ACT.Exp)
                act.wait_ge(S["c_x3T"], it * TP + TP)
                act.activation(x3T[:, :, bass.ds(it * PT, PT)], PS[0:DC, 0:KC, 0:PT], ACT.Copy).then_inc(S["c_x3s"], 1)
                for j in () if last else range(7, len(PROJECTIONS)):
                    projection_out(it + 1, j)
                if not last:
                    values_out(it + 1)

            with act.Fori(0, PAIRS - 1) as it:
                pair(it, False)
            pair(PAIRS - 1, True)

            act.wait_ge(S["c_ls"], 1)
            act.activation(lg[:, :, :], lg[:, :, :], ACT.Exp).then_inc(S["c_ex"], 1)

            def shared(e, first):
                with act.Fori(0, 3 - first) as s:
                    for m in range(FM):
                        n = (e * 3 + first) * FM + m
                        act.wait_ge(S["e_up"], s * FM + (n + 1))
                        act.wait_ge(S["e_gu"], s * FM + (n + 1))
                        act.activation(sg[:, m % 2, :], PS[:, m % 2, :], ACT.Silu).then_inc(S["e_sg"], 1)

            for m in range(FM):
                act.wait_ge(S["e_up"], m + 1)
                act.wait_ge(S["e_gu"], m + 1)
                act.activation(sg[:, m % 2, :], PS[:, m % 2, :], ACT.Silu).then_inc(S["e_sg"], 1)
                act.activation(su[:, m % 2, :], PS[:, 2 + m % 2, :], ACT.Copy).then_inc(S["e_su"], 1)
            shared(0, 1)
            act.sem_inc(S["r_ye"], 2)

            def tokens_out(i, j):
                act.wait_ge(S["r_xT"], i + 1)
                act.activation(xt[:, j, :, :], PS[0:DC, 6 + j, 0:KC * 128].rearrange("p (c t) -> p c t", c=KC), ACT.Copy
                               ).then_inc(S["r_xe"], 1)

            def results_out(i, n, j):
                act.wait_ge(S["r_y"], i + 3)
                if not isinstance(i, int) or i >= 2:
                    act.wait_ge(S[f"r_st{j}"], n * 16)
                act.activation(ys[:, j, :], PS[:, 4 + j, 0:D], ACT.Copy).then_inc(S["r_ye"], 1)

            tokens_out(0, 0)

            def gate(i, n, j):
                static = isinstance(i, int)
                e = act.value_load(expert[0:1, slice(i, i + 1) if static else bass.ds(i, 1)], min_val=0, max_val=E_R - 1)
                act.wait_ge(S["r_g"], i + 1)
                act.activation(rsg[:, j, :], PS[:, 0:2, :].rearrange("p a b -> p (a b)")[:, 0:FF], ACT.Silu).then_inc(S["r_sg"], 1)
                act.wait_ge(S["r_y"], i + 1)
                act.dma_start(w_rdn[:, j, :, :], a["wd"][bass.ds(e, 1)].rearrange("o p c n -> p (o c) n")).then_inc(S[f"r_d{j}"], 16)
                if not static or i + 1 < RT:
                    tokens_out(i + 1, 1 - j)
                if not static or i >= 1:
                    results_out(i - 1, n - 1 + j, 1 - j)

            in_order(gate)(act, 3, 2)
            results_out(RT - 1, (RT - 1) // 2, (RT - 1) % 2)
            shared(1, 0)

        @block.vector
        def _(dve):
            links = [0, 0]

            def carry():
                dve.memset(carrier[:, :], 0.0)

            def link(ins, alone=False):
                links[0] += 1
                ins.then_inc(vs, 1)
                dve.wait_ge(vs, links[1] + links[0])
                if alone:
                    carry()

            def statistics(src, k, eps, s, m, v):
                link(dve.bn_stats(s, src), True)
                link(dve.bn_aggr(m[:, k, :], s))
                return dve.tensor_scalar(v[:, k:k + 1], m[:, k, 1:2], eps, None, ALU.add)

            dve.wait_ge(ld_const, 48)
            dve.tensor_scalar(phi_b[:, :], cols[:, COLS["q2_b"]:COLS["q2_b"] + 2 * HG], 1e-4, None, ALU.add)
            for i in range(IT):
                dve.wait_ge(S["patch_mm"], i + 1)
                statistics(PS[:, i, 0:D], i, 1e-5, st[:, 0, :], mv, ve).then_inc(S["a_ve"], 1)
            for i in range(IT):
                dve.wait_ge(S["a_rs"], i + 1)
                dve.tensor_scalar(zA[:, i, :], PS[:, i, 0:D], mv[:, i, 0:1], rs[:, i:i + 1], ALU.subtract, ALU.mult
                                  ).then_inc(S["a_z"], 1)
            dve.wait_ge(ld_tok, 7 * 16)
            for c in range(KC):
                dve.wait_ge(S["a_xg"], c + 1)
                v = xT[:, c, :].rearrange("p (b s) -> p b s", s=IMG)
                dve.tensor_tensor(v, v, pe_tab[:, c:c + 1, :].broadcast_to([DC, B, IMG]), ALU.add).then_inc(S["a_x"], 1)

            def text_sum(b):
                dve.wait_ge(S["t_pm"], b + 1)
                link(dve.tensor_tensor(words[:, b, :], PS[:, 7, 0:D], words[:, b, :], ALU.add))
                dve.wait_ge(S["t_tp"], b + 1)
                link(dve.tensor_tensor(words[:, b, :], words[:, b, :], types[:, b, :], ALU.add))
                statistics(words[:, b, :], b, 1e-12, stT[:, :], mvT, veT).then_inc(S["t_ve"], 1)
                if b >= 1:
                    text_norm(b - 1)

            def text_norm(b):
                dve.wait_ge(S["t_rs"], b + 1)
                if b >= 2:
                    dve.wait_ge(S["h_txt"], b - 1)
                dve.tensor_scalar(zT_[:, b % 2, :], words[:, b, :], mvT[:, b, 0:1], rsT[:, b:b + 1], ALU.subtract, ALU.mult
                                  ).then_inc(S["t_z"], 1)

            for b in range(4):
                text_sum(b)
            for c in range(KC):
                dve.wait_ge(S["a_ff2"], c + 1)
                dve.tensor_scalar(y1T[:, c, :], PS[0:DC, 4 + c, :], col("tok_ff2_b", c, DC), None, ALU.add
                                  ).then_inc(S["a_y"], 1)
            for g in range(HG):
                text_sum(4 + g)
                dve.wait_ge(S["a_mm"], 2 * g + 1)
                dve.tensor_scalar(tq[:, g, :], PS[:, (2 * g) % 4, :], col("tok_q_b", g), DH ** -0.5, ALU.add, ALU.mult
                                  ).then_inc(S["a_q"], 1)
            text_sum(B - 1)
            text_norm(B - 1)

            def less_maximum(i):
                dve.wait_ge(S["a_s"], i + 1)
                sc = PS[:, 0:4, 0:HG * IMG].rearrange("p r (g k) -> p r g k", k=IMG)
                link(dve.reduce_max(mxA[:, :].rearrange("p (r g) -> p r g", r=4), sc, AX.X))
                if i >= 2:
                    dve.wait_ge(S["a_pT"], i - 1)
                dve.tensor_tensor(pA[:, i % 2, :, :].rearrange("p (r g) k -> p r g k", r=4), sc,
                                  mxA[:, :].rearrange("p (r g o) -> p r g o", r=4, o=1).broadcast_to([128, 4, HG, IMG]),
                                  ALU.subtract).then_inc(S["a_sub"], 1)

            def tile_of(t):
                return TP * t if t < IT else TP * ((t - IT) // 2) + 1 + (t - IT) % 2

            def z_in(t):
                return zA[:, t, :] if t < IT else words[:, t - IT, :]

            def norm_statistics(src, tiles, done, arrived=None):
                for t in tiles:
                    if arrived is not None:
                        dve.wait_ge(S[arrived], t + 1)
                    ins = dve.bn_stats(st_in[:, t, :], src(t))
                link(ins)
                for t in tiles:
                    ins = dve.bn_aggr(mv_in[:, t, :], st_in[:, t, :])
                link(ins)
                at = slice(tiles[0], tiles[-1] + 1)
                dve.tensor_scalar(ve_in[:, at], mv_in[:, at, 1], 1e-5, None, ALU.add).then_inc(S[done], 1)

            def norm_apply(src, dst, tiles, n, ready, done):
                dve.wait_ge(S[ready], n + 1)
                for t in tiles:
                    dve.tensor_scalar(dst(t), src(t), mv_in[:, t, 0:1], rs_in[:, t:t + 1], ALU.subtract, ALU.mult
                                      ).then_inc(S[done], 1)

            def in_h(t):
                return h_sb[:, t, :]

            def in_acc(t):
                return acc[:, tile_of(t), :]

            text_tiles, image_tiles = range(IT, IT + B), range(IT)

            less_maximum(0)
            for i in range(IT):
                if i + 1 < IT:
                    dve.wait_ge(S["a_sub"], i + 1)
                    less_maximum(i + 1)
                if i == 0:
                    dve.wait_ge(S["h_txt"], B)
                    norm_statistics(in_h, text_tiles, "p_ve1")
                elif i == 1:
                    norm_apply(in_h, in_acc, text_tiles, 0, "p_rs1", "p_x")
                    dve.wait_ge(S["p_x"], B)
                    norm_statistics(in_acc, text_tiles, "p_ve2")
                elif i == 2:
                    norm_apply(in_acc, z_in, text_tiles, 0, "p_rs2", "p_z")
                dve.wait_ge(S["a_o"], i + 1)
                o = PS[:, 7, 0:NH * (DH + 1)].rearrange("p (h e) -> p h e", e=DH + 1)
                if i >= 1:
                    dve.wait_ge(S["a_on"], i)
                link(dve.reciprocal(rcA[:, :].rearrange("p (h o) -> p h o", o=1), o[:, :, DH:DH + 1]))
                dve.tensor_tensor(oA[:, i, :, :], o[:, :, 0:DH],
                                  rcA[:, :].rearrange("p (h o) -> p h o", o=1).broadcast_to([128, NH, DH]), ALU.mult
                                  ).then_inc(S["a_on"], 1)
            for c in range(KC):
                dve.wait_ge(S["a_pj"], c + 1)
                dve.scalar_tensor_tensor(y1T[:, c, :], PS[0:DC, c, :], col("tok_proj_b", c, DC), xT[:, c, :],
                                         ALU.add, ALU.add).then_inc(S["a_x1"], 1)

            def norm(src, dst, v, r, done, n, arrive=None):
                for t in range(TP):
                    if arrive is not None:
                        link(arrive(t), True)
                    ins = dve.bn_stats(st[:, t, :], src(t))
                link(ins, True)
                for t in range(TP):
                    ins = dve.bn_aggr(mv[:, t, :], st[:, t, :])
                link(ins)
                dve.tensor_scalar(ve[:, 0:TP], mv[:, 0:TP, 1], 1e-5, None, ALU.add).then_inc(S[v], 1)
                dve.wait_ge(S[r], n + 1)
                for t in range(TP):
                    dve.tensor_scalar(dst(t), src(t), mv[:, t, 0:1], rs[:, t:t + 1], ALU.subtract, ALU.mult
                                      ).then_inc(S[done], 1)

            norm_statistics(in_h, image_tiles, "p_ve1", "h_img")
            norm_apply(in_h, in_acc, image_tiles, 1, "p_rs1", "p_x")
            dve.wait_ge(S["p_x"], B + IT)
            norm_statistics(in_acc, image_tiles, "p_ve2")
            norm_apply(in_acc, z_in, image_tiles, 1, "p_rs2", "p_z")

            def projection_out(n, j):
                ty, g, bank = PROJECTIONS[j]
                if ty == 1:
                    return
                dve.wait_ge(S["b_mm"], n * len(PROJECTIONS) + (j + 1))
                if ty == 0:
                    dve.tensor_scalar(qk[:, 0, g, :], PS[:, bank, 0:PT], col("q_b", g), DH ** -0.5, ALU.add, ALU.mult
                                      ).then_inc(S["b_q"], 1)
                else:
                    dve.tensor_scalar(qk[:, ty, g, :], PS[:, bank, 0:PT], phi_b[:, HG * (ty - 2) + g:HG * (ty - 2) + g + 1], 1e-4,
                                      ALU.add, ALU.max).then_inc(S["b_r"], 1)

            dve.wait_ge(S["p_xn"], 3)
            dve.tensor_copy(xnT[:, :, :], x3T[:, :, 0:PT]).then_inc(S["b_xc"], 1)
            dve.wait_ge(set_up, 6)
            dve.wait_ge(ld_attn, 11 * 16)
            for j in range(len(PROJECTIONS)):
                projection_out(0, j)
            straight = links[0]
            def pair(it, last):
                links[0], links[1] = 0, it * LINKS_PER_PAIR + straight

                o = PS[0:QC, 4, :].rearrange("p (k e) -> p k e", e=HS)

                def group_reciprocals(n):
                    at = it * (2 * HG) + (n + 1)
                    dve.wait_ge(S["b_dn"], at)
                    dve.tensor_tensor(rd[:, :], o[:, :, DH], eps_sum[:, :], ALU.add).then_inc(S["b_sm"], 1)
                    dve.wait_ge(S["b_sm"], at)
                    dve.reciprocal(rd[:, :], rd[:, :]).then_inc(S["b_rc"], 1)

                def group_scaled(n):
                    at = it * (2 * HG) + (n + 1)
                    dve.wait_ge(S["b_rc"], at)
                    if n >= 1:
                        dve.wait_ge(S["b_oT"], at - 1)
                    dve.tensor_tensor(oN[:, :, :], o[:, :, 0:DH], rd[:, :].rearrange("p (k o) -> p k o", o=1).broadcast_to([QC, 16, DH]),
                                      ALU.mult).then_inc(S["b_on"], 1)

                for u in range(2 * NH):
                    dve.wait_ge(S["b_s"], it * (2 * NH) + (u + 1))
                    if u >= 2:
                        dve.wait_ge(S["b_ex"], it * (2 * NH) + (u - 1))
                    carry()
                    dve.copy_predicated(sm[:, u % 2, 0:SQ], keep[:, :], PS[0:QC, u % 2, 0:SQ]).then_inc(S["b_cp"], 1)
                    dve.wait_ge(S["b_cp"], it * (2 * NH) + (u + 1))
                    dve.reduce_max(nm[:, u % 2, 0:1], sm[:, u % 2, Q0:SQ + 1], AX.X, negate=True)
                    dve.reduce_max(nm[:, u % 2, 1:2], sm[:, u % 2, 0:L], AX.X, negate=True).then_inc(S["b_nm"], 1)
                    dve.wait_ge(S["b_att"], it * (2 * NH) + (u + 1))
                    if u >= 2:
                        dve.wait_ge(S["b_o"], it * (2 * NH) + (u - 1))
                    dve.tensor_tensor(lin[:, u % 2, :], PS[0:QC, 2, 0:L + QC], causal[:, :], ALU.mult
                                      ).then_inc(S["b_lin"], 1)
                    if u >= 7 and u % 4 == 3:
                        group_reciprocals(u // 4 - 1)
                    if u >= 8 and u % 4 == 0:
                        group_scaled(u // 4 - 2)
                group_scaled(2 * HG - 2)
                if not last:
                    projection_out(it + 1, 0)
                group_reciprocals(2 * HG - 1)
                group_scaled(2 * HG - 1)
                if not last:
                    projection_out(it + 1, 1)
                dve.wait_ge(S["c_so"], it * TP + TP)
                dve.wait_ge(S["c_x3c"], it + 1)
                norm(lambda t: PS[:, t, 0:D], lambda t: z[:, t, :], "c_ve1", "c_rs1", "c_z1", it)
                for c in range(KC):
                    dve.wait_ge(S["c_pj"], it * KC + (c + 1))
                    dve.wait_ge(S["c_sl"], it * KC + (c + 1))
                    dve.scalar_tensor_tensor(uT[:, c, :], PS[0:DC, 6 + c, 0:PT], col("attn_proj_b", c, DC), slT[:, c, :],
                                             ALU.add, ALU.add).then_inc(S["c_u"], 1)
                if not last:
                    projection_out(it + 1, 2)

                def x2_tile(t):
                    dve.wait_ge(S["c_mm"], it * TP + (t + 1))
                    return dve.tensor_tensor(x2[:, t:t + 1, :], PS[:, t:t + 1, 0:D], acc[:, bass.ds(it * TP + t, 1), :], ALU.add)

                norm(lambda t: x2[:, t, :], lambda t: z[:, t, :], "c_ve2", "c_rs2", "c_z2", it, x2_tile)
                for j in () if last else range(3, 7):
                    projection_out(it + 1, j)
                dve.wait_ge(S["c_hx"], it + 1)

                def h2_tile(t):
                    dve.wait_ge(S["c_ff2"], it * TP + (t + 1))
                    return dve.tensor_tensor(acc[:, bass.ds(it * TP + t, 1), :], PS[:, 4 + t:5 + t, 0:D], hx[:, t:t + 1, :], ALU.add)

                norm(lambda t: acc[:, bass.ds(it * TP + t, 1), :], lambda t: z[:, t:t + 1, :],
                     "c_ve3", "c_rs3", "c_x3", it, h2_tile)
                for j in () if last else range(7, len(PROJECTIONS)):
                    projection_out(it + 1, j)
                assert links[0] == LINKS_PER_PAIR, links

            with dve.Fori(0, PAIRS - 1) as it:
                pair(it, False)
            pair(PAIRS - 1, True)

            dve.wait_ge(S["c_x3c"], PAIRS + 1)
            dve.wait_ge(S["b_phi"], PAIRS * 2 * HG)
            dve.sem_inc(S["e_gu"], 2)
            dve.sem_inc(S["e_acc"], 4)
            links[0], links[1] = 0, straight + PAIRS * LINKS_PER_PAIR
            dve.wait_ge(S["c_lg"], 1)

            def over(v):
                return v.rearrange("p (t o) -> p t o", o=1).broadcast_to([128, NT, E_R])

            logits = PS[:, 4, 0:NT * E_R].rearrange("p (t e) -> p t e", e=E_R)
            link(dve.reduce_max(r1[:, 0, :], logits, AX.X))
            dve.tensor_tensor(lg[:, :, :], logits, over(r1[:, 0, :]), ALU.subtract).then_inc(S["c_ls"], 1)
            dve.wait_ge(S["c_ex"], 1)
            link(dve.reduce_sum(r1[:, 1, :], lg[:, :, :], AX.X))
            link(dve.reciprocal(r1[:, 1, :], r1[:, 1, :]))
            link(dve.tensor_tensor(lg[:, :, :], lg[:, :, :], over(r1[:, 1, :]), ALU.mult))
            for k in range(TOPK):
                top, first, hot = r1[:, 2 + k, :], r1[:, 0, :], chosen[:, k, :, :]
                link(dve.reduce_max(top, lg[:, :, :], AX.X))
                link(dve.tensor_tensor(hot, lg[:, :, :], over(top), ALU.is_equal))
                link(dve.tensor_tensor(hot, hot, rank[:, :, :], ALU.mult))
                link(dve.reduce_max(first, hot, AX.X))
                link(dve.tensor_tensor(hot, rank[:, :, :], over(first), ALU.is_equal))
                if k == 0:
                    link(dve.scalar_tensor_tensor(lg[:, :, :], hot, -2.0, lg[:, :, :], ALU.mult, ALU.add))
            link(dve.tensor_tensor(r1[:, 0, :], r1[:, 2, :], r1[:, 3, :], ALU.add))
            link(dve.tensor_scalar(r1[:, 0, :], r1[:, 0, :], 1e-8, None, ALU.add))
            link(dve.reciprocal(r1[:, 0, :], r1[:, 0, :]))
            for k in range(TOPK):
                dve.tensor_tensor(weight[:, k, :], r1[:, 2 + k, :], r1[:, 0, :], ALU.mult).then_inc(S["c_cw"], 1)

            dve.wait_ge(ld_moe, 16 * (3 + 3 * E_S))
            dve.tensor_tensor(mask[:, :, :], chosen[:, 0, :, :], chosen[:, 1, :, :], ALU.add).then_inc(S["d_m"], 1)
            dve.memset(ones_e[:, :], 1.0)
            link(dve.memset(before[:, 0, :], 0.0))
            dve.wait_ge(S["d_cnt"], 2)
            in_tile = PS[:, 7, NT * E_R:2 * NT * E_R].rearrange("p (t e) -> p t e", e=E_R)
            for t in range(NT):
                dst = before[:, t + 1, :] if t + 1 < NT else count[:, :]
                link(dve.tensor_tensor(dst, before[:, t, :], in_tile[:, t, :], ALU.add))

            def per_expert(v, n):
                return v.rearrange("p (e o) -> p e o", o=1).broadcast_to([v.shape[0], E_R, n])

            def to_all(v, n):
                return v.rearrange("p (o e) -> p o e", o=1).broadcast_to([v.shape[0], n, v.shape[1]])

            link(dve.tensor_tensor(beyond[:, :, :], per_expert(count[:, :], NT), to_all(steps[:, :], E_R), ALU.is_gt))
            link(dve.reduce_sum(tiles_of[:, :], beyond[:, :, :], AX.X))
            link(dve.tensor_tensor_scan(ends[:, :], ones_e[:, :], tiles_of[:, :], 0.0, ALU.mult, ALU.add))
            link(dve.tensor_tensor(base[:, :], ends[:, :], tiles_of[:, :], ALU.subtract))
            link(dve.tensor_scalar(base[:, :], base[:, :], 128.0, None, ALU.mult))
            rank_in = PS[:, 7, 0:NT * E_R].rearrange("p (t e) -> p t e", e=E_R)
            link(dve.tensor_tensor(at_slot[:, :, :], rank_in, before[:, :, :], ALU.add))
            link(dve.tensor_tensor(at_slot[:, :, :], at_slot[:, :, :], to_all(base[:, :], NT), ALU.add))
            for k in range(TOPK):
                link(dve.tensor_tensor(pick[:, :, :], at_slot[:, :, :], chosen[:, k, :, :], ALU.mult))
                link(dve.reduce_sum(slot_f[:, k, :], pick[:, :, :], AX.X))
            link(dve.tensor_copy(slot[:, :, :], slot_f[:, :, :]))
            link(dve.tensor_tensor(passed[:, :, :], to_all(ends[0:1, :], RT),
                                   tile_no[:, :].rearrange("p (i o) -> p i o", o=1).broadcast_to([1, RT, E_R]), ALU.is_le))
            link(dve.reduce_sum(expert_f[:, :], passed[:, :, :], AX.X))
            link(dve.tensor_scalar(expert_f[:, :], expert_f[:, :], float(E_R - 1), None, ALU.min))
            dve.tensor_copy(expert[:, :], expert_f[:, :]).then_inc(S["d_slot"], 1)

            def add_shared(at, src):
                res = acc[:, at, :]
                dve.scalar_tensor_tensor(res, src, 1.0 / E_S, res, ALU.mult, ALU.add).then_inc(S["e_acc"], 1)

            def gate_times_up(m, ready):
                dve.wait_ge(S["e_sg"], ready)
                dve.tensor_tensor(gu[:, m, :], sg[:, m % 2, :], PS[:, 2 + m % 2, :], ALU.mult).then_inc(S["e_gu"], 1)

            for t in range(4):
                dve.wait_ge(S["e_dn"], 2 * (t // 2) + 2)
                add_shared(slice(t, t + 1), PS[:, 4 + t // 2:5 + t // 2, D * (t % 2):D * (t % 2) + D])
            with dve.Fori(0, 2) as s:
                for m in range(FM):
                    gate_times_up(m, s * FM + (FM + m + 1))
                for t in range(4):
                    dve.wait_ge(S["e_dn"], s * 4 + (4 + t + 1))
                    add_shared(bass.ds(s * 4 + (4 + t), 1), PS[:, 4 + t:5 + t, 0:D])

            def hidden(i, n, j):
                dve.wait_ge(S["r_sg"], i + 1)
                dve.wait_ge(S["r_u"], i + 1)
                dve.tensor_tensor(rh[:, j, :], rsg[:, j, :], PS[:, 2:4, :].rearrange("p a b -> p (a b)")[:, 0:FF], ALU.mult
                                  ).then_inc(S["r_h"], 1)

            in_order(hidden)(dve, 1, 0)
            for s in range(3):
                for m in range(FM):
                    gate_times_up(m, (3 + s) * FM + m + 1)
                dve.wait_ge(S[f"fetched{s}"], 16 * TOPK * 4)
                for k in range(TOPK):
                    for t in range(4 * s, 4 * s + 4):
                        ins = dve.scalar_tensor_tensor(acc[:, t, :], yg[k][:, t, :], weight[:, k, t:t + 1], acc[:, t, :],
                                                       ALU.mult, ALU.add)
                    link(ins)
                for t in range(4):
                    dve.wait_ge(S["e_dn"], 12 + 4 * s + t + 1)
                    add_shared(slice(4 * s + t, 4 * s + t + 1), PS[:, 4 + t:5 + t, 0:D])

        @block.tensor
        def _(pe):
            def accumulate(dst, pairs):
                for k, (lhs, rhs) in enumerate(pairs):
                    mm = pe.matmul(dst, lhs, rhs, start=(k == 0), stop=(k == len(pairs) - 1))
                return mm

            pe.wait_ge(ld_patch, 32)
            pe.wait_ge(ld_const, 48)
            pe.wait_ge(set_up, 3)
            for i in range(IT):
                accumulate(PS[:, i, 0:D], [(patches[:, j, 128 * i:128 * i + 128], w_patch[:, j, :]) for j in range(FM)]
                           + [(ones[:, 0:128], row("patch_b"))]).then_inc(S["patch_mm"], 1)
            for i in range(IT):
                pe.wait_ge(S["a_z"], i + 1)
                for c in range(KC):
                    mm = pe.transpose(PS[0:DC, 4 + c, 128 * i:128 * i + 128], zA[:, i, DC * c:DC * c + DC], ident[:, :])
                mm.then_inc(S["a_zT"], 1)
            pe.wait_ge(ld_tok, 7 * 16)

            def text_step(b):
                if b >= 1:
                    pe.wait_ge(S["t_dc"], b)
                    if b >= 2:
                        pe.wait_ge(S["t_ve"], b - 1)
                    accumulate(PS[:, 7, 0:D], [(domT[:, (b - 1) % 2, :], w_txt[:, :]), (ones[:, 0:128], row("txt_proj_b"))]
                               ).then_inc(S["t_pm"], 1)
                if b < B:
                    pe.wait_ge(gathered[b], 64)
                    pe.transpose(PS[:, 6, 0:128], dom[:, b, :], ident[:, :]).then_inc(S["t_dT"], 1)

            pe.wait_ge(ld_txt, 48)

            def tok_up(src, base, bank0):
                for m in range(FM):
                    if m >= 4:
                        pe.wait_ge(S["a_h"], base + m - 3)
                    accumulate(PS[:, bank0 + m % 4, :], [(w_tff1[:, c, 128 * m:128 * m + 128], src[:, c, :]) for c in range(KC)]
                               ).then_inc(S["a_ff1"], 1)
                    if base == 0 and m >= 2:
                        text_step(m - 2)

            pe.wait_ge(S["a_x"], KC)
            tok_up(xT, 0, 0)
            pe.wait_ge(S["a_h"], FM)
            for c in range(KC):
                accumulate(PS[0:DC, 4 + c, :], [(w_tff2[:, m, DC * c:DC * c + DC], h1T[:, m, :]) for m in range(FM)]
                           ).then_inc(S["a_ff2"], 1)
                text_step(4 + c)
            pe.wait_ge(S["a_y"], KC)
            for g in range(HG):
                for w, done in ((w_tq, "a_q"), (w_tk, "a_k")):
                    j = 2 * g + (w is w_tk)
                    if g == 2:
                        pe.wait_ge(S[done], 1)
                    accumulate(PS[:, j % 4, :], [(w[:, c, 128 * g:128 * g + 128], y1T[:, c, :]) for c in range(KC)]
                               ).then_inc(S["a_mm"], 1)
                text_step(FM + g)
            pe.wait_ge(S["t_ve"], B)
            for w in range(B):
                if w >= 2:
                    pe.wait_ge(S["a_v"], w - 1)
                accumulate(PS[0:IMG, 6 + w % 2, 0:D],
                           [(y1T[:, c, IMG * w:IMG * w + IMG], w_tv[:, c, :]) for c in range(KC)]
                           + [(ones[:, 0:IMG], row("tok_v_b"))]).then_inc(S["a_vmm"], 1)

            def img_scores(i):
                if i >= 1:
                    pe.wait_ge(S["a_sub"], i)
                for w in range(2):
                    at = 128 * i + IMG * w
                    for r in range(4):
                        for g in range(HG):
                            mm = pe.matmul(PS[IMG * w:IMG * w + IMG, r, IMG * g:IMG * g + IMG],
                                           tq[32 * r:32 * r + DH, g, at:at + IMG], tk[32 * r:32 * r + DH, g, at:at + IMG],
                                           start=True, stop=True)
                mm.then_inc(S["a_s"], 1)

            def img_turn_outputs(i):
                pe.wait_ge(S["a_on"], i + 1)
                for c in range(KC):
                    mm = pe.transpose(PS[0:DC, 7, 256 + 128 * c:384 + 128 * c],
                                      oA[:, i, 6 * c:6 * c + 6, :].rearrange("p h e -> p (h e)"), ident[:, :])
                mm.then_inc(S["a_oT"], 1)

            pe.wait_ge(S["a_q"], HG)
            pe.wait_ge(S["a_k"], HG)
            img_scores(0)
            pe.wait_ge(S["a_v"], B)
            for i in range(IT):
                if i + 1 < IT:
                    img_scores(i + 1)
                pe.wait_ge(S["a_exp"], i + 1)
                if i >= 1:
                    pe.wait_ge(S["a_ptc"], i)
                for k in range(NH):
                    mm = pe.transpose(PS[0:IMG, 4 + k // 4, 128 * (k % 4):128 * (k % 4) + 128], pA[:, i % 2, k, :],
                                      ident[:, :])
                mm.then_inc(S["a_pT"], 1)
                if i >= 1:
                    img_turn_outputs(i - 1)
                    pe.wait_ge(S["a_at"], i)
                pe.wait_ge(S["a_ptc"], i + 1)
                for w in range(2):
                    for k in range(NH):
                        h = 4 * (k % HG) + k // HG
                        mm = pe.matmul(PS[IMG * w:IMG * w + IMG, 7, (DH + 1) * h:(DH + 1) * (h + 1)],
                                       ptA[:, k, IMG * w:IMG * w + IMG], tv[:, 2 * i + w, h, :], start=True, stop=True)
                mm.then_inc(S["a_o"], 1)
            img_turn_outputs(IT - 1)
            pe.wait_ge(S["a_at"], IT)
            for c in range(KC):
                accumulate(PS[0:DC, c, :], [(w_tproj[:, k, DC * c:DC * c + DC], aTA[:, k, :]) for k in range(KC)]
                           ).then_inc(S["a_pj"], 1)
            pe.wait_ge(S["a_x1"], KC)

            def turn_text(n):
                pe.wait_ge(S["p_z"], 4 * n + 4)
                if n >= 1:
                    pe.wait_ge(S["p_xn"], n)
                for c in range(KC):
                    for b in range(4 * n, 4 * n + 4):
                        mm = pe.transpose(PS[0:DC, c, 128 * (b % 4):128 * (b % 4) + 128], words[:, b, DC * c:DC * c + DC], ident[:, :])
                mm.then_inc(S["p_zT"], 1)

            turn_text(0)
            tok_up(y1T, FM, 2)
            turn_text(1)
            pe.wait_ge(S["a_h"], 2 * FM)
            for i in range(IT):
                if i >= 2:
                    pe.wait_ge(S["h_img"], i - 1)
                at = slice(128 * i, 128 * i + 128)
                dst = PS[:, 6 + i % 2, :]
                for k, (lhs, rhs) in enumerate([(h1T[:, m, at], w_tff2[:, m, :]) for m in range(FM)]
                                               + [(ones[:, 0:128], row("tok_ff2_b"))]):
                    pe.matmul(dst[:, 0:D], lhs, rhs, start=(k == 0), stop=False)
                for c in range(KC):
                    mm = pe.matmul(dst[:, DC * c:DC * c + DC], y1T[:, c, at], ident[0:DC, 0:DC], start=False, stop=(c == KC - 1))
                mm.then_inc(S["a_hmm"], 1)

            pe.wait_ge(S["p_z"], B + IT)
            pe.wait_ge(S["p_xn"], 2)
            for c in range(KC):
                for i in range(IT):
                    mm = pe.transpose(PS[0:DC, c, 128 * i:128 * i + 128], zA[:, i, DC * c:DC * c + DC], ident[:, :])
            mm.then_inc(S["p_zT"], 1)

            def project(n, j):
                ty, g, bank = PROJECTIONS[j]
                for i in range(j):
                    if PROJECTIONS[i][2] == bank:
                        read = i
                if bank in [x[2] for x in PROJECTIONS[:j]]:
                    used_by(n, read)
                accumulate(PS[:, bank, 0:PT], [(w_qk[:, ty, c, 128 * g:128 * g + 128], xnT[:, c, :]) for c in range(KC)]
                           ).then_inc(S["b_mm"], 1)

            def used_by(n, j):
                ty, g, _ = PROJECTIONS[j]
                if ty <= 1:
                    pe.wait_ge(S[("b_q", "b_k")[ty]], n * HG + (g + 1))
                else:
                    pe.wait_ge(S["b_e"], n * (2 * HG) + (2 * g + ty - 1))

            def project_values(n):
                for k in range(4):
                    if k >= 2:
                        pe.wait_ge(S["b_v"], n * 4 + (k - 1))
                    accumulate(PS[0:QC, 4 + k % 2, 0:2 * D],
                               [(xnT[:, c, QC * k:QC * k + QC], w_v[:, c, :]) for c in range(KC)]
                               + [(ones[:, 0:QC], row("v_b", 2 * D))]).then_inc(S["b_vmm"], 1)
                pe.wait_ge(S["b_v"], n * 4 + 4)
                for j in (9, 10, 11):
                    used_by(n, j)
                for bb in range(2):
                    pe.matmul(PS[QC:QC + 1, 6 + bb, 0:NH * HS], ones_sq[0:QC, 0:1],
                              va[0:QC, 2 * bb + 1, 0, :, :].rearrange("p h e -> p (h e)"), start=True, stop=True
                              ).then_inc(S["b_vs"], 1)

            pe.wait_ge(set_up, 6)
            pe.wait_ge(ld_attn, 11 * 16)
            pe.wait_ge(S["b_xc"], 1)
            for j in range(len(PROJECTIONS)):
                project(0, j)
            project_values(0)
            def pair(it, last):
                def turned(z, ready, done, bank):
                    for t in range(TP):
                        pe.wait_ge(S[ready], it * TP + (t + 1))
                        for c in range(KC):
                            mm = pe.transpose(PS[0:DC, bank + c, 128 * t:128 * t + 128], z(t)[:, DC * c:DC * c + DC], ident[:, :])
                        mm.then_inc(S[done], 1)

                pe.wait_ge(S["b_phi"], it * (2 * HG) + 2 * HG)

                def scores(u):
                    bb, h = divmod(u, NH)
                    g, seq = h // 4, L * bb
                    pe.wait_ge(S["b_qx"], it * (2 * NH) + (u + 1))
                    if u >= 2:
                        pe.wait_ge(S["b_cp"], it * (2 * NH) + (u - 1))
                    for q, at, k, n in ((1, 0, QC, QC), (1, QC, 0, QC + 1), (0, Q0, 0, QC)):
                        mm = pe.matmul(PS[0:QC, u % 2, at:at + n], qx[:, u % 2, 0, QC * q:QC * q + QC],
                                       qk[:, 1, g, seq + k:seq + k + n], start=True, stop=True)
                    mm.then_inc(S["b_s"], 1)
                    if u >= 1:
                        pe.wait_ge(S["b_lin"], it * (2 * NH) + u)
                    for k in range(2):
                        mm = pe.matmul(PS[0:QC, 2, L * k:L * k + L - QC * k], qk[:, 3, g, seq + QC * k:seq + QC * k + QC],
                                       qx[:, u % 2, 1, QC * k:L], start=True, stop=True)
                    mm.then_inc(S["b_att"], 1)

                def turn(u):
                    pe.wait_ge(S["b_ex"], it * (2 * NH) + (u + 1))
                    if u >= 1:
                        pe.wait_ge(S["b_ptc"], it * (2 * NH) + u)
                    for at, src in ((0, Q0), (QC, QC), (2 * QC, 0)):
                        mm = pe.transpose(PS[0:QC + 1, 3, at:at + QC], pb[:, u % 2, src:src + QC + 1], ident[0:QC, 0:QC])
                    mm.then_inc(S["b_pT"], 1)

                def values(u):
                    bb, h = divmod(u, NH)
                    r, g = h % 4, h // 4
                    pe.wait_ge(S["b_ptc"], it * (2 * NH) + (u + 1))
                    pe.wait_ge(S["b_lin"], it * (2 * NH) + (u + 1))
                    if bb == 1 and r == 0:
                        pe.wait_ge(S["b_oc"], it * (2 * HG) + (g + 1))
                    o = PS[HS * r:HS * r + HS, 5 + g, :]
                    pe.matmul(o[:, 0:L], va[:, 2 * bb, 0, h, :], pts[:, u % 2, 0:L], start=True, stop=False)
                    pe.matmul(o[:, QC:L], va[0:QC, 2 * bb + 1, 0, h, :], pts[0:QC, u % 2, L:L + QC], start=False, stop=True)
                    for k in range(2):
                        mm = pe.matmul(o[:, L + QC * k:2 * L], va[0:QC, 2 * bb + k, 1, h, :], lin[:, u % 2, L * k:L * k + L - QC * k],
                                       start=(k == 0), stop=(k == 1))
                    mm.then_inc(S["b_o"], 1)

                def turn_sums(n):
                    pe.wait_ge(S["b_oc"], it * (2 * HG) + (n + 1))
                    if n >= 1:
                        pe.wait_ge(S["b_ao"], it * (2 * HG) + n)
                    for k in range(4):
                        src = L * (k % 2) + QC * (k // 2)
                        mm = pe.transpose(PS[0:QC, 4, 128 * k:128 * k + 128], o_raw[:, n % 2, src:src + QC], ident[:, :])
                    mm.then_inc(S["b_dn"], 1)

                def turn_outputs(n):
                    pe.wait_ge(S["b_on"], it * (2 * HG) + (n + 1))
                    for c in range(2):
                        mm = pe.transpose(PS[:, 4, QC * c:QC * c + QC], oN[:, 8 * c:8 * c + 8, :].rearrange("p r e -> p (r e)"),
                                          ident[0:QC, 0:QC])
                    mm.then_inc(S["b_oT"], 1)

                scores(0)
                pe.wait_ge(S["b_vc"], it * 2 + 2)
                for u in range(2 * NH):
                    if u + 1 < 2 * NH:
                        scores(u + 1)
                    turn(u)
                    if u >= 1:
                        values(u - 1)
                    if u >= 6 and u % 4 == 2:
                        turn_sums(u // 4 - 1)
                    if u >= 9 and u % 4 == 1:
                        turn_outputs(u // 4 - 2)
                values(2 * NH - 1)
                if not last:
                    pe.wait_ge(S["b_xc"], it + 2)
                    project(it + 1, 0)
                turn_outputs(2 * HG - 2)
                turn_sums(2 * HG - 1)
                if not last:
                    project(it + 1, 1)
                turn_outputs(2 * HG - 1)
                tiles = [slice(128 * t, 128 * t + 128) for t in range(TP)]
                pe.wait_ge(S["b_ao"], it * (2 * HG) + 2 * HG)
                for t in range(TP):
                    accumulate(PS[:, t, 0:D], [(aoT[FG:2 * FG, g, tiles[t]], w_heads[FG:2 * FG, g, :]) for g in range(HG)]
                               + [(ones[:, 0:128], row("ssm_out_b"))]).then_inc(S["c_so"], 1)
                for c in range(KC):
                    accumulate(PS[0:DC, 6 + c, 0:PT], [(w_heads[0:FG, g, DC * c:DC * c + DC], aoT[0:FG, g, :]) for g in range(HG)]
                               ).then_inc(S["c_pj"], 1)
                if not last:
                    used_by(it + 1, 1)
                turned(lambda t: z[:, t, :], "c_z1", "c_z1T", 4)
                if not last:
                    project(it + 1, 2)
                pe.wait_ge(S["c_u"], it * KC + KC)
                for t in range(TP):
                    accumulate(PS[:, t, 0:D], [(uT[:, c, tiles[t]], w_out[:, c, :]) for c in range(KC)]
                               + [(ones[:, 0:128], row("out_b"))]).then_inc(S["c_mm"], 1)
                if not last:
                    project(it + 1, 3)
                    project(it + 1, 4)
                turned(lambda t: z[:, t, :], "c_z2", "c_z2T", 4)
                if not last:
                    project(it + 1, 5)
                    project(it + 1, 6)
                pe.wait_ge(S["c_m"], it * KC + KC)
                for m in range(FM):
                    if m >= 3:
                        pe.wait_ge(S["c_h"], it * FM + (m - 2))
                    accumulate(PS[:, m % 3, 0:PT], [(w_m1[:, c, 128 * m:128 * m + 128], mT[:, c, :]) for c in range(KC)]
                               ).then_inc(S["c_ff1"], 1)
                for t in range(TP):
                    if t == 2 and not last:
                        used_by(it + 1, 4)
                    pe.matmul(PS[:, 4 + t, 0:D], ones[:, 0:128], row("mlp_b2"), start=True, stop=False)
                    for m in range(FM):
                        if t == 0:
                            pe.wait_ge(S["c_h"], it * FM + (m + 1))
                        mm = pe.matmul(PS[:, 4 + t, 0:D], hT[:, m, tiles[t]], w_m2[:, m, :], start=False, stop=(m == FM - 1))
                    mm.then_inc(S["c_ff2"], 1)
                if not last:
                    project(it + 1, 7)
                    project(it + 1, 8)
                turned(lambda t: z[:, t, :], "c_x3", "c_x3T", 0)
                for j in () if last else range(9, len(PROJECTIONS)):
                    project(it + 1, j)
                if not last:
                    project_values(it + 1)
                pe.wait_ge(S["c_x3s"], it + 1)

            with pe.Fori(0, PAIRS - 1) as it:
                pair(it, False)
            pair(PAIRS - 1, True)

            for t in range(NT):
                mm = accumulate(PS[:, 4, E_R * t:E_R * t + E_R],
                                [(x3T[:, c, 128 * t:128 * t + 128], w_gate[:, c, :]) for c in range(KC)])
            mm.then_inc(S["c_lg"], 1)

            pe.wait_ge(ld_moe, 16 * (3 + 3 * E_S))

            def up_chunk(e, m, x, read):
                pe.wait_ge(S["e_gu"], read)
                for k in range(2):
                    mm = accumulate(PS[:, 2 * k + m % 2, :],
                                    [(w_sgu[:, e, k, c, 128 * m:128 * m + 128], x[:, c, :]) for c in range(KC)])
                mm.then_inc(S["e_up"], 1)

            def down_tile(e, t, dst, multiplied):
                for m in range(FM):
                    if t == 0:
                        pe.wait_ge(S["e_gu"], multiplied(m))
                    mm = pe.matmul(dst, gu[:, m, 128 * t:128 * t + 128], w_sdn[:, e, m, :], start=(m == 0), stop=(m == FM - 1))
                mm.then_inc(S["e_dn"], 1)

            def shared(e, first):
                with pe.Fori(0, 3 - first) as s:
                    x = x3T[:, :, bass.ds(s * 512 + 512 * first, 512)]
                    for m in range(FM):
                        up_chunk(e, m, x, s * FM + ((e * 3 + first) * FM + m + 1))
                    for t in range(4):
                        pe.wait_ge(S["e_acc"], s * 4 + (12 * e + 4 * first + t + 1))
                        down_tile(e, t, PS[:, 4 + t, 0:D], lambda m: s * FM + ((e * 3 + first) * FM + m + 3))

            for m in range(FM):
                up_chunk(0, m, x3T[:, :, 0:512], m + 1)
            pe.wait_ge(S["d_m"], 1)
            for k, w in enumerate((earlier, ones_sq)):
                pe.matmul(PS[:, 7, NT * E_R * k:NT * E_R * (k + 1)], w[:, :], mask[:, :, :].rearrange("p t e -> p (t e)"),
                          start=True, stop=True).then_inc(S["d_cnt"], 1)
            for t in range(4):
                down_tile(0, t, PS[:, 4 + t // 2, D * (t % 2):D * (t % 2) + D], lambda m: m + 3)
            pe.wait_ge(S["d_slot"], 1)
            pe.wait_ge(S["e_acc"], 4 + 4)
            shared(0, 1)
            pe.wait_ge(S["e_acc"], 4 + NT)
            pe.sem_inc(S["r_y"], 2)

            def turn_tokens(n, j):
                pe.wait_ge(S[f"r_x{j}"], n * 16 + 16)
                for c in range(KC):
                    mm = pe.transpose(PS[0:DC, 6 + j, 128 * c:128 * c + 128], xs[:, j, DC * c:DC * c + DC], ident[:, :])
                mm.then_inc(S["r_xT"], 1)

            def down(i, n, j):
                pe.wait_ge(S["r_h"], i + 1)
                pe.wait_ge(S[f"r_d{j}"], n * 16 + 16)
                pe.wait_ge(S["r_ye"], i + 1)
                accumulate(PS[:, 4 + j, 0:D], [(rh[:, j, 128 * m:128 * m + 128], w_rdn[:, j, m, :]) for m in range(FM)]
                           ).then_inc(S["r_y"], 1)

            turn_tokens(0, 0)

            def up(i, n, j):
                static = isinstance(i, int)
                pe.wait_ge(S["r_xe"], i + 1)
                pe.wait_ge(S[f"r_w{j}"], n * 32 + 32)
                for k, (done, read) in enumerate((("r_g", "r_sg"), ("r_u", "r_h"))):
                    if not static or i >= 1:
                        pe.wait_ge(S[read], i)
                    for m in range(FM):
                        mm = accumulate(PS[:, 2 * k + m // 4, 128 * (m % 4):128 * (m % 4) + 128],
                                        [(w_rgu[:, j, k, c, 128 * m:128 * m + 128], xt[:, j, c, :]) for c in range(KC)])
                    mm.then_inc(S[done], 1)
                if not static or i + 1 < RT:
                    turn_tokens(n + j, 1 - j)
                if not static or i >= 1:
                    down(i - 1, n - 1 + j, 1 - j)

            in_order(up)(pe, 1, 2)
            down(RT - 1, (RT - 1) // 2, (RT - 1) % 2)
            shared(1, 0)


LINKS_PER_PAIR = 12


def layout(i):
    f = np.float32

    def chunks(w, p):
        return np.ascontiguousarray(w.reshape(-1, p, w.shape[-1]).transpose(1, 0, 2))

    def spread(w):
        o = np.zeros(w.shape[:-1] + (NH, 32), f)
        o[..., :DH] = w.reshape(w.shape[:-1] + (NH, DH))
        return o.reshape(w.shape[:-1] + (NH * 32,))

    def vec(v, p):
        o = np.zeros((128, v.size // p), f)
        o[:p] = v.reshape(-1, p).T
        return o

    a = {}
    x = i["x"].reshape(B, 3, 8, 16, 8, 16).transpose(1, 3, 5, 0, 2, 4).reshape(FF, NI)
    a["patches"] = chunks(x, 128)
    a["w_patch"] = chunks(i["L0_tok_patch_w"].reshape(D, FF).T, 128)
    tqkv, tb = i["L0_tok_qkv_w"], i["L0_tok_qkv_b"]
    a["w_tff1"] = chunks(i["L0_tok_ff1_w"], DC)
    a["w_tff2"] = chunks(i["L0_tok_ff2_w"], 128)
    a["w_tq"] = chunks(spread(tqkv[:, 0:D]), DC)
    a["w_tk"] = chunks(spread(tqkv[:, D:2 * D]), DC)
    a["w_tv"] = chunks(tqkv[:, 2 * D:], DC)
    a["w_tproj"] = chunks(i["L0_tok_proj_w"], DC)
    a["w_txt"] = np.ascontiguousarray(i["L0_txt_proj_w"].T)
    a["gam_txt"] = np.ascontiguousarray(np.broadcast_to(i["L0_txt_ln_gamma"], (128, D)))
    a["bet_txt"] = np.ascontiguousarray(np.broadcast_to(i["L0_txt_ln_beta"], (128, D)))
    w1, b1 = i["L0_attn_attn_qkv_w"], i["L0_attn_attn_qkv_b"]
    w2, b2 = i["L0_attn_ssm_qkv_w"], i["L0_attn_ssm_qkv_b"]
    a["w_qk"] = np.ascontiguousarray(np.stack([chunks(spread(w[:, k * D:k * D + D]), DC) for w in (w1, w2) for k in (0, 1)], 1))
    a["w_v"] = chunks(np.concatenate([w1[:, 2 * D:], w2[:, 2 * D:]], 1), DC)
    a["w_heads"] = np.concatenate([chunks(i["L0_attn_" + n], 4 * DH) for n in ("attn_proj_w", "ssm_out_w")], 0)
    a["w_out"] = chunks(i["L0_attn_out_w"], DC)
    a["w_m1"] = chunks(i["L0_attn_mlp_w1"], DC)
    a["w_m2"] = chunks(i["L0_attn_mlp_w2"], 128)
    a["w_gate"] = chunks(i["L0_ffn_gate_w"].T, DC)
    v = {"tok_ln_g": (i["L0_tok_ln_g"], DC), "tok_ln_b": (i["L0_tok_ln_b"], DC), "tok_ff1_b": (i["L0_tok_ff1_b"], 128),
         "tok_ff2_b": (i["L0_tok_ff2_b"], DC), "tok_q_b": (spread(tb[0:D]), 128), "tok_k_b": (spread(tb[D:2 * D]), 128),
         "tok_proj_b": (i["L0_tok_proj_b"], DC), "ln1_g": (i["L0_attn_ln1_g"], DC), "ln1_b": (i["L0_attn_ln1_b"], DC),
         "q_b": (spread(b1[0:D]), 128), "k_b": (spread(b1[D:2 * D]), 128), "q2_b": (spread(b2[0:D]), 128),
         "k2_b": (spread(b2[D:2 * D]), 128), "attn_proj_b": (i["L0_attn_attn_proj_b"], DC),
         "ssm_ln_g": (i["L0_attn_ssm_ln_g"], DC), "ssm_ln_b": (i["L0_attn_ssm_ln_b"], DC),
         "lnm_g": (i["L0_attn_lnm_g"], DC), "lnm_b": (i["L0_attn_lnm_b"], DC), "mlp_b1": (i["L0_attn_mlp_b1"], 128)}
    a["cols"] = np.concatenate([vec(*v[n]) for n in COLS], 1)
    r = {"patch_b": i["L0_tok_patch_b"], "tok_v_b": tb[2 * D:], "tok_ff2_b": i["L0_tok_ff2_b"], "txt_proj_b": i["L0_txt_proj_b"],
         "v_b": np.concatenate([b1[2 * D:], b2[2 * D:]]), "ssm_out_b": i["L0_attn_ssm_out_b"], "out_b": i["L0_attn_out_b"],
         "mlp_b2": i["L0_attn_mlp_b2"]}
    a["rows"] = np.concatenate([r[n] for n in ROWS])[None]
    a["word_table"], a["type_table"] = i["L0_txt_word_table"], i["L0_txt_type_table"]
    a["pos_table"], a["domain_table"] = i["L0_txt_pos_table"], i["L0_txt_domain_table"]
    a["ids"] = np.ascontiguousarray(np.stack([i["x_txt"].T, i["mask_BS_i0_1"].T, i["pos_BS"].T, i["itok_BS_0_4999"].T], 1))
    for n in ("wg", "wu", "shared_wg", "shared_wu"):
        a[n] = np.ascontiguousarray(i["L0_ffn_" + n].reshape(-1, KC, DC, FF).transpose(0, 2, 1, 3))
    for n in ("wd", "shared_wd"):
        a[n] = np.ascontiguousarray(i["L0_ffn_" + n].reshape(-1, FM, 128, D).transpose(0, 2, 1, 3))
    a["ident"] = np.eye(128, dtype=f)
    a["earlier"] = np.triu(np.ones((128, 128), f), 1)
    a["steps"] = np.ascontiguousarray(np.broadcast_to(np.arange(NT, dtype=f) * f(128), (128, NT)))
    p, r = np.arange(128)[:, None], np.arange(4)[None]
    a["head_rows"] = ((p // HS == r) & (p % HS < DH)).astype(f)
    a["tile_no"] = np.arange(RT, dtype=f)[None]
    q, k = np.arange(L)[:, None], np.arange(L)[None]
    near = (k <= q) & (k > q - WINDOW)
    a["keep"] = np.concatenate([near[QC:, QC:], near[QC:, 0:QC], np.zeros((QC, 1), bool), near[0:QC, 0:QC]], 1).astype(np.int32)
    past = np.where(k.T <= q.T, f(DH ** -0.5), f(0))
    a["causal"] = np.concatenate([past[0:QC], past[QC:, QC:]], 1)
    a["rank"] = np.ascontiguousarray(np.broadcast_to(np.arange(E_R, 0, -1, dtype=f), (128, NT, E_R)))
    ang = np.arange(IMG, dtype=f)[:, None] / np.power(f(10000.0), f(2.0) * np.arange(D // 2, dtype=f)[None] / f(D))
    pe = np.zeros((IMG, D), f)
    pe[:, 0::2], pe[:, 1::2] = np.sin(ang), np.cos(ang)
    a["pe_tab"] = chunks(np.ascontiguousarray(pe.T), DC)
    return a


def kernel(**inputs):
    import concourse.bacc as bacc
    from concourse.bass_utils import run_bass_kernel_spmd

    nc = bacc.Bacc("TRN2", target_bir_lowering=False, num_devices=1)
    arrays = layout({k: np.asarray(v) for k, v in inputs.items()})
    args = {n: nc.dram_tensor(f"in_{n}", v.shape, mybir.dt.from_np(v.dtype), kind="ExternalInput").ap()
            for n, v in arrays.items()}
    out = nc.dram_tensor("out_h", (B, L, D), F32, kind="ExternalOutput").ap()
    build(nc, args, out)
    r = run_bass_kernel_spmd(nc, [{f"in_{n}": v for n, v in arrays.items()}], core_ids=[0])
    return r.results[0]["out_h"]
```
